# Optimizing a Trainium2 kernel written in Bass

```python
import numpy as np
import jax
import jax.numpy as jnp

def _softmax(x, axis=-1):
    return jax.nn.softmax(x, axis=axis)

def _gelu(x):
    return jax.nn.gelu(x, approximate=True)

def _silu(x):
    return jax.nn.silu(x)

def _sigmoid(x):
    return jax.nn.sigmoid(x)

def _layernorm(x, axis=-1, eps=1e-05):
    m = jnp.mean(x, axis=axis, keepdims=True)
    v = jnp.var(x, axis=axis, keepdims=True)
    return (x - m) / jnp.sqrt(v + eps)

def _scatter_add(tgt, idx, src, axis=0):
    return tgt.at[idx].add(src)

def _segment_sum(src, seg, n):
    return jax.ops.segment_sum(src, seg, n)
kernel_name = 'mk_gnn_resnorm_d2_gnn_r8_ed14ac'

def setup_inputs(seed: int=0):
    np.random.seed(seed)
    _w = jnp.asarray

    def _rec_inputs():
        import jax
        import jax.numpy as jnp
        _gk = jax.random.key(seed)
        x = -0.0003713 + 1 * jax.random.normal(jax.random.fold_in(_gk, 1), (6250, 256), jnp.float32)
        _s = jax.random.randint(jax.random.fold_in(_gk, 2), (50000,), 0, 6250, jnp.int32)
        _d = jax.random.randint(jax.random.fold_in(_gk, 3), (50000,), 0, 6250, jnp.int32)
        _loop = jnp.arange(6250, dtype=jnp.int32)
        src = jnp.concatenate([_s, _d, _loop])
        dst = jnp.concatenate([_d, _s, _loop])
        _o = jnp.argsort(dst, stable=True)
        src = src[_o]
        dst = dst[_o]
        edge_type_8 = jax.random.randint(jax.random.fold_in(_gk, 12), (106250,), 0, 8, jnp.int32)
        return (x, src, dst, edge_type_8)
    x, src, dst, edge_type_8 = _rec_inputs()

    def _L0_gnn_setup():
        import jax, jax.numpy as jnp
        import numpy as np
        N_NODES = 6250
        N_EDGES = 100000
        D_IN = 256
        D_OUT = 256
        key = jax.random.key(seed)
        k1, k2, k3, k4 = jax.random.split(key, 4)
        bound = 1.0 / np.sqrt(D_IN)
        vertex_features = jax.random.normal(k1, (N_NODES, D_IN), dtype=jnp.float32)
        edge_index = jax.random.randint(k2, (2, N_EDGES), 0, N_NODES, dtype=jnp.int32)
        w0 = jax.random.uniform(k3, (D_IN, D_OUT), minval=-bound, maxval=bound, dtype=jnp.float32)
        w1 = jax.random.uniform(k4, (D_IN, D_OUT), minval=-bound, maxval=bound, dtype=jnp.float32)
        return {'vertex_features': vertex_features, 'edge_index': edge_index, 'w0': w0, 'w1': w1}
    _L0_gnn_all = _L0_gnn_setup()
    _L0_gnn_in = {k: v for k, v in _L0_gnn_all.items() if k in ('w0', 'w1')}
    del _L0_gnn_all

    def _L1_gnn_setup():
        import jax, jax.numpy as jnp
        import numpy as np
        N, E, R, H, D = (3750, 37500, 8, 8, 32)
        IN_F = 256
        NEG_SLOPE = 0.2
        key = jax.random.key(seed)
        k = jax.random.split(key, 6)
        x = jax.random.normal(k[0], (N, IN_F), dtype=jnp.float32)
        W = jax.random.normal(k[1], (R, H * D, IN_F), dtype=jnp.float32) * 0.05
        attn_src = jax.random.normal(k[2], (H, D), dtype=jnp.float32) * 0.1
        attn_dst = jax.random.normal(k[3], (H, D), dtype=jnp.float32) * 0.1
        edge_index = jax.random.randint(k[4], (2, E), 0, N, dtype=jnp.int64) if jax.config.read('jax_enable_x64') else jax.random.randint(k[4], (2, E), 0, N, dtype=jnp.int32)
        edge_type = jax.random.randint(k[5], (E,), 0, R, dtype=edge_index.dtype)
        return dict(x=x, W=W, attn_src=attn_src, attn_dst=attn_dst, edge_index=edge_index, edge_type=edge_type)
    _L1_gnn_all = _L1_gnn_setup()
    _L1_gnn_in = {k: v for k, v in _L1_gnn_all.items() if k in ('W', 'attn_src', 'attn_dst')}
    del _L1_gnn_all
    return {'x': x, 'src': src, 'dst': dst, 'edge_type_8': edge_type_8, 'L0_gnn_w0': _L0_gnn_in['w0'], 'L0_gnn_w1': _L0_gnn_in['w1'], 'L1_gnn_W': _L1_gnn_in['W'], 'L1_gnn_attn_src': _L1_gnn_in['attn_src'], 'L1_gnn_attn_dst': _L1_gnn_in['attn_dst']}

def reference(x, src, dst, edge_type_8, L0_gnn_w0, L0_gnn_w1, L1_gnn_W, L1_gnn_attn_src, L1_gnn_attn_dst):
    import jax
    import jax.numpy as jnp

    def _L0_gnn_ref(vertex_features, edge_index, w0, w1):
        import jax, jax.numpy as jnp
        import numpy as np
        N_NODES = 6250
        N_EDGES = 100000
        D_IN = 256
        D_OUT = 256
        w0_features = vertex_features @ w0
        w1_features = vertex_features @ w1
        dst, src = (edge_index[0], edge_index[1])
        messages = w1_features[src]
        neighbours = jax.ops.segment_sum(messages, dst, num_segments=vertex_features.shape[0])
        return jax.nn.relu(w0_features + neighbours)

    def _L1_gnn_ref(x, W, attn_src, attn_dst, edge_index, edge_type):
        import jax, jax.numpy as jnp
        import numpy as np
        N, E, R, H, D = (3750, 37500, 8, 8, 32)
        IN_F = 256
        NEG_SLOPE = 0.2
        n = x.shape[0]
        r = W.shape[0]
        h, d = attn_src.shape
        h_all = jnp.einsum('nf,rof->rno', x, W).reshape(r, n, h, d)
        src, dst = (edge_index[0], edge_index[1])
        h_src = h_all[edge_type, src]
        h_dst = h_all[edge_type, dst]
        scores = jnp.einsum('ehd,hd->eh', h_src, attn_src) + jnp.einsum('ehd,hd->eh', h_dst, attn_dst)
        scores = jnp.where(scores > 0, scores, NEG_SLOPE * scores)
        amax = jnp.maximum(jax.ops.segment_max(scores, dst, num_segments=n), 0.0)
        w = jnp.exp(scores - amax[dst])
        denom = jax.ops.segment_sum(w, dst, num_segments=n) + 1e-12
        w = w / denom[dst]
        msg = h_src * w[..., None]
        out = jax.ops.segment_sum(msg, dst, num_segments=n)
        return out.reshape(n, h * d)
    edge_index = jnp.stack([src, dst])
    x = _layernorm(x + _L0_gnn_ref(x, edge_index, L0_gnn_w0, L0_gnn_w1), axis=-1)
    x = _layernorm(x + _L1_gnn_ref(x, L1_gnn_W, L1_gnn_attn_src, L1_gnn_attn_dst, edge_index, edge_type_8), axis=-1)
    return x

_drawn_inputs = setup_inputs


def setup_inputs(seed=0):
    import zlib

    import numpy as np

    out = dict(_drawn_inputs(seed))
    spreads = {}
    factors = {}
    for name, (base, spread) in spreads.items():
        noise = np.random.default_rng([zlib.crc32(name.encode()), seed]).standard_normal(out[name].shape)
        drawn = base * np.exp(spread * noise) if base else spread * noise
        out[name] = jnp.asarray(drawn.astype(out[name].dtype))
    for name, factor in factors.items():
        out[name] = (out[name] * factor).astype(out[name].dtype)
    return out
```

```python
from contextlib import ExitStack

import concourse.bass as bass
from concourse import mybir

P = 128
F32 = mybir.dt.float32
BF16 = mybir.dt.bfloat16
I32 = mybir.dt.int32
I16 = mybir.dt.int16
ALU = mybir.AluOpType
ACT = mybir.ActivationFunctionType
X = mybir.AxisListType.X

BIG = 1.0e30
NO_NODE = 8191.0
LN_EPS = 1e-5
DEN_EPS = 1e-12
SLOPE = 0.2


def graph_layers(nc, x, xT, src, dst, etype, w0, w1, W, WT, attn_src, attn_dst, out):
    N, D = x.shape
    E = src.shape[0]
    R = W.shape[0]
    H, HD = attn_src.shape
    DC = D // P
    NT = -(-N // P) + 1
    NP_ = NT * P
    ET = -(-E // P)
    TAIL = E - (ET - 1) * P
    CHUNKS = 16
    LEN = -(-(ET + NT - 2) // CHUNKS)
    STEPS = CHUNKS * LEN
    BLK = -(-STEPS // P)
    KP = BLK * P
    FULL = (ET - 1) // P
    REST = (ET - 1) - FULL * P
    RH = R * H
    SCAN = LEN * P
    NACC = 4
    assert P == CHUNKS * H and  D == H * HD

    def dram(name, shape, dt):
        return nc.dram_tensor(name, shape, dt, kind="Internal").ap()

    edge_rows_d = dram("edge_rows_d", [KP, 4 * P], F32)
    step_rows_d = dram("step_rows_d", [KP, 2, P], I16)
    step_tile_d = dram("step_tile_d", [KP], I32)
    sums_d = [dram(f"sums_d{u}", [NP_, D], F32) for u in range(NACC)]
    ab_d = dram("ab_d", [NP_, RH], F32)
    b_d = dram("b_d", [NP_, RH], F32)
    h_d = dram("h_d", [NP_, R * D], F32)
    x1T_d = dram("x1T_d", [NP_, DC * P], F32)
    ends_d = dram("ends_d", [P, 4], F32)
    carry_d = dram("carry_d", [P, 2], F32)

    with ExitStack() as ctx:
        def sb(name, shape, dt):
            return ctx.enter_context(nc.sbuf_tensor(name, shape, dt))

        def sem(name):
            return ctx.enter_context(nc.semaphore(name))

        nodes = sb("nodes", [P, NT * D], F32)
        region = sb("region", [P, 2 * DC * NP_], F32)
        ZW = STEPS * H
        edge_z = sb("edge_z", [P, ZW], F32)
        dst_t = sb("dst_t", [P, KP], F32)
        type_t = sb("type_t", [P, KP], F32)
        local_t = sb("local_t", [P, KP], F32)
        idx_t = sb("idx_t", [P, KP], I32)
        mask_t = sb("mask_t", [P, KP], F32)
        ident = sb("ident", [P, P], F32)
        iota_row = sb("iota_row", [P, P], F32)
        before = sb("before", [P, P], BF16)
        part = sb("part", [P, 1], F32)
        minus_half = sb("minus_half", [P, 1], F32)
        iota8 = sb("iota8", [P, R], F32)
        idx_slot = sb("idx_slot", [P, 16], I32)
        ps = ctx.enter_context(nc.psum_tensor("ps", [P, 8, 512], F32))
        HALF = DC * NP_
        assert D * NT <= HALF

        def view(base, at, *shape):
            n = 1
            for s in shape:
                n *= s
            v = base[:, at:at + n]
            names = "abcd"[:len(shape)]
            if len(shape) > 1:
                v = v.rearrange(f"p ({' '.join(names)}) -> p {' '.join(names)}",
                                **{k: s for k, s in zip(names, shape)})
            return v

        o = 0
        rows_i = view(nodes, o, 3, BLK, P).bitcast(I32); o += 3 * BLK * P
        rows_f = view(nodes, o, BLK, 4 * P); o += BLK * 4 * P
        step_f = view(nodes, o, BLK, 4 * P); o += BLK * 4 * P
        firsts = view(nodes, o, KP); o += KP
        cmp = view(nodes, o, KP); o += KP
        step_local = view(nodes, o, BLK, P); o += BLK * P
        assert o <= NT * D
        w_nat = view(region, HALF, R, DC, D)
        o = 2 * KP + 2 * DC * D
        step16 = view(edge_z, o, BLK * P).bitcast(I16).rearrange("p (b a e) -> p b a e", b=BLK, a=2); o += BLK * P
        misc = view(edge_z, o, 512); o += 512
        xs0 = [view(edge_z, o + DC * P * h, DC, P) for h in range(2)]; o += 2 * DC * P
        assert o <= ZW
        NZ = 800
        ki = misc[:, 0:8].bitcast(I32)
        kt = misc[:, 8:16].bitcast(I32)
        kf = misc[:, 16:24]
        kh = misc[:, 24:32]
        jfi = misc[:, 32:40].bitcast(I32)
        cf = misc[:, 40:48]
        i_f = misc[:, 48:56]
        j_f = misc[:, 56:64]
        j128 = misc[:, 64:72]
        i_i = misc[:, 72:80].bitcast(I32)
        j_i = misc[:, 80:88].bitcast(I32)
        acol = misc[:, 96:96 + 2 * DC].rearrange("p (a c) -> p a c", a=2)
        hsel = misc[:, 104:108]
        q32 = misc[:, 108:109]
        tmp4 = misc[:, 112:116]
        it_i = misc[:, 128:256].bitcast(I32)
        pt_i = misc[:, 256:257].bitcast(I32)
        blk = misc[:, 264:264 + DC * 2 * H].rearrange("p (c n) -> p c n", c=DC)
        tile_row = sb("tile_row", [1, KP], I32)
        wab = sb("wab", [P, DC, 2 * RH], F32)

        xT_sb = view(region, 0, DC, NP_)
        y_sb = view(region, HALF, NT * D)
        o = 0
        src_t = view(edge_z, o, KP); o += KP
        trash_t = view(edge_z, o, KP); o += KP
        w0_sb = view(edge_z, o, DC, D); o += DC * D
        w1_sb = view(edge_z, o, DC, D); o += DC * D
        eq = [view(edge_z, o + 256 * h, 256).bitcast(BF16).rearrange("p (u e) -> p u e", u=4) for h in range(2)]; o += 512
        onehot = [view(edge_z, o + 256 * h, 256).bitcast(BF16).rearrange("p (u e) -> p u e", u=4) for h in range(2)]; o += 512
        counts = [view(edge_z, o + 512 * h, 4, P) for h in range(2)]; o += 1024
        xs = [view(edge_z, o + DC * P * h, DC, P) for h in range(2)]; o += 2 * DC * P
        sums = [sb("sums0", [P, 4, D], F32)]
        zeros = sums[0][:, :, :].rearrange("p u n -> p (u n)")[:, 0:NZ]
        sums.append(view(edge_z, o, 4, D)); o += 4 * D
        eqj = view(edge_z, o, 2 * P).bitcast(BF16).rearrange("p (u e) -> p u e", u=4); o += 2 * P
        assert o <= ZW
        row16 = [sb(f"row16_{h}", [P, 4, P], I16) for h in range(2)]
        dup = sb("dup", [P, 8], F32)
        dup2 = sb("dup2", [P, 8], F32)

        o = 2 * KP + 2 * DC * D
        parts = [view(edge_z, o + NACC * D * h, NACC, D) for h in range(1)]; o += NACC * D
        parts.append(sums[0])
        o2 = 2 * KP + 2 * DC * D + 512 + 512 + 1024 + 2 * DC * P
        o = o2
        xn = [view(edge_z, o + D * h, D) for h in range(2)]; o += 2 * D
        xts = [view(edge_z, 0 + DC * P * h, DC, P) for h in range(2)]
        ab_s = [view(edge_z, 2 * DC * P + 2 * RH * h, 2 * RH) for h in range(2)]
        assert o <= ZW
        tmp = [view(edge_z, KP + D * h, D) for h in range(2)]
        stats = [sb(f"stats{h}", [P, 6], F32) for h in range(2)]
        veps = [sb(f"veps{h}", [P, 1], F32) for h in range(2)]
        agg2 = [sb(f"agg2_{h}", [P, 2], F32) for h in range(2)]
        rstd = [sb(f"rstd{h}", [P, 1], F32) for h in range(2)]

        o = 0
        wT_sb = view(region, o, DC, R * D); o += DC * R * D
        h_out = view(region, o, 4, 512); o += 2048
        b_sb = view(region, o, NT * RH); o += NT * RH
        st = [view(region, o + 4 * P * h, 4, P) for h in range(2)]; o += 8 * P
        prod = view(region, o, 4, H, R); o += 4 * RH
        tmask = view(region, o, 4, R); o += 4 * R
        bsel = view(region, o, 4, H); o += 4 * H
        zt = view(region, o, 4, H); o += 4 * H
        zl = view(region, o, 4, H); o += 4 * H
        a_slot = view(region, o, 16, H); o += 16 * H
        x1s = view(region, o, DC, P); o += DC * P
        zblock = view(region, o, 16, H); o += P
        dblock = view(region, o, CHUNKS, H); o += P
        assert o <= HALF
        o = HALF
        keep = view(region, o, SCAN + 1); o += SCAN + 1
        d_row = view(region, o, P + 1); o += P + 1
        s_row = view(region, o, P); o += P
        run = view(region, o, P); o += P
        lead = view(region, o, P); o += P
        led = view(region, o, P); o += P
        lmax = view(region, o, 2); o += 2
        d_first = view(region, o, 1); o += 1
        d_prev = view(region, o, 1); o += 1
        d_next = view(region, o, 1); o += 1
        k_first = view(region, o, 2); o += 2
        ends = view(region, o, 4); o += 4
        carry = view(region, o, 2); o += 2
        crow = view(region, o, CHUNKS, 4); o += 4 * CHUNKS
        cres = view(region, o, 2, CHUNKS + 1); o += 2 * (CHUNKS + 1)
        assert o <= 2 * HALF
        fwd = view(region, 0, SCAN)
        s_T = view(edge_z, 0, SCAN)

        AW = D + H
        o = 0
        acc = view(region, o, NT * AW); o += NT * AW
        h_slot = view(region, o, 16, D); o += 16 * D
        msg = view(region, o, 8, AW); o += 8 * AW
        sel = view(region, o, 8, P); o += 8 * P
        e_row = view(region, o, P); o += P
        w_col = view(region, o, 16, H); o += P
        den = [view(region, o + 2 * H * h, 2, H) for h in range(2)]; o += 4 * H
        res = [view(region, o + D * h, D) for h in range(2)]; o += 2 * D
        fin = [view(region, o + D * h, D) for h in range(2)]; o += 2 * D
        assert o <= 2 * HALF

        names = """pads_set edges_in weights_in iotas setup rows_stored firsts_made step_rows steps_stored
            tables_ps tables_out local_out wab_ps x_in xT_in nodes_padded y_x y_ps y_done zeroed
            onehots eq_used dup_scaled slots_ready counts_made counts_copied sums_made sums_copied
            pooled parts_used x0_x x0_ps x0_used relu_made stats_made stats_seen aggr_made veps_made rstd_made
            xn_made x1_kept xt_ps xts_made ab_ps ab_copied
            tabs_in idx_ready x1s_in h_made h_copied st_built mask_made b_made prod_made bsel_made z_made
            z_sloped scored dblock_made turned block_out keep_made run_made lead_made led_made lmax_made
            blocks_done first_turned first_out ends_made borders_in ends_io carry_io shifted
            exps w_turned w_ready w_placed acc_zero pool_turns msgs segs added
            den_made rden_made res_made sum_made fstats_made fstats_seen faggr_made fveps_made frstd_made
            fin_made""".split()
        (pads_set, edges_in, weights_in, iotas, setup, rows_stored, firsts_made, step_rows, steps_stored,
         tables_ps, tables_out, local_out, wab_ps, x_in, xT_in, nodes_padded, y_x, y_ps, y_done, zeroed,
         onehots, eq_used, dup_scaled, slots_ready, counts_made, counts_copied, sums_made, sums_copied,
         pooled, parts_used, x0_x, x0_ps, x0_used, relu_made, stats_made, stats_seen, aggr_made, veps_made, rstd_made,
         xn_made, x1_kept, xt_ps, xts_made, ab_ps, ab_copied,
         tabs_in, idx_ready, x1s_in, h_made, h_copied, st_built, mask_made, b_made, prod_made, bsel_made, z_made,
         z_sloped, scored, dblock_made, turned, block_out, keep_made, run_made, lead_made, led_made, lmax_made,
         blocks_done, first_turned, first_out, ends_made, borders_in, ends_io, carry_io, shifted,
         exps, w_turned, w_ready, w_placed, acc_zero, pool_turns, msgs, segs, added,
         den_made, rden_made, res_made, sum_made, fstats_made, fstats_seen, faggr_made, fveps_made, frstd_made,
         fin_made) = [sem(n) for n in names]
        row_in = [sem(f"row_in{h}") for h in range(2)]
        drow_in = [sem(f"drow_in{h}") for h in range(2)]
        parts_in = [sem(f"parts_in{h}") for h in range(2)]
        node_out = [sem(f"node_out{h}") for h in range(2)]
        stored = [sem(f"stored{h}") for h in range(2)]
        h_stored = [sem(f"h_stored{q}") for q in range(4)]
        scattered = [[sem(f"scattered{h}{u}") for u in range(4)] for h in range(2)]
        gath = [sem(f"gath{k}") for k in range(16)]

        block = ctx.enter_context(nc.Block())
        ds = bass.ds
        NQ = STEPS // 4
        ITN = NT // 2
        ITS = LEN
        assert NT % 2 == 0 and NT < ITS
        SU = {}

        def rows_left(eng, h, times):
            if isinstance(times, int) and times <= 0:
                return
            for u in range(4):
                eng.wait_ge(scattered[h][u], 16 * times)

        def read_tiles(eng, at, n):
            regs = [eng.alloc_register(f"tile{k}_{nc.next_id()}") for k in range(n)]
            eng.load(regs, tile_row[0:1, ds(at, n)])
            return [eng.snap(r, min_val=0, max_val=NT - 1) for r in regs]

        @block.vector
        def _(v):
            n = [0]

            def do(ins):
                n[0] += 1
                ins.then_inc(setup, 1)
                v.wait_ge(setup, n[0])

            for a, pad in enumerate((int(NO_NODE), 0, 0)):
                v.memset(rows_i[:, a, FULL, :], pad).then_inc(pads_set, 1)
            v.memset(zeros, 0.0).then_inc(pads_set, 1)
            v.memset(xT_sb[:, :, N:NP_], 0.0).then_inc(pads_set, 1)
            v.memset(minus_half[:, :], -0.5).then_inc(pads_set, 1)
            v.wait_ge(iotas, 2)
            do(v.tensor_copy(iota_row[:, :], it_i))
            do(v.tensor_copy(part[:, :], pt_i))
            do(v.tensor_copy(iota8[:, :], it_i[:, 0:R]))
            do(v.tensor_scalar(ident[:, :], iota_row[:, :], part[:, 0:1], None, ALU.is_equal))
            do(v.tensor_scalar(before[:, :], iota_row[:, :], part[:, 0:1], None, ALU.is_lt))
            do(v.tensor_scalar(ki[:, 0:1], pt_i, CHUNKS - 1, None, ALU.bitwise_and))
            do(v.tensor_scalar(kt[:, 0:1], pt_i, 4, None, ALU.logical_shift_right))
            do(v.tensor_copy(kh[:, 0:1], ki[:, 0:1]))
            do(v.tensor_copy(kh[:, 1:2], kt[:, 0:1]))
            do(v.scalar_tensor_tensor(out=kh[:, 2:3], in0=kh[:, 0:1], scalar=float(LEN), in1=kh[:, 1:2],
                                      op0=ALU.mult, op1=ALU.add))
            for b in range(BLK):
                last = v.tensor_scalar(kf[:, b:b + 1], kh[:, 2:3], float(P // CHUNKS * b), None, ALU.add)
            do(last)
            v.wait_ge(edges_in, 16 * 9)
            for a in range(3):
                last = v.tensor_copy(rows_f[:, :, a * P:(a + 1) * P], rows_i[:, a, :, :])
            do(last)
            do(v.scalar_tensor_tensor(out=rows_f[:, :, 3 * P:4 * P], in0=rows_f[:, :, P:2 * P], scalar=float(R),
                                      in1=rows_f[:, :, 2 * P:3 * P], op0=ALU.mult, op1=ALU.add))
            SU["rows"] = n[0]
            do(v.tensor_scalar(jfi[:, 0:BLK], rows_i[:, 0, :, 0], 7, None, ALU.logical_shift_right))
            do(v.tensor_copy(cf[:, 0:BLK], jfi[:, 0:BLK]))
            for b in range(BLK):
                last = v.tensor_scalar(cf[:, b:b + 1], cf[:, b:b + 1], part[:, 0:1], float(P * b), ALU.add, ALU.add)
            do(last)
            SU["firsts"] = n[0]
            v.wait_ge(firsts_made, 1)
            do(v.tensor_copy(firsts, ps[:, 4:6, :].rearrange("p a n -> p (a n)")[:, 0:KP]))
            for b in range(BLK):
                do(v.tensor_scalar(cmp[:, 1:ET], firsts[:, 1:ET], kf[:, b:b + 1], None, ALU.is_le))
                do(v.tensor_reduce(i_f[:, b:b + 1], cmp[:, 1:ET], X, ALU.add))
            do(v.tensor_tensor(j_f[:, 0:BLK], kf[:, 0:BLK], i_f[:, 0:BLK], ALU.subtract))
            do(v.tensor_scalar(j128[:, 0:BLK], j_f[:, 0:BLK], float(P), None, ALU.mult))
            do(v.tensor_copy(i_i[:, 0:BLK], i_f[:, 0:BLK]))
            do(v.tensor_copy(j_i[:, 0:BLK], j_f[:, 0:BLK]))
            SU["tiles"] = n[0]
            v.wait_ge(weights_in, 80)
            do(v.memset(blk, 0.0))
            for h in range(H // DC):
                do(v.tensor_scalar(hsel[:, h:h + 1], part[:, 0:1], float(HD * h), None, ALU.is_ge))
                do(v.tensor_scalar(tmp4[:, h:h + 1], part[:, 0:1], float(HD * (h + 1)), None, ALU.is_lt))
            do(v.tensor_tensor(hsel[:, 0:4], hsel[:, 0:4], tmp4[:, 0:4], ALU.mult))
            for c in range(DC):
                for a in range(2):
                    last = v.tensor_scalar(blk[:, c, a * H + 4 * c:a * H + 4 * c + 4], hsel[:, 0:4],
                                           acol[:, a, c:c + 1], None, ALU.mult)
            do(last)
            SU["blk"] = n[0]
            v.wait_ge(step_rows, 16 * BLK)
            for b in range(BLK):
                last = v.tensor_scalar(step_local[:, b, :], step_f[:, b, 0:P], j128[:, b:b + 1], None, ALU.subtract)
            do(last)
            SU["local"] = n[0]
            do(v.tensor_copy(step16[:, :, 0, :], step_f[:, :, P:2 * P]))
            do(v.tensor_copy(step16[:, :, 1, :], step_local))
            SU["step16"] = n[0]
            for b in range(BLK):
                v.wait_ge(tables_ps, b + 1)
                v.tensor_copy(local_t[:, b * P:b * P + P], ps[:, 2 * (b % 2) + 1, 0:P]).then_inc(local_out, 1)
            v.wait_ge(tables_out, BLK)
            v.wait_ge(local_out, BLK)
            do(v.tensor_scalar(mask_t[:, :], local_t[:, :], 0.0, None, ALU.is_ge))
            do(v.scalar_tensor_tensor(out=mask_t[:, :], in0=local_t[:, :], scalar=float(P), in1=mask_t[:, :],
                                      op0=ALU.is_lt, op1=ALU.mult))
            do(v.tensor_scalar(mask_t[:, :], mask_t[:, :], BIG, -BIG, ALU.mult, ALU.add))
            do(v.tensor_scalar(part[:, :], part[:, :], float(N), None, ALU.add))
            do(v.tensor_scalar(trash_t, src_t, -1.0, part[:, 0:1], ALU.mult, ALU.add))
            do(v.tensor_scalar(part[:, :], part[:, :], float(-N), None, ALU.add))
            v.wait_ge(wab_ps, 1)
            wps = ps[:, 6, 0:DC * 2 * RH].rearrange("p (c r a h) -> p c r a h", c=DC, r=R, a=2)
            for c in range(DC):
                v.tensor_copy(wab[:, c, 0:RH].rearrange("p (r h) -> p r h", r=R), wps[:, c, :, 0, :])
                last = v.tensor_copy(wab[:, c, RH:2 * RH].rearrange("p (h r) -> p r h", r=R), wps[:, c, :, 1, :])
            do(last)
            SU["end"] = n[0]

            v.wait_ge(rows_stored, 16)
            v.memset(nodes[:, N // P * D:NT * D], 0.0).then_inc(nodes_padded, 1)

            v.wait_ge(wab_ps, 1)
            v.wait_ge(steps_stored, 32)
            v.wait_ge(y_x, NT)
            v.sem_inc(eq_used, 2)

            def match_sources(it):
                for q in range(4):
                    h, g, k = q % 2, 4 * it + q, 16 * it + 4 * q
                    v.wait_ge(counts_made, g + 1)
                    v.tensor_tensor(onehot[h], iota_row[:, :].unsqueeze(1).to_broadcast([P, 4, P]),
                                    local_t[:, ds(k, 4)].unsqueeze(2).to_broadcast([P, 4, P]), ALU.is_equal)
                    v.wait_ge(row_in[h], 16 * (2 * it + q // 2 + 1))
                    for u in range(4):
                        last = v.tensor_scalar(eq[h][:, u, :], row16[h][:, u, :], src_t[:, ds(k + u, 1)],
                                               None, ALU.is_equal)
                    last.then_inc(onehots, 1)
                    v.wait_ge(onehots, g + 1)
                    for u in range(4):
                        last = v.tensor_tensor_reduce(out=eqj[:, u, :], in0=eq[h][:, u, :], in1=before[:, :], scale=1.0,
                                                      scalar=0.0, op0=ALU.mult, op1=ALU.add,
                                                      accum_out=dup[:, 4 * h + u:4 * h + u + 1])
                    last.then_inc(eq_used, 1)
                    v.wait_ge(eq_used, g + 3)
                    v.scalar_tensor_tensor(out=dup2[:, 4 * h:4 * h + 4], in0=dup[:, 4 * h:4 * h + 4], scalar=1.0,
                                           in1=trash_t[:, ds(k, 4)], op0=ALU.min,
                                           op1=ALU.mult).then_inc(dup_scaled, 1)
                    v.wait_ge(dup_scaled, g + 1)
                    rows_left(v, h, 2 * it + q // 2 - 1)
                    v.tensor_tensor(idx_slot[:, 4 * q:4 * q + 4], dup2[:, 4 * h:4 * h + 4],
                                    src_t[:, ds(k, 4)], ALU.add).then_inc(slots_ready, 1)

            match_sources(0)
            with v.Fori(1, ITS) as it:
                match_sources(it)

            v.wait_ge(sums_copied, NQ + 2)
            v.wait_ge(x_in, 32)
            for h in range(2):
                rows_left(v, h, 2 * ITS)
            v.sem_inc(parts_used, 2)
            v.sem_inc(x0_used, 2)
            with v.Fori(0, ITN) as it:
                for h in range(2):
                    v.wait_ge(pooled, 2 * it + h + 1)
                    v.tensor_tensor(tmp[h], parts[h][:, 0, :], parts[h][:, 1, :], ALU.add).then_inc(parts_used, 1)
                for h in range(2):
                    v.wait_ge(x0_ps, 2 * it + h + 3)
                    v.wait_ge(parts_used, 2 * it + h + 3)
                    v.tensor_tensor(tmp[h], ps[:, h, 0:D], tmp[h], ALU.add).then_inc(x0_used, 1)
                for h in range(2):
                    v.wait_ge(x0_used, 2 * it + h + 3)
                    v.scalar_tensor_tensor(out=tmp[h], in0=tmp[h], scalar=0.0, in1=nodes[:, ds((2 * it + h) * D, D)],
                                           op0=ALU.max, op1=ALU.add).then_inc(relu_made, 1)
                for h in range(2):
                    v.wait_ge(relu_made, 2 * it + h + 1)
                    v.bn_stats(stats[h][:, :], tmp[h]).then_inc(stats_made, 1)
                for h in range(2):
                    v.wait_ge(stats_made, 2 * it + h + 1)
                    v.sem_inc(stats_seen, 1)
                    v.bn_aggr(agg2[h][:, :], stats[h][:, :]).then_inc(aggr_made, 1)
                for h in range(2):
                    v.wait_ge(aggr_made, 2 * it + h + 1)
                    v.tensor_scalar(veps[h][:, :], agg2[h][:, 1:2], LN_EPS, None, ALU.add).then_inc(veps_made, 1)
                for h in range(2):
                    v.wait_ge(rstd_made, 2 * it + h + 1)
                    v.wait_ge(xt_ps, 2 * it + h + 1)
                    v.wait_ge(x1_kept, 2 * it + h + 1)
                    v.tensor_scalar(xn[h], tmp[h], agg2[h][:, 0:1], rstd[h][:, 0:1], ALU.subtract,
                                    ALU.mult).then_inc(xn_made, 1)

            v.wait_ge(tabs_in, 32)
            v.wait_ge(x1_kept, NT + 2)
            v.memset(run, 0.0)
            v.memset(lead, 1.0)
            v.memset(lmax, 0.0).then_inc(keep_made, 1)
            v.wait_ge(first_turned, 1)
            v.tensor_copy(d_first, ps[:, 5, 0:1])
            v.tensor_copy(d_row[:, 0:1], ps[:, 5, 0:1]).then_inc(first_out, 1)
            v.sem_inc(st_built, 2)
            v.sem_inc(scored, 4)
            v.sem_inc(blocks_done, 1)

            def score(it):
                for q in range(4):
                    g, h, k = 4 * it + q, q % 2, 16 * it + 4 * q
                    v.wait_ge(drow_in[h], 16 * (2 * it + q // 2 + 1))
                    v.wait_ge(b_made, g + 1)
                    for u in range(4):
                        last = v.tensor_scalar(st[h][:, u, :], row16[h][:, u, :], part[:, 0:1], None, ALU.is_equal)
                    last.then_inc(st_built, 1)
                    v.tensor_tensor(tmask, type_t[:, ds(k, 4)].unsqueeze(2).to_broadcast([P, 4, R]),
                                    iota8[:, :].unsqueeze(1).to_broadcast([P, 4, R]), ALU.is_equal).then_inc(mask_made, 1)
                    v.wait_ge(mask_made, g + 1)
                    v.wait_ge(b_made, g + 3)
                    v.tensor_tensor(prod, ps[:, h, 0:4 * RH].rearrange("p (u h r) -> p u h r", u=4, h=H),
                                    tmask.unsqueeze(2).to_broadcast([P, 4, H, R]), ALU.mult).then_inc(prod_made, 1)
                    v.wait_ge(prod_made, g + 1)
                    v.tensor_reduce(bsel, prod, X, ALU.add).then_inc(bsel_made, 1)
                    v.wait_ge(bsel_made, g + 1)
                    for u in range(4):
                        v.wait_ge(gath[4 * q + u], 16 * (it + 1))
                    v.tensor_tensor(zt, a_slot[:, 4 * q:4 * q + 4, :], bsel, ALU.add).then_inc(z_made, 1)
                    v.wait_ge(z_made, g + 1)
                    v.scalar_tensor_tensor(out=zl, in0=zt, scalar=SLOPE, in1=zt, op0=ALU.mult,
                                           op1=ALU.max).then_inc(z_sloped, 1)
                    v.wait_ge(z_sloped, g + 1)
                    v.tensor_tensor(zblock[:, 4 * q:4 * q + 4, :], zl,
                                    mask_t[:, ds(k, 4)].unsqueeze(2).to_broadcast([P, 4, H]),
                                    ALU.add).then_inc(scored, 1)
                at = ds(it * P, P)
                v.wait_ge(block_out, it + 1)
                v.tensor_tensor(keep[:, at], d_row[:, 1:P + 1], d_row[:, 0:P], ALU.is_equal).then_inc(keep_made, 1)
                v.wait_ge(keep_made, it + 2)
                v.tensor_tensor_scan(run, keep[:, at], s_row, run[:, P - 1:P], ALU.mult, ALU.max).then_inc(run_made, 1)
                v.tensor_tensor_scan(lead, keep[:, at], keep[:, at], lead[:, P - 1:P], ALU.mult,
                                     ALU.mult).then_inc(lead_made, 1)
                v.tensor_copy(d_row[:, 0:1], d_row[:, P:P + 1])
                v.wait_ge(lead_made, it + 1)
                v.tensor_tensor(led, lead, s_row, ALU.mult).then_inc(led_made, 1)
                v.wait_ge(led_made, it + 1)
                v.tensor_reduce(lmax[:, 1:2], led, X, ALU.max).then_inc(lmax_made, 1)
                v.wait_ge(lmax_made, it + 1)
                v.tensor_tensor(lmax[:, 0:1], lmax[:, 0:1], lmax[:, 1:2], ALU.max).then_inc(blocks_done, 1)
                v.wait_ge(run_made, it + 1)

            v.wait_ge(keep_made, 1)
            v.wait_ge(first_out, 1)
            with v.Fori(0, ITS) as it:
                score(it)
                v.wait_ge(blocks_done, it + 2)

            v.memset(d_prev, -1.0)
            v.memset(d_next, -1.0).then_inc(ends_made, 1)
            v.wait_ge(borders_in, 32)
            v.tensor_tensor(k_first[:, 0:1], d_first, d_prev, ALU.is_equal)
            v.tensor_tensor(k_first[:, 1:2], d_row[:, 0:1], d_next, ALU.is_equal).then_inc(ends_made, 1)
            v.wait_ge(ends_made, 2)
            v.tensor_copy(keep[:, 0:1], k_first[:, 0:1])
            v.tensor_copy(keep[:, SCAN:SCAN + 1], k_first[:, 1:2])
            v.tensor_copy(ends[:, 0:1], run[:, P - 1:P])
            v.tensor_copy(ends[:, 2:3], lmax[:, 0:1])
            v.tensor_tensor(ends[:, 1:2], lead[:, P - 1:P], k_first[:, 0:1], ALU.mult)
            v.tensor_tensor(ends[:, 3:4], lead[:, P - 1:P], k_first[:, 1:2], ALU.mult).then_inc(ends_made, 1)
            v.memset(cres[0:H, 0, 0:1], 0.0)
            v.memset(cres[0:H, 1, CHUNKS:CHUNKS + 1], 0.0)
            v.wait_ge(ends_io, 32)
            v.tensor_tensor_scan(cres[0:H, 0, 1:CHUNKS + 1], crow[0:H, :, 1], crow[0:H, :, 0], 0.0, ALU.mult, ALU.max)
            v.tensor_tensor_scan(cres[0:H, 1, 0:CHUNKS][:, ::-1], crow[0:H, :, 3][:, ::-1], crow[0:H, :, 2][:, ::-1],
                                 0.0, ALU.mult, ALU.max).then_inc(ends_made, 1)
            v.wait_ge(carry_io, 48)
            v.tensor_tensor_scan(fwd, keep[:, 0:SCAN], s_T, carry[:, 0:1], ALU.mult, ALU.max).then_inc(shifted, 1)
            v.wait_ge(shifted, 1)
            v.tensor_tensor_scan(fwd[:, ::-1], keep[:, 1:SCAN + 1][:, ::-1], fwd[:, ::-1], carry[:, 1:2],
                                 ALU.mult, ALU.max).then_inc(shifted, 1)
            v.wait_ge(shifted, 2)
            v.tensor_tensor(s_T, s_T, fwd, ALU.subtract).then_inc(shifted, 1)
            v.wait_ge(shifted, 3)

            v.memset(acc, 0.0).then_inc(acc_zero, 1)
            v.wait_ge(acc_zero, 1)
            def add_sums(g, tile):
                for u in range(4):
                    v.wait_ge(segs, 4 * g + u + 9)
                    v.wait_ge(added, 4 * g + u + 4)
                    v.tensor_tensor(acc[:, ds(tile[u] * AW, AW)], ps[:, u, 0:AW], acc[:, ds(tile[u] * AW, AW)],
                                    ALU.add).then_inc(added, 1)

            def weigh(it, q):
                h = q % 2
                v.tensor_tensor(sel[:, 4 * h:4 * h + 4, :], iota_row[:, :].unsqueeze(1).to_broadcast([P, 4, P]),
                                local_t[:, ds(16 * it + 4 * q, 4)].unsqueeze(2).to_broadcast([P, 4, P]), ALU.is_equal)
                if q == 0:
                    v.wait_ge(w_ready, it + 1)
                for u in range(4):
                    v.wait_ge(gath[4 * q + u], 16 * (ITS + it + 1))
                v.tensor_tensor(msg[:, 4 * h:4 * h + 4, 0:D].rearrange("p u (h d) -> p u h d", h=H),
                                h_slot[:, 4 * q:4 * q + 4, :].rearrange("p u (h d) -> p u h d", h=H),
                                w_col[:, 4 * q:4 * q + 4, :].unsqueeze(3).to_broadcast([P, 4, H, HD]),
                                ALU.mult).then_inc(msgs, 1)

            v.sem_inc(added, 4)
            tile = read_tiles(v, 0, 12)
            for q in range(4):
                weigh(0, q)
                if q:
                    add_sums(q - 1, tile[4 * q - 4:4 * q])
            with v.Fori(1, ITS) as it:
                tile = read_tiles(v, 16 * it - 4, 16)
                for q in range(4):
                    weigh(it, q)
                    add_sums(4 * it + q - 1, tile[4 * q:4 * q + 4])
            add_sums(NQ - 1, read_tiles(v, STEPS - 4, 4))
            v.wait_ge(added, STEPS + 4)

            v.sem_inc(fin_made, 2)
            for h in range(2):
                v.sem_inc(stored[h], 16)
            with v.Fori(0, ITN) as it:
                for h in range(2):
                    v.tensor_scalar(den[h][:, 0, :], acc[:, ds((2 * it + h) * AW + D, H)], DEN_EPS, None,
                                    ALU.add).then_inc(den_made, 1)
                for h in range(2):
                    v.wait_ge(den_made, 2 * it + h + 1)
                    v.reciprocal(den[h][:, 1, :], den[h][:, 0, :]).then_inc(rden_made, 1)
                for h in range(2):
                    v.wait_ge(rden_made, 2 * it + h + 1)
                    v.tensor_tensor(res[h].rearrange("p (h d) -> p h d", h=H),
                                    acc[:, ds((2 * it + h) * AW, D)].rearrange("p (h d) -> p h d", h=H),
                                    den[h][:, 1, :].unsqueeze(2).to_broadcast([P, H, HD]), ALU.mult).then_inc(res_made, 1)
                for h in range(2):
                    v.wait_ge(res_made, 2 * it + h + 1)
                    v.tensor_tensor(res[h], res[h], nodes[:, ds((2 * it + h) * D, D)], ALU.add).then_inc(sum_made, 1)
                for h in range(2):
                    v.wait_ge(sum_made, 2 * it + h + 1)
                    v.bn_stats(stats[h][:, :], res[h]).then_inc(fstats_made, 1)
                for h in range(2):
                    v.wait_ge(fstats_made, 2 * it + h + 1)
                    v.sem_inc(fstats_seen, 1)
                    v.bn_aggr(agg2[h][:, :], stats[h][:, :]).then_inc(faggr_made, 1)
                for h in range(2):
                    v.wait_ge(faggr_made, 2 * it + h + 1)
                    v.tensor_scalar(veps[h][:, :], agg2[h][:, 1:2], LN_EPS, None, ALU.add).then_inc(fveps_made, 1)
                for h in range(2):
                    v.wait_ge(frstd_made, 2 * it + h + 1)
                    v.wait_ge(stored[h], 16 * (it + 1))
                    v.tensor_scalar(fin[h], res[h], agg2[h][:, 0:1], rstd[h][:, 0:1], ALU.subtract,
                                    ALU.mult).then_inc(fin_made, 1)

        @block.sync
        def _(sp):
            sp.wait_ge(pads_set, 3)
            for a, arr in enumerate((dst, src, etype)):
                sp.dma_start(rows_i[:, a, 0:FULL, :],
                             arr[0:FULL * P * P].rearrange("(b p e) -> p b e", p=P, e=P)).then_inc(edges_in, 16)
                sp.dma_start(rows_i[0:REST, a, FULL, :],
                             arr[FULL * P * P:(ET - 1) * P].rearrange("(p e) -> p e", e=P)).then_inc(edges_in, 16)
                sp.dma_start(rows_i[REST:REST + 1, a, FULL, 0:TAIL],
                             arr[(ET - 1) * P:E].rearrange("(p e) -> p e", p=1)).then_inc(edges_in, 16)
            for a, att in enumerate((attn_src, attn_dst)):
                sp.dma_start(acol[:, a, :], att.rearrange("h d -> (h d)").rearrange("(c p) -> p c", p=P),
                             allow_slow_non_contiguous=True).then_inc(weights_in, 16)
            sp.dma_start(w_nat, W.rearrange("r (c p) f -> p r c f", p=P)).then_inc(weights_in, 16)
            sp.dma_start(w0_sb, w0.rearrange("(c p) n -> p c n", p=P)).then_inc(weights_in, 16)
            sp.dma_start(w1_sb, w1.rearrange("(c p) n -> p c n", p=P)).then_inc(weights_in, 16)
            sp.dma_start(xT_sb[:, :, 0:N], xT.rearrange("(c p) n -> p c n", p=P)).then_inc(xT_in, 16)
            sp.wait_ge(setup, SU["rows"])
            sp.dma_start(edge_rows_d.rearrange("(b p) n -> p b n", p=P), rows_f).then_inc(rows_stored, 16)
            sp.wait_ge(pads_set, 4)
            for u in range(NACC):
                sp.dma_start(sums_d[u].rearrange("(p n) w -> p (n w)", p=P).rearrange("p (a n) -> p a n", n=NZ),
                             zeros.unsqueeze(1).to_broadcast([P, HALF // NZ, NZ])).then_inc(zeroed, 16)
            sp.wait_ge(setup, SU["tiles"])
            sp.dma_start(step_tile_d.rearrange("(b p) -> p b", p=P), j_i[:, 0:BLK],
                         allow_slow_non_contiguous=True).then_inc(steps_stored, 16)
            sp.wait_ge(setup, SU["step16"])
            sp.dma_start(step_rows_d.rearrange("(b p) a e -> p b a e", p=P), step16).then_inc(steps_stored, 16)
            sp.wait_ge(steps_stored, 32)
            sp.dma_start(tile_row[:, :], step_tile_d.rearrange("(a k) -> a k", a=1)).then_inc(steps_stored, 16)
            sp.wait_ge(steps_stored, 48)

            def source_rows(it):
                for q in range(4):
                    sp.wait_ge(eq_used, 4 * it + q + 1)
                    sp.dma_start(row16[q % 2][:, :, :],
                                 step_rows_d[ds(16 * it + 4 * q, 4), 0, :].partition_broadcast(P)).then_inc(row_in[q % 2], 16)

            source_rows(0)
            sp.wait_ge(setup, SU["end"])
            sp.wait_ge(tables_out, BLK)
            sp.wait_ge(nodes_padded, 1)
            NF = N // P
            sp.dma_start(nodes[:, 0:NF * D].rearrange("p (t w) -> p t w", w=D),
                         x[0:NF * P, :].rearrange("(t p) w -> p t w", p=P)).then_inc(x_in, 16)
            sp.dma_start(nodes[0:N - NF * P, NF * D:(NF + 1) * D], x[NF * P:N, :]).then_inc(x_in, 16)
            with sp.Fori(1, ITS) as it:
                source_rows(it)

            for h in range(2):
                rows_left(sp, h, 2 * ITS)
            with sp.Fori(0, ITN) as it:
                for h in range(2):
                    sp.wait_ge(parts_used, 2 * it + h + 1)
                    for u in range(NACC):
                        sp.dma_start(parts[h][:, u, :], sums_d[u][ds((2 * it + h) * P, P), :]).then_inc(parts_in[h], 16)
                for h in range(2):
                    sp.wait_ge(ab_copied, 2 * it + h + 3)
                    rows = ds((2 * it + h) * P, P)
                    sp.dma_start(x1T_d[rows, :], xts[h].rearrange("p c n -> p (c n)")).then_inc(node_out[h], 16)
                    sp.dma_start(ab_d[rows, :], ab_s[h][:, 0:RH]).then_inc(node_out[h], 16)
                    sp.dma_start(b_d[rows, :], ab_s[h][:, RH:2 * RH]).then_inc(node_out[h], 16)

            for h in range(2):
                sp.wait_ge(node_out[h], 48 * (ITN + 1))
            sp.dma_start(wT_sb, WT.rearrange("(c p) n -> p c n", p=P)).then_inc(tabs_in, 16)
            sp.dma_start(b_sb.rearrange("p (t n) -> p t n", n=RH),
                         b_d.rearrange("(t p) n -> p t n", p=P)).then_inc(tabs_in, 16)
            for q in range(4):
                sp.sem_inc(h_stored[q], 16)

            def store_h(it, q):
                sp.wait_ge(h_copied, 4 * it + q + 3)
                sp.dma_start(h_d[ds(it * P, P), 512 * q:512 * q + 512], h_out[:, q, :]).then_inc(h_stored[q], 16)

            def destination_rows(it, with_h):
                if with_h:
                    sp.wait_ge(h_made, 4 * it + 4)
                    sp.dma_start(x1s.rearrange("p c n -> p (c n)"), x1T_d[ds(it * P, P), :]).then_inc(x1s_in, 16)
                for q in range(4):
                    sp.wait_ge(st_built, 4 * it + q + 1)
                    sp.dma_start(row16[q % 2][:, :, :],
                                 step_rows_d[ds(16 * it + 4 * q, 4), 1, :].partition_broadcast(P)).then_inc(drow_in[q % 2], 16)
                    if with_h and q:
                        store_h(it, q - 1)
                if with_h:
                    store_h(it, 3)

            with sp.Fori(0, NT) as it:
                destination_rows(it, True)
            with sp.Fori(NT, ITS) as it:
                destination_rows(it, False)

            sp.wait_ge(ends_made, 1)
            sp.dma_start(d_prev[H:P, :], d_row[0:P - H, 0:1]).then_inc(borders_in, 16)
            sp.dma_start(d_next[0:P - H, :], d_first[H:P, :]).then_inc(borders_in, 16)
            sp.wait_ge(ends_made, 3)
            sp.dma_start(ends_d, ends).then_inc(ends_io, 16)
            sp.wait_ge(ends_io, 16)
            sp.dma_start(crow[0:H, :, :], ends_d.rearrange("(c h) f -> h c f", h=H)).then_inc(ends_io, 16)
            sp.wait_ge(ends_made, 4)
            for a in range(2):
                sp.dma_start(carry_d.rearrange("(c h) f -> h f c", h=H)[:, a, :],
                             cres[0:H, a, a:a + CHUNKS], allow_slow_non_contiguous=True).then_inc(carry_io, 16)
            sp.wait_ge(carry_io, 32)
            sp.dma_start(carry, carry_d).then_inc(carry_io, 16)

            with sp.Fori(0, (NT - 2) // 2) as it:
                for h in range(2):
                    sp.wait_ge(fin_made, 2 * it + h + 3)
                    sp.dma_start(out[ds((2 * it + h) * P, P), :], fin[h]).then_inc(stored[h], 16)
            sp.wait_ge(fin_made, NT - 2 + 3)
            sp.dma_start(out[(NT - 2) * P:N, :], fin[0][0:N - (NT - 2) * P, :]).then_inc(stored[0], 16)
            sp.wait_ge(stored[0], 16 * ((NT - 2) // 2 + 2))
            sp.wait_ge(stored[1], 16 * ((NT - 2) // 2 + 1))

        @block.gpsimd
        def _(g):
            g.iota(it_i, [[1, P]], base=0, channel_multiplier=0).then_inc(iotas, 1)
            g.iota(pt_i, [[0, 1]], base=0, channel_multiplier=1).then_inc(iotas, 1)
            g.wait_ge(setup, SU["tiles"])
            g.wait_ge(rows_stored, 16)
            for b in range(BLK):
                g.indirect_dma_start(step_f[:, b, :], None, edge_rows_d,
                                     bass.IndirectOffsetOnAxis(ap=i_i[:, b:b + 1], axis=0),
                                     bounds_check=KP - 1, oob_is_err=True).then_inc(step_rows, 16)
            node_bound = g.snap(g.to_reg(NP_ - 1))
            row_bound = g.snap(g.to_reg(NP_ * R - 1))

            def scatter(it):
                for q in range(4):
                    h = q % 2
                    g.wait_ge(sums_copied, 4 * it + q + 3)
                    g.wait_ge(slots_ready, 4 * it + q + 1)
                    for u in range(4):
                        if not isinstance(it, int) or q:
                            g.wait_ge(scattered[1 - h][u], 16 * (2 * it + (q + 1) // 2))
                        g.sem_inc(pool_turns, 1)
                        g.indirect_dma_start(sums_d[u],
                                             bass.IndirectOffsetOnAxis(ap=idx_slot[:, 4 * q + u:4 * q + u + 1], axis=0),
                                             sums[h][:, u, :], None, bounds_check=node_bound, oob_is_err=True,
                                             compute_op=ALU.add).then_inc(scattered[h][u], 16)

            g.wait_ge(zeroed, 16 * NACC)
            scatter(0)
            with g.Fori(1, ITS) as it:
                scatter(it)

            with g.Fori(0, ITN) as it:
                for h in range(2):
                    g.wait_ge(parts_in[h], 16 * NACC * (it + 1))
                    g.tensor_tensor(parts[h][:, 0:2, :], parts[h][:, 0:2, :], parts[h][:, 2:4, :],
                                    ALU.add).then_inc(pooled, 1)
                for h in range(2):
                    g.wait_ge(veps_made, 2 * it + h + 1)
                    g.tensor_tensor(rstd[h][:, :], veps[h][:, :], minus_half[:, :], ALU.pow).then_inc(rstd_made, 1)

            for h in range(2):
                g.wait_ge(node_out[h], 48 * (ITN + 1))
            a_rows = ab_d.rearrange("n (r h) -> (n r) h", h=H)
            with g.Fori(0, ITS) as it:
                for q in range(4):
                    g.wait_ge(idx_ready, 4 * it + q + 1)
                    g.sem_inc(pool_turns, 1)
                    for u in range(4):
                        k = 4 * q + u
                        g.indirect_dma_start(a_slot[:, k, :], None, a_rows,
                                             bass.IndirectOffsetOnAxis(ap=idx_slot[:, k:k + 1], axis=0),
                                             bounds_check=row_bound, oob_is_err=True).then_inc(gath[k], 16)

            for q in range(4):
                g.wait_ge(h_stored[q], 16 * (NT + 1))
            h_rows = h_d.rearrange("n (r w) -> (n r) w", w=D)
            with g.Fori(0, ITS) as it:
                for q in range(4):
                    g.wait_ge(idx_ready, NQ + 4 * it + q + 1)
                    g.sem_inc(pool_turns, 1)
                    for u in range(4):
                        k = 4 * q + u
                        g.indirect_dma_start(h_slot[:, k, :], None, h_rows,
                                             bass.IndirectOffsetOnAxis(ap=idx_slot[:, k:k + 1], axis=0),
                                             bounds_check=row_bound, oob_is_err=True).then_inc(gath[k], 16)

            with g.Fori(0, ITN) as it:
                for h in range(2):
                    g.wait_ge(fveps_made, 2 * it + h + 1)
                    g.tensor_tensor(rstd[h][:, :], veps[h][:, :], minus_half[:, :], ALU.pow).then_inc(frstd_made, 1)

        @block.scalar
        def _(a):
            a.wait_ge(xT_in, 16)
            a.wait_ge(pads_set, 6)
            a.wait_ge(wab_ps, 1)
            a.sem_inc(y_done, 2)
            with a.Fori(0, ITN) as it:
                for h in range(2):
                    a.wait_ge(y_ps, 2 * it + h + 1)
                    a.copy(xs0[h], xT_sb[:, :, ds((2 * it + h) * P, P)]).then_inc(y_x, 1)
                for h in range(2):
                    a.wait_ge(y_ps, 2 * it + h + 3)
                    a.copy(y_sb[:, ds((2 * it + h) * D, D)], ps[:, h, 0:D]).then_inc(y_done, 1)
            for b in range(BLK):
                a.wait_ge(tables_ps, b + 1)
                bank = ps[:, 2 * (b % 2):2 * (b % 2) + 2, :].rearrange("p a n -> p (a n)")
                cols = slice(b * P, b * P + P)
                for n, t in ((0, dst_t), (2, type_t), (3, idx_t)):
                    a.copy(t[:, cols], bank[:, n * P:n * P + P])
                a.copy(src_t[:, cols], bank[:, P:2 * P]).then_inc(tables_out, 1)

            a.sem_inc(counts_copied, 2)
            a.sem_inc(sums_copied, 2)

            def copy_sums(it, q):
                h = q % 2
                a.wait_ge(sums_made, 4 * it + q + 3)
                rows_left(a, h, 2 * it + q // 2)
                a.copy(sums[h][:, :, :],
                       ps[:, 2 + 2 * h:4 + 2 * h, :].rearrange("p b (u n) -> p (b u) n", u=2)).then_inc(sums_copied, 1)

            def evacuate(it):
                for q in range(4):
                    a.wait_ge(counts_made, 4 * it + q + 3)
                    a.wait_ge(sums_made, 4 * it + q + 1)
                    a.copy(counts[q % 2], ps[:, q % 2, :].rearrange("p (u e) -> p u e", u=4)).then_inc(counts_copied, 1)
                    if q:
                        copy_sums(it, q - 1)
                copy_sums(it, 3)

            a.wait_ge(zeroed, 16 * NACC)
            evacuate(0)
            with a.Fori(1, ITS) as it:
                evacuate(it)

            for h in range(2):
                rows_left(a, h, 2 * ITS)
            a.sem_inc(ab_copied, 2)
            a.sem_inc(x1_kept, 2)
            for h in range(2):
                a.sem_inc(node_out[h], 48)
            with a.Fori(0, ITN) as it:
                for h in range(2):
                    a.wait_ge(x0_ps, 2 * it + h + 1)
                    a.copy(xs[h], xT_sb[:, :, ds((2 * it + h) * P, P)]).then_inc(x0_x, 1)
                for h in range(2):
                    a.wait_ge(xn_made, 2 * it + h + 1)
                    a.copy(nodes[:, ds((2 * it + h) * D, D)], xn[h]).then_inc(x1_kept, 1)
                for h in range(2):
                    a.wait_ge(xt_ps, 2 * it + h + 3)
                    a.wait_ge(ab_ps, 2 * it + h + 1)
                    a.wait_ge(node_out[h], 48 * (it + 1))
                    a.copy(xts[h], ps[:, 2 + h, 0:DC * P].rearrange("p (c n) -> p c n", c=DC)).then_inc(xts_made, 1)
                for h in range(2):
                    a.wait_ge(ab_ps, 2 * it + h + 3)
                    a.copy(ab_s[h], ps[:, 4 + h, 0:2 * RH]).then_inc(ab_copied, 1)

            for h in range(2):
                a.wait_ge(node_out[h], 48 * (ITN + 1))
            a.wait_ge(tabs_in, 32)
            a.sem_inc(h_copied, 2)
            a.copy(dblock, dst_t[:, 0:CHUNKS].unsqueeze(2).to_broadcast([P, CHUNKS, H])).then_inc(dblock_made, 1)
            a.wait_ge(first_turned, 1)

            def tables_of_iteration(it, with_h):
                for q in range(4):
                    a.wait_ge(scored, 4 * it + q + 1)
                    a.copy(idx_slot[:, 4 * q:4 * q + 4], idx_t[:, ds(16 * it + 4 * q, 4)]).then_inc(idx_ready, 1)
                    if q == 0:
                        a.copy(dblock, dst_t[:, ds(16 * it, CHUNKS)].unsqueeze(2)
                               .to_broadcast([P, CHUNKS, H])).then_inc(dblock_made, 1)
                    if with_h:
                        a.wait_ge(h_made, 4 * it + q + 5)
                        a.wait_ge(h_stored[q], 16 * (it + 1))
                        a.copy(h_out[:, q, :], ps[:, 2 + q % 2, :]).then_inc(h_copied, 1)
                a.wait_ge(turned, it + 1)
                a.wait_ge(blocks_done, it + 1)
                a.copy(s_row, ps[:, 4, 0:P])
                a.copy(d_row[:, 1:P + 1], ps[:, 4, P:2 * P])
                a.copy(s_T[:, ds(it * P, P)], ps[:, 4, 0:P]).then_inc(block_out, 1)

            with a.Fori(0, NT) as it:
                tables_of_iteration(it, True)
            with a.Fori(NT, ITS) as it:
                tables_of_iteration(it, False)

            for q in range(4):
                a.wait_ge(h_stored[q], 16 * (NT + 1))
            a.wait_ge(shifted, 3)

            def exponentials(it):
                a.activation(e_row, s_T[:, ds(it * P, P)], ACT.Exp).then_inc(exps, 1)

            def weights(it):
                a.wait_ge(w_turned, it + 1)
                a.copy(w_col.rearrange("p k h -> p (k h)"), ps[:, 4, 0:P]).then_inc(w_ready, 1)

            def indices(it, q):
                a.copy(idx_slot[:, 4 * q:4 * q + 4], idx_t[:, ds(16 * it + 4 * q, 4)]).then_inc(idx_ready, 1)

            def weights_and_indices(it, more):
                for q in range(4):
                    a.wait_ge(segs, 16 * it + 4 * q + 4)
                    if q == 0:
                        a.wait_ge(w_ready, it + 1)
                    a.copy(msg[:, 4 * (q % 2):4 * (q % 2) + 4, D:AW], w_col[:, 4 * q:4 * q + 4, :]).then_inc(w_placed, 1)
                    if more and q == 0:
                        exponentials(it + 1)
                    if more:
                        a.wait_ge(msgs, 4 * it + q + 1)
                        indices(it + 1, q)
                if more:
                    a.wait_ge(w_placed, 4 * it + 4)
                    weights(it + 1)

            for q in range(4):
                indices(0, q)
            exponentials(0)
            weights(0)
            with a.Fori(0, ITS - 1) as it:
                weights_and_indices(it, True)
            weights_and_indices(ITS - 1, False)

        @block.tensor
        def _(t):
            t.wait_ge(setup, SU["firsts"])
            for b in range(BLK):
                mm = t.matmul(ps[:, 4 + b // 4, (b % 4) * P:(b % 4) * P + P], lhsT=cf[:, b:b + 1].to_broadcast([P, P]),
                              rhs=ident[:, :], start=True, stop=True)
            mm.then_inc(firsts_made, 1)
            t.wait_ge(setup, SU["blk"])
            t.wait_ge(weights_in, 80)
            for fc in range(DC):
                for r in range(R):
                    for c in range(DC):
                        mm = t.matmul(ps[:, 6, fc * 2 * RH + r * 2 * H:fc * 2 * RH + (r + 1) * 2 * H],
                                      lhsT=w_nat[:, r, c, fc * P:(fc + 1) * P], rhs=blk[:, c, :],
                                      start=(c == 0), stop=(c == DC - 1))
            mm.then_inc(wab_ps, 1)
            t.sem_inc(y_ps, 2)
            with t.Fori(0, ITN) as it:
                for h in range(2):
                    t.wait_ge(y_x, 2 * it + h + 1)
                    t.wait_ge(y_done, 2 * it + h + 1)
                    for c in range(DC):
                        mm = t.matmul(ps[:, h, 0:D], lhsT=xs0[h][:, c, :], rhs=w1_sb[:, c, :],
                                      start=(c == 0), stop=(c == DC - 1))
                    mm.then_inc(y_ps, 1)
            t.wait_ge(y_done, NT + 2)
            t.wait_ge(setup, SU["local"])
            for b in range(BLK):
                if b >= 2:
                    t.wait_ge(tables_out, b - 1)
                    t.wait_ge(local_out, b - 1)
                for n in range(5):
                    s = step_f[:, b, n * P:(n + 1) * P] if n < 4 else step_local[:, b, :]
                    mm = t.transpose(ps[:, 2 * (b % 2) + n // 4, (n % 4) * P:(n % 4) * P + P], s, ident[:, :])
                mm.then_inc(tables_ps, 1)
            t.wait_ge(tables_out, BLK)
            t.wait_ge(local_out, BLK)

            t.wait_ge(steps_stored, 48)
            t.sem_inc(counts_made, 2)
            t.sem_inc(sums_made, 2)

            def sum_rows(it, q, tile):
                h = q % 2
                t.wait_ge(counts_copied, 4 * it + q + 3)
                t.wait_ge(sums_copied, 4 * it + q + 1)
                for u in range(4):
                    mm = t.matmul(ps[:, 2 + 2 * h + u // 2, (u % 2) * D:(u % 2) * D + D], lhsT=counts[h][:, u, :],
                                  rhs=y_sb[:, ds(tile[4 * q + u] * D, D)], start=True, stop=True)
                mm.then_inc(sums_made, 1)

            with t.Fori(0, ITS) as it:
                tile = read_tiles(t, 16 * it, 16)
                for q in range(4):
                    h = q % 2
                    t.wait_ge(onehots, 4 * it + q + 1)
                    t.wait_ge(counts_copied, 4 * it + q + 1)
                    for u in range(4):
                        mm = t.matmul(ps[:, h, u * P:(u + 1) * P], lhsT=onehot[h][:, u, :], rhs=eq[h][:, u, :],
                                      start=True, stop=True)
                    mm.then_inc(counts_made, 1)
                    if q:
                        sum_rows(it, q - 1, tile)
                sum_rows(it, 3, tile)

            t.wait_ge(sums_copied, NQ + 2)
            t.sem_inc(x0_ps, 2)
            t.sem_inc(xt_ps, 2)
            t.sem_inc(ab_ps, 2)
            with t.Fori(0, ITN) as it:
                for h in range(2):
                    t.wait_ge(x0_x, 2 * it + h + 1)
                    t.wait_ge(x0_used, 2 * it + h + 1)
                    for c in range(DC):
                        mm = t.matmul(ps[:, h, 0:D], lhsT=xs[h][:, c, :], rhs=w0_sb[:, c, :],
                                      start=(c == 0), stop=(c == DC - 1))
                    mm.then_inc(x0_ps, 1)
                for h in range(2):
                    t.wait_ge(xn_made, 2 * it + h + 1)
                    for c in range(DC):
                        mm = t.transpose(ps[:, 2 + h, c * P:(c + 1) * P], xn[h][:, c * P:(c + 1) * P], ident[:, :])
                    mm.then_inc(xt_ps, 1)
                for h in range(2):
                    t.wait_ge(xts_made, 2 * it + h + 1)
                    t.wait_ge(ab_copied, 2 * it + h + 1)
                    for c in range(DC):
                        mm = t.matmul(ps[:, 4 + h, 0:2 * RH], lhsT=xts[h][:, c, :], rhs=wab[:, c, :],
                                      start=(c == 0), stop=(c == DC - 1))
                    mm.then_inc(ab_ps, 1)

            def tables_of_iteration(it, with_h):
                tile = read_tiles(t, 16 * it, 16)
                for q in range(4):
                    if with_h:
                        if q == 0:
                            t.wait_ge(x1s_in, 16 * (it + 1))
                        t.wait_ge(h_copied, 4 * it + q + 1)
                        for c in range(DC):
                            mm = t.matmul(ps[:, 2 + q % 2, :], lhsT=x1s[:, c, :], rhs=wT_sb[:, c, 512 * q:512 * q + 512],
                                          start=(c == 0), stop=(c == DC - 1))
                        mm.then_inc(h_made, 1)
                    t.wait_ge(st_built, 4 * it + q + 3)
                    t.wait_ge(scored, 4 * it + q + 3)
                    for u in range(4):
                        mm = t.matmul(ps[:, q % 2, u * RH:(u + 1) * RH], lhsT=st[q % 2][:, u, :],
                                      rhs=b_sb[:, ds(tile[4 * q + u] * RH, RH)], start=True, stop=True)
                    mm.then_inc(b_made, 1)
                t.wait_ge(scored, 4 * it + 8)
                t.wait_ge(dblock_made, it + 2)
                t.wait_ge(blocks_done, it + 1)
                t.transpose(ps[:, 4, 0:P], zblock.rearrange("p k h -> p (k h)"), ident[:, :])
                t.transpose(ps[:, 4, P:2 * P], dblock.rearrange("p c h -> p (c h)"), ident[:, :]).then_inc(turned, 1)

            t.wait_ge(tabs_in, 32)
            t.wait_ge(ab_copied, NT + 2)
            t.wait_ge(dblock_made, 1)
            t.transpose(ps[:, 5, 0:P], dblock.rearrange("p c h -> p (c h)"), ident[:, :]).then_inc(first_turned, 1)
            t.wait_ge(first_out, 1)
            t.sem_inc(b_made, 2)
            t.sem_inc(h_made, 4)
            with t.Fori(0, NT) as it:
                tables_of_iteration(it, True)
            with t.Fori(NT, ITS) as it:
                tables_of_iteration(it, False)

            t.sem_inc(segs, 8)

            def turn_weights(it):
                t.wait_ge(exps, it + 1)
                if not isinstance(it, int):
                    t.wait_ge(w_ready, it)
                t.transpose(ps[:, 4, 0:P], e_row, ident[:, :]).then_inc(w_turned, 1)

            def sum_edges(it, more):
                for q in range(4):
                    t.wait_ge(w_placed, 4 * it + q + 1)
                    t.wait_ge(msgs, 4 * it + q + 1)
                    for u in range(4):
                        k = 4 * (q % 2) + u
                        t.wait_ge(added, 16 * it + 4 * q + u + 1)
                        t.matmul(ps[:, u, 0:AW], lhsT=sel[:, k, :], rhs=msg[:, k, :],
                                 start=True, stop=True).then_inc(segs, 1)
                    if more and q == 1:
                        turn_weights(it + 1)

            turn_weights(0)
            with t.Fori(0, ITS - 1) as it:
                sum_edges(it, True)
            sum_edges(ITS - 1, False)


def kernel(x, src, dst, edge_type_8, L0_gnn_w0, L0_gnn_w1, L1_gnn_W, L1_gnn_attn_src, L1_gnn_attn_dst):
    import numpy as np
    import concourse.bacc as bacc
    from concourse.bass_utils import run_bass_kernel_spmd

    x, W = np.asarray(x), np.asarray(L1_gnn_W)
    n, d = x.shape
    r = W.shape[0]
    arrays = {
        "x": x, "xT": np.ascontiguousarray(x.T),
        "src": np.asarray(src), "dst": np.asarray(dst), "etype": np.asarray(edge_type_8),
        "w0": np.asarray(L0_gnn_w0), "w1": np.asarray(L0_gnn_w1),
        "W": W, "WT": np.ascontiguousarray(W.transpose(2, 0, 1).reshape(d, r * d)),
        "attn_src": np.asarray(L1_gnn_attn_src), "attn_dst": np.asarray(L1_gnn_attn_dst),
    }
    nc = bacc.Bacc("TRN2", target_bir_lowering=False, num_devices=1)
    aps = {k: nc.dram_tensor(k + "_in", a.shape, mybir.dt.from_np(a.dtype), kind="ExternalInput").ap()
           for k, a in arrays.items()}
    out = nc.dram_tensor("out", (n, d), F32, kind="ExternalOutput").ap()
    graph_layers(nc, out=out, **aps)
    r = run_bass_kernel_spmd(nc, [{k + "_in": a for k, a in arrays.items()}], core_ids=[0])
    return r.results[0]["out"]
```

```python
from contextlib import ExitStack

import concourse.bass as bass
from concourse import mybir

P = 128
F32 = mybir.dt.float32
BF16 = mybir.dt.bfloat16
I32 = mybir.dt.int32
I16 = mybir.dt.int16
ALU = mybir.AluOpType
ACT = mybir.ActivationFunctionType
X = mybir.AxisListType.X

BIG = 1.0e30
NO_NODE = 8191.0
LN_EPS = 1e-5
DEN_EPS = 1e-12
SLOPE = 0.2


def graph_layers(nc, x, xT, src, dst, etype, w0, w1, W, WT, attn_src, attn_dst, out):
    N, D = x.shape
    E = src.shape[0]
    R = W.shape[0]
    H, HD = attn_src.shape
    DC = D // P
    NT = -(-N // P) + 1
    NP_ = NT * P
    ET = -(-E // P)
    TAIL = E - (ET - 1) * P
    CHUNKS = 16
    LEN = -(-(ET + NT - 2) // CHUNKS)
    STEPS = CHUNKS * LEN
    BLK = -(-STEPS // P)
    KP = BLK * P
    FULL = (ET - 1) // P
    REST = (ET - 1) - FULL * P
    RH = R * H
    SCAN = LEN * P
    NACC = 4
    assert P == CHUNKS * H and  D == H * HD

    def dram(name, shape, dt):
        return nc.dram_tensor(name, shape, dt, kind="Internal").ap()

    edge_rows_d = dram("edge_rows_d", [KP, 4 * P], F32)
    step_rows_d = dram("step_rows_d", [KP, 2, P], I16)
    step_tile_d = dram("step_tile_d", [KP], I32)
    sums_d = [dram(f"sums_d{u}", [NP_, D], F32) for u in range(NACC)]
    a_d = dram("a_d", [NP_, RH], F32)
    h_d = dram("h_d", [NP_, R * D], F32)
    x1T_d = dram("x1T_d", [NP_, DC * P], F32)
    ends_d = dram("ends_d", [P, 4], F32)
    carry_d = dram("carry_d", [P, 2], F32)

    with ExitStack() as ctx:
        def sb(name, shape, dt):
            return ctx.enter_context(nc.sbuf_tensor(name, shape, dt))

        def sem(name):
            return ctx.enter_context(nc.semaphore(name))

        nodes = sb("nodes", [P, NT * D], F32)
        region = sb("region", [P, 2 * DC * NP_], F32)
        ZW = STEPS * H
        edge_z = sb("edge_z", [P, ZW], F32)
        dst_t = sb("dst_t", [P, KP], F32)
        type_t = sb("type_t", [P, KP], F32)
        local_t = sb("local_t", [P, KP], F32)
        idx_t = sb("idx_t", [P, KP], I32)
        mask_t = sb("mask_t", [P, KP], F32)
        ident = sb("ident", [P, P], F32)
        iota_row = sb("iota_row", [P, P], F32)
        before = sb("before", [P, P], BF16)
        part = sb("part", [P, 1], F32)
        minus_half = sb("minus_half", [P, 1], F32)
        iota8 = sb("iota8", [P, R], F32)
        idx_slot = sb("idx_slot", [P, 16], I32)
        ps = ctx.enter_context(nc.psum_tensor("ps", [P, 8, 512], F32))
        HALF = DC * NP_
        assert D * NT <= HALF

        def view(base, at, *shape):
            n = 1
            for s in shape:
                n *= s
            v = base[:, at:at + n]
            names = "abcd"[:len(shape)]
            if len(shape) > 1:
                v = v.rearrange(f"p ({' '.join(names)}) -> p {' '.join(names)}",
                                **{k: s for k, s in zip(names, shape)})
            return v

        o = 0
        rows_i = view(nodes, o, 3, BLK, P).bitcast(I32); o += 3 * BLK * P
        rows_f = view(nodes, o, BLK, 4 * P); o += BLK * 4 * P
        step_f = view(nodes, o, BLK, 4 * P); o += BLK * 4 * P
        firsts = view(nodes, o, KP); o += KP
        cmp = view(nodes, o, KP); o += KP
        step_local = view(nodes, o, BLK, P); o += BLK * P
        assert o <= NT * D
        w_nat = view(region, HALF, R, DC, D)
        o = 2 * KP + 2 * DC * D
        step16 = view(edge_z, o, BLK * P).bitcast(I16).rearrange("p (b a e) -> p b a e", b=BLK, a=2); o += BLK * P
        misc = view(edge_z, o, 512); o += 512
        xs0 = [view(edge_z, o + DC * P * h, DC, P) for h in range(2)]; o += 2 * DC * P
        assert o <= ZW
        NZ = 800
        ki = misc[:, 0:8].bitcast(I32)
        kt = misc[:, 8:16].bitcast(I32)
        kf = misc[:, 16:24]
        kh = misc[:, 24:32]
        jfi = misc[:, 32:40].bitcast(I32)
        cf = misc[:, 40:48]
        i_f = misc[:, 48:56]
        j_f = misc[:, 56:64]
        j128 = misc[:, 64:72]
        i_i = misc[:, 72:80].bitcast(I32)
        j_i = misc[:, 80:88].bitcast(I32)
        acol = misc[:, 96:96 + 2 * DC].rearrange("p (a c) -> p a c", a=2)
        hsel = misc[:, 104:108]
        q32 = misc[:, 108:109]
        tmp4 = misc[:, 112:116]
        it_i = misc[:, 128:256].bitcast(I32)
        pt_i = misc[:, 256:257].bitcast(I32)
        blk = misc[:, 264:264 + DC * 2 * H].rearrange("p (c n) -> p c n", c=DC)
        tile_row = sb("tile_row", [1, KP], I32)
        wab = sb("wab", [P, DC, 2 * RH], F32)

        xT_sb = view(region, 0, DC, NP_)
        y_sb = view(region, HALF, NT * D)
        o = 0
        src_t = view(edge_z, o, KP); o += KP
        trash_t = view(edge_z, o, KP); o += KP
        w0_sb = view(edge_z, o, DC, D); o += DC * D
        w1_sb = view(edge_z, o, DC, D); o += DC * D
        eq = [view(edge_z, o + 256 * h, 256).bitcast(BF16).rearrange("p (u e) -> p u e", u=4) for h in range(2)]; o += 512
        onehot = [view(edge_z, o + 256 * h, 256).bitcast(BF16).rearrange("p (u e) -> p u e", u=4) for h in range(2)]; o += 512
        counts = [view(edge_z, o + 512 * h, 4, P) for h in range(2)]; o += 1024
        xs = [view(edge_z, o + DC * P * h, DC, P) for h in range(2)]; o += 2 * DC * P
        sums = [sb("sums0", [P, 4, D], F32)]
        zeros = sums[0][:, :, :].rearrange("p u n -> p (u n)")[:, 0:NZ]
        sums.append(view(edge_z, o, 4, D)); o += 4 * D
        eqj = view(edge_z, o, 2 * P).bitcast(BF16).rearrange("p (u e) -> p u e", u=4); o += 2 * P
        assert o <= ZW
        row16 = [sb(f"row16_{h}", [P, 4, P], I16) for h in range(2)]
        dup = sb("dup", [P, 8], F32)
        dup2 = sb("dup2", [P, 8], F32)

        o = 2 * KP + 2 * DC * D
        parts = [view(edge_z, o + NACC * D * h, NACC, D) for h in range(1)]; o += NACC * D
        parts.append(sums[0])
        o2 = 2 * KP + 2 * DC * D + 512 + 512 + 1024 + 2 * DC * P
        o = o2
        xn = [view(edge_z, o + D * h, D) for h in range(2)]; o += 2 * D
        xts = [view(edge_z, 0 + DC * P * h, DC, P) for h in range(2)]
        a_out = [view(edge_z, 2 * DC * P + RH * h, RH) for h in range(2)]
        assert o <= ZW
        tmp = [view(edge_z, KP + D * h, D) for h in range(2)]
        stats = [sb(f"stats{h}", [P, 6], F32) for h in range(2)]
        veps = [sb(f"veps{h}", [P, 1], F32) for h in range(2)]
        agg2 = [sb(f"agg2_{h}", [P, 2], F32) for h in range(2)]
        rstd = [sb(f"rstd{h}", [P, 1], F32) for h in range(2)]

        o = 0
        wT_sb = view(region, o, DC, R * D); o += DC * R * D
        h_out = view(region, o, 4, 512); o += 2048
        st = [view(region, o + 4 * P * h, 4, P) for h in range(2)]; o += 8 * P
        prod = view(region, o, 4, H, R); o += 4 * RH
        tmask = view(region, o, 4, R); o += 4 * R
        bsel = view(region, o, 4, H); o += 4 * H
        zt = view(region, o, 4, H); o += 4 * H
        zl = view(region, o, 4, H); o += 4 * H
        a_slot = view(region, o, 16, H); o += 16 * H
        x1s = [view(region, o + DC * P * h, DC, P) for h in range(2)]; o += 2 * DC * P
        zblock = [view(region, o + P * h, 16, H) for h in range(2)]; o += 2 * P
        dblock = view(region, o, CHUNKS, H); o += P
        assert o <= HALF
        o = HALF
        keep = view(region, o, SCAN + 1); o += SCAN + 1
        d_row = view(region, o, P + 1); o += P + 1
        s_row = view(region, o, P); o += P
        run = view(region, o, P); o += P
        lead = view(region, o, P); o += P
        led = view(region, o, P); o += P
        lmax = view(region, o, 2); o += 2
        d_first = view(region, o, 1); o += 1
        d_prev = view(region, o, 1); o += 1
        d_next = view(region, o, 1); o += 1
        k_first = view(region, o, 2); o += 2
        ends = view(region, o, 4); o += 4
        carry = view(region, o, 2); o += 2
        crow = view(region, o, CHUNKS, 4); o += 4 * CHUNKS
        cres = view(region, o, 2, CHUNKS + 1); o += 2 * (CHUNKS + 1)
        b_sb = view(region, o, NT * RH); o += NT * RH
        assert o <= 2 * HALF
        fwd = view(region, 0, SCAN)
        s_T = view(edge_z, 0, SCAN)

        AW = D + H
        o = 0
        acc = view(region, o, NT * AW); o += NT * AW
        h_slot = view(region, o, 16, D); o += 16 * D
        msg = view(region, o, 8, AW); o += 8 * AW
        sel = view(region, o, 8, P); o += 8 * P
        e_row = view(region, o, P); o += P
        w_col = view(region, o, 16, H); o += P
        den = [view(region, o + 2 * H * h, 2, H) for h in range(2)]; o += 4 * H
        res = [view(region, o + D * h, D) for h in range(2)]; o += 2 * D
        fin = [view(region, o + D * h, D) for h in range(2)]; o += 2 * D
        assert o <= 2 * HALF

        names = """pads_set edges_in weights_in iotas setup rows_stored firsts_made step_rows steps_stored
            tables_ps tables_out local_out wab_ps x_in xT_in nodes_padded y_x y_ps y_done zeroed
            onehots eq_used dup_scaled slots_ready counts_made counts_copied sums_made sums_copied
            halves_made pooled parts_used x0_x x0_ps x0_used relu_made stats_made stats_seen aggr_made veps_made rstd_made
            xn_made x1_kept xt_ps xts_made ab_ps ab_copied
            tabs_in idx_ready h_made h_copied st_built mask_made b_made prod_made bsel_made z_made
            z_sloped scored dblock_made turned block_out keep_made run_made lead_made led_made lmax_made
            blocks_done first_turned first_out ends_made borders_in ends_io carry_io shifted
            exps w_turned w_ready w_placed acc_zero pool_turns msgs segs added
            den_made rden_made res_made sum_made fstats_made fstats_seen faggr_made fveps_made frstd_made
            fin_made""".split()
        (pads_set, edges_in, weights_in, iotas, setup, rows_stored, firsts_made, step_rows, steps_stored,
         tables_ps, tables_out, local_out, wab_ps, x_in, xT_in, nodes_padded, y_x, y_ps, y_done, zeroed,
         onehots, eq_used, dup_scaled, slots_ready, counts_made, counts_copied, sums_made, sums_copied,
         halves_made, pooled, parts_used, x0_x, x0_ps, x0_used, relu_made, stats_made, stats_seen, aggr_made, veps_made, rstd_made,
         xn_made, x1_kept, xt_ps, xts_made, ab_ps, ab_copied,
         tabs_in, idx_ready, h_made, h_copied, st_built, mask_made, b_made, prod_made, bsel_made, z_made,
         z_sloped, scored, dblock_made, turned, block_out, keep_made, run_made, lead_made, led_made, lmax_made,
         blocks_done, first_turned, first_out, ends_made, borders_in, ends_io, carry_io, shifted,
         exps, w_turned, w_ready, w_placed, acc_zero, pool_turns, msgs, segs, added,
         den_made, rden_made, res_made, sum_made, fstats_made, fstats_seen, faggr_made, fveps_made, frstd_made,
         fin_made) = [sem(n) for n in names]
        row_in = [sem(f"row_in{h}") for h in range(2)]
        x1s_in = [sem(f"x1s_in{h}") for h in range(2)]
        drow_in = [sem(f"drow_in{h}") for h in range(2)]
        parts_in = [sem(f"parts_in{h}") for h in range(2)]
        node_out = [sem(f"node_out{h}") for h in range(2)]
        stored = [sem(f"stored{h}") for h in range(2)]
        h_stored = [sem(f"h_stored{q}") for q in range(4)]
        scattered = [[sem(f"scattered{h}{u}") for u in range(4)] for h in range(2)]
        gath = [sem(f"gath{k}") for k in range(16)]

        block = ctx.enter_context(nc.Block())
        ds = bass.ds
        NQ = STEPS // 4
        ITN = NT // 2
        ITS = LEN
        assert NT % 2 == 0 and NT < ITS
        SU = {}

        def rows_left(eng, h, times):
            if isinstance(times, int) and times <= 0:
                return
            for u in range(4):
                eng.wait_ge(scattered[h][u], 16 * times)

        def read_tiles(eng, at, n):
            regs = [eng.alloc_register(f"tile{k}_{nc.next_id()}") for k in range(n)]
            eng.load(regs, tile_row[0:1, ds(at, n)])
            return [eng.snap(r, min_val=0, max_val=NT - 1) for r in regs]

        def in_pairs(eng, first, end, body):
            with eng.Fori(0, (end - first) // 2) as i:
                for n in range(first, first + 2):
                    body(2 * i + n, n % 2, i + n // 2)
            if (end - first) % 2:
                body(end - 1, (end - 1) % 2, (end - 1) // 2)

        @block.vector
        def _(v):
            n = [0]

            def do(ins):
                n[0] += 1
                ins.then_inc(setup, 1)
                v.wait_ge(setup, n[0])

            for a, pad in enumerate((int(NO_NODE), 0, 0)):
                v.memset(rows_i[:, a, FULL, :], pad).then_inc(pads_set, 1)
            v.memset(zeros, 0.0).then_inc(pads_set, 1)
            v.memset(xT_sb[:, :, N:NP_], 0.0).then_inc(pads_set, 1)
            v.memset(minus_half[:, :], -0.5).then_inc(pads_set, 1)
            v.wait_ge(iotas, 2)
            do(v.tensor_copy(iota_row[:, :], it_i))
            do(v.tensor_copy(part[:, :], pt_i))
            do(v.tensor_copy(iota8[:, :], it_i[:, 0:R]))
            do(v.tensor_scalar(ident[:, :], iota_row[:, :], part[:, 0:1], None, ALU.is_equal))
            do(v.tensor_scalar(before[:, :], iota_row[:, :], part[:, 0:1], None, ALU.is_lt))
            do(v.tensor_scalar(ki[:, 0:1], pt_i, CHUNKS - 1, None, ALU.bitwise_and))
            do(v.tensor_scalar(kt[:, 0:1], pt_i, 4, None, ALU.logical_shift_right))
            do(v.tensor_copy(kh[:, 0:1], ki[:, 0:1]))
            do(v.tensor_copy(kh[:, 1:2], kt[:, 0:1]))
            do(v.scalar_tensor_tensor(out=kh[:, 2:3], in0=kh[:, 0:1], scalar=float(LEN), in1=kh[:, 1:2],
                                      op0=ALU.mult, op1=ALU.add))
            for b in range(BLK):
                last = v.tensor_scalar(kf[:, b:b + 1], kh[:, 2:3], float(P // CHUNKS * b), None, ALU.add)
            do(last)
            v.wait_ge(edges_in, 16 * 9)
            for a in range(3):
                last = v.tensor_copy(rows_f[:, :, a * P:(a + 1) * P], rows_i[:, a, :, :])
            do(last)
            do(v.scalar_tensor_tensor(out=rows_f[:, :, 3 * P:4 * P], in0=rows_f[:, :, P:2 * P], scalar=float(R),
                                      in1=rows_f[:, :, 2 * P:3 * P], op0=ALU.mult, op1=ALU.add))
            SU["rows"] = n[0]
            do(v.tensor_scalar(jfi[:, 0:BLK], rows_i[:, 0, :, 0], 7, None, ALU.logical_shift_right))
            do(v.tensor_copy(cf[:, 0:BLK], jfi[:, 0:BLK]))
            for b in range(BLK):
                last = v.tensor_scalar(cf[:, b:b + 1], cf[:, b:b + 1], part[:, 0:1], float(P * b), ALU.add, ALU.add)
            do(last)
            SU["firsts"] = n[0]
            v.wait_ge(firsts_made, 1)
            do(v.tensor_copy(firsts, ps[:, 4:6, :].rearrange("p a n -> p (a n)")[:, 0:KP]))
            for b in range(BLK):
                do(v.tensor_scalar(cmp[:, 1:ET], firsts[:, 1:ET], kf[:, b:b + 1], None, ALU.is_le))
                do(v.tensor_reduce(i_f[:, b:b + 1], cmp[:, 1:ET], X, ALU.add))
            do(v.tensor_tensor(j_f[:, 0:BLK], kf[:, 0:BLK], i_f[:, 0:BLK], ALU.subtract))
            do(v.tensor_scalar(j128[:, 0:BLK], j_f[:, 0:BLK], float(P), None, ALU.mult))
            do(v.tensor_copy(i_i[:, 0:BLK], i_f[:, 0:BLK]))
            do(v.tensor_copy(j_i[:, 0:BLK], j_f[:, 0:BLK]))
            SU["tiles"] = n[0]
            v.wait_ge(weights_in, 80)
            do(v.memset(blk, 0.0))
            for h in range(H // DC):
                do(v.tensor_scalar(hsel[:, h:h + 1], part[:, 0:1], float(HD * h), None, ALU.is_ge))
                do(v.tensor_scalar(tmp4[:, h:h + 1], part[:, 0:1], float(HD * (h + 1)), None, ALU.is_lt))
            do(v.tensor_tensor(hsel[:, 0:4], hsel[:, 0:4], tmp4[:, 0:4], ALU.mult))
            for c in range(DC):
                for a in range(2):
                    last = v.tensor_scalar(blk[:, c, a * H + 4 * c:a * H + 4 * c + 4], hsel[:, 0:4],
                                           acol[:, a, c:c + 1], None, ALU.mult)
            do(last)
            SU["blk"] = n[0]
            v.wait_ge(step_rows, 16 * BLK)
            for b in range(BLK):
                last = v.tensor_scalar(step_local[:, b, :], step_f[:, b, 0:P], j128[:, b:b + 1], None, ALU.subtract)
            do(last)
            SU["local"] = n[0]
            do(v.tensor_copy(step16[:, :, 0, :], step_f[:, :, P:2 * P]))
            do(v.tensor_copy(step16[:, :, 1, :], step_local))
            SU["step16"] = n[0]
            for b in range(BLK):
                v.wait_ge(tables_ps, b + 1)
                v.tensor_copy(local_t[:, b * P:b * P + P], ps[:, 2 * (b % 2) + 1, 0:P]).then_inc(local_out, 1)
            v.wait_ge(tables_out, BLK)
            v.wait_ge(local_out, BLK)
            do(v.tensor_scalar(mask_t[:, :], local_t[:, :], 0.0, None, ALU.is_ge))
            do(v.scalar_tensor_tensor(out=mask_t[:, :], in0=local_t[:, :], scalar=float(P), in1=mask_t[:, :],
                                      op0=ALU.is_lt, op1=ALU.mult))
            do(v.tensor_scalar(mask_t[:, :], mask_t[:, :], BIG, -BIG, ALU.mult, ALU.add))
            do(v.tensor_scalar(part[:, :], part[:, :], float(N), None, ALU.add))
            do(v.tensor_scalar(trash_t, src_t, -1.0, part[:, 0:1], ALU.mult, ALU.add))
            do(v.tensor_scalar(part[:, :], part[:, :], float(-N), None, ALU.add))
            v.wait_ge(wab_ps, 1)
            wps = ps[:, 6, 0:DC * 2 * RH].rearrange("p (c r a h) -> p c r a h", c=DC, r=R, a=2)
            for c in range(DC):
                v.tensor_copy(wab[:, c, 0:RH].rearrange("p (r h) -> p r h", r=R), wps[:, c, :, 0, :])
                last = v.tensor_copy(wab[:, c, RH:2 * RH].rearrange("p (h r) -> p r h", r=R), wps[:, c, :, 1, :])
            do(last)
            SU["end"] = n[0]

            v.wait_ge(rows_stored, 16)
            v.memset(nodes[:, N // P * D:NT * D], 0.0).then_inc(nodes_padded, 1)

            v.wait_ge(wab_ps, 1)
            v.wait_ge(steps_stored, 32)
            v.wait_ge(y_x, NT)
            v.sem_inc(eq_used, 2)

            def match_sources(it):
                for q in range(4):
                    h, g, k = q % 2, 4 * it + q, 16 * it + 4 * q
                    v.wait_ge(counts_made, g + 1)
                    v.tensor_tensor(onehot[h], iota_row[:, :].unsqueeze(1).to_broadcast([P, 4, P]),
                                    local_t[:, ds(k, 4)].unsqueeze(2).to_broadcast([P, 4, P]), ALU.is_equal)
                    v.wait_ge(row_in[h], 16 * (2 * it + q // 2 + 1))
                    for u in range(4):
                        last = v.tensor_scalar(eq[h][:, u, :], row16[h][:, u, :], src_t[:, ds(k + u, 1)],
                                               None, ALU.is_equal)
                    last.then_inc(onehots, 1)
                    v.wait_ge(onehots, g + 1)
                    for u in range(4):
                        last = v.tensor_tensor_reduce(out=eqj[:, u, :], in0=eq[h][:, u, :], in1=before[:, :], scale=1.0,
                                                      scalar=0.0, op0=ALU.mult, op1=ALU.add,
                                                      accum_out=dup[:, 4 * h + u:4 * h + u + 1])
                    last.then_inc(eq_used, 1)
                    v.wait_ge(eq_used, g + 3)
                    v.scalar_tensor_tensor(out=dup2[:, 4 * h:4 * h + 4], in0=dup[:, 4 * h:4 * h + 4], scalar=1.0,
                                           in1=trash_t[:, ds(k, 4)], op0=ALU.min,
                                           op1=ALU.mult).then_inc(dup_scaled, 1)
                    v.wait_ge(dup_scaled, g + 1)
                    rows_left(v, h, 2 * it + q // 2 - 1)
                    v.tensor_tensor(idx_slot[:, 4 * q:4 * q + 4], dup2[:, 4 * h:4 * h + 4],
                                    src_t[:, ds(k, 4)], ALU.add).then_inc(slots_ready, 1)

            match_sources(0)
            with v.Fori(1, ITS) as it:
                match_sources(it)

            v.wait_ge(sums_copied, NQ + 2)
            v.wait_ge(x_in, 32)
            for h in range(2):
                rows_left(v, h, 2 * ITS)
            v.sem_inc(parts_used, 2)
            v.sem_inc(x0_used, 2)
            v.sem_inc(xn_made, 2)
            with v.Fori(0, ITN) as it:
                for h in range(2):
                    v.wait_ge(parts_in[h], 16 * NACC * (it + 1))
                    v.wait_ge(xn_made, 2 * it + h + 1)
                    v.tensor_tensor(tmp[h], parts[h][:, 0, :], parts[h][:, 1, :], ALU.add).then_inc(halves_made, 1)
                for h in range(2):
                    v.wait_ge(halves_made, 2 * it + h + 1)
                    v.wait_ge(pooled, 2 * it + h + 1)
                    v.tensor_tensor(tmp[h], tmp[h], parts[h][:, 2, :], ALU.add).then_inc(parts_used, 1)
                for h in range(2):
                    v.wait_ge(x0_ps, 2 * it + h + 3)
                    v.wait_ge(parts_used, 2 * it + h + 3)
                    v.tensor_tensor(tmp[h], ps[:, h, 0:D], tmp[h], ALU.add).then_inc(x0_used, 1)
                for h in range(2):
                    v.wait_ge(x0_used, 2 * it + h + 3)
                    v.scalar_tensor_tensor(out=tmp[h], in0=tmp[h], scalar=0.0, in1=nodes[:, ds((2 * it + h) * D, D)],
                                           op0=ALU.max, op1=ALU.add).then_inc(relu_made, 1)
                for h in range(2):
                    v.wait_ge(relu_made, 2 * it + h + 1)
                    v.bn_stats(stats[h][:, :], tmp[h]).then_inc(stats_made, 1)
                for h in range(2):
                    v.wait_ge(stats_made, 2 * it + h + 1)
                    v.sem_inc(stats_seen, 1)
                    v.bn_aggr(agg2[h][:, :], stats[h][:, :]).then_inc(aggr_made, 1)
                for h in range(2):
                    v.wait_ge(aggr_made, 2 * it + h + 1)
                    v.tensor_scalar(veps[h][:, :], agg2[h][:, 1:2], LN_EPS, None, ALU.add).then_inc(veps_made, 1)
                for h in range(2):
                    v.wait_ge(rstd_made, 2 * it + h + 1)
                    v.wait_ge(xt_ps, 2 * it + h + 1)
                    v.wait_ge(x1_kept, 2 * it + h + 1)
                    v.tensor_scalar(xn[h], tmp[h], agg2[h][:, 0:1], rstd[h][:, 0:1], ALU.subtract,
                                    ALU.mult).then_inc(xn_made, 1)

            v.wait_ge(tabs_in, 16)
            v.wait_ge(x1_kept, NT + 2)
            v.memset(run, 0.0)
            v.memset(lead, 1.0)
            v.memset(lmax, 0.0).then_inc(keep_made, 1)
            v.wait_ge(first_turned, 1)
            v.tensor_copy(d_first, ps[:, 5, 0:1])
            v.tensor_copy(d_row[:, 0:1], ps[:, 5, 0:1]).then_inc(first_out, 1)
            v.sem_inc(st_built, 2)
            v.sem_inc(scored, 4)
            v.sem_inc(blocks_done, 1)

            def compare(b, q):
                h = q % 2
                v.wait_ge(drow_in[h], 16 * (2 * b + q // 2 + 1))
                v.wait_ge(b_made, 4 * b + q + 1)
                for u in range(4):
                    last = v.tensor_scalar(st[h][:, u, :], row16[h][:, u, :], part[:, 0:1], None, ALU.is_equal)
                last.then_inc(st_built, 1)

            def score(b, par, q):
                g, h, k = 4 * b + q, q % 2, 16 * b + 4 * q
                v.tensor_tensor(tmask, type_t[:, ds(k, 4)].unsqueeze(2).to_broadcast([P, 4, R]),
                                iota8[:, :].unsqueeze(1).to_broadcast([P, 4, R]), ALU.is_equal).then_inc(mask_made, 1)
                v.wait_ge(mask_made, g + 1)
                v.wait_ge(b_made, g + 3)
                v.tensor_tensor(prod, ps[:, h, 0:4 * RH].rearrange("p (u h r) -> p u h r", u=4, h=H),
                                tmask.unsqueeze(2).to_broadcast([P, 4, H, R]), ALU.mult).then_inc(prod_made, 1)
                v.wait_ge(prod_made, g + 1)
                v.tensor_reduce(bsel, prod, X, ALU.add).then_inc(bsel_made, 1)
                v.wait_ge(bsel_made, g + 1)
                for u in range(4):
                    v.wait_ge(gath[4 * q + u], 16 * (b + 1))
                v.tensor_tensor(zt, a_slot[:, 4 * q:4 * q + 4, :], bsel, ALU.add).then_inc(z_made, 1)
                v.wait_ge(z_made, g + 1)
                v.scalar_tensor_tensor(out=zl, in0=zt, scalar=SLOPE, in1=zt, op0=ALU.mult,
                                       op1=ALU.max).then_inc(z_sloped, 1)
                v.wait_ge(z_sloped, g + 1)
                if q == 0:
                    v.wait_ge(turned, b + 1)
                v.tensor_tensor(zblock[par][:, 4 * q:4 * q + 4, :], zl,
                                mask_t[:, ds(k, 4)].unsqueeze(2).to_broadcast([P, 4, H]),
                                ALU.add).then_inc(scored, 1)

            def scan_block(b):
                at = ds(b * P, P)
                v.wait_ge(block_out, b + 2)
                v.tensor_tensor(keep[:, at], d_row[:, 1:P + 1], d_row[:, 0:P], ALU.is_equal).then_inc(keep_made, 1)
                v.wait_ge(keep_made, b + 2)
                v.tensor_tensor_scan(run, keep[:, at], s_row, run[:, P - 1:P], ALU.mult, ALU.max).then_inc(run_made, 1)
                v.tensor_tensor_scan(lead, keep[:, at], keep[:, at], lead[:, P - 1:P], ALU.mult,
                                     ALU.mult).then_inc(lead_made, 1)
                v.tensor_copy(d_row[:, 0:1], d_row[:, P:P + 1])
                v.wait_ge(lead_made, b + 1)
                v.tensor_tensor(led, lead, s_row, ALU.mult).then_inc(led_made, 1)
                v.wait_ge(led_made, b + 1)
                v.tensor_reduce(lmax[:, 1:2], led, X, ALU.max).then_inc(lmax_made, 1)
                v.wait_ge(lmax_made, b + 1)
                v.wait_ge(run_made, b + 1)
                v.tensor_tensor(lmax[:, 0:1], lmax[:, 0:1], lmax[:, 1:2], ALU.max).then_inc(blocks_done, 1)

            def score_block(b, par, turn):
                for q in range(4):
                    compare(b + (q + 1) // 4, (q + 1) % 4)
                    score(b, par, q)
                    if q == 1 and not (isinstance(b, int) and b == 0):
                        scan_block(b - 1)
                        v.wait_ge(blocks_done, b + 1)

            v.wait_ge(keep_made, 1)
            v.wait_ge(first_out, 1)
            compare(0, 0)
            score_block(0, 0, 0)
            in_pairs(v, 1, ITS, score_block)
            scan_block(ITS - 1)
            v.wait_ge(blocks_done, ITS + 1)

            v.memset(d_prev, -1.0)
            v.memset(d_next, -1.0).then_inc(ends_made, 1)
            v.wait_ge(borders_in, 32)
            v.tensor_tensor(k_first[:, 0:1], d_first, d_prev, ALU.is_equal)
            v.tensor_tensor(k_first[:, 1:2], d_row[:, 0:1], d_next, ALU.is_equal).then_inc(ends_made, 1)
            v.wait_ge(ends_made, 2)
            v.tensor_copy(keep[:, 0:1], k_first[:, 0:1])
            v.tensor_copy(keep[:, SCAN:SCAN + 1], k_first[:, 1:2])
            v.tensor_copy(ends[:, 0:1], run[:, P - 1:P])
            v.tensor_copy(ends[:, 2:3], lmax[:, 0:1])
            v.tensor_tensor(ends[:, 1:2], lead[:, P - 1:P], k_first[:, 0:1], ALU.mult)
            v.tensor_tensor(ends[:, 3:4], lead[:, P - 1:P], k_first[:, 1:2], ALU.mult).then_inc(ends_made, 1)
            v.memset(cres[0:H, 0, 0:1], 0.0)
            v.memset(cres[0:H, 1, CHUNKS:CHUNKS + 1], 0.0)
            v.wait_ge(ends_io, 32)
            v.tensor_tensor_scan(cres[0:H, 0, 1:CHUNKS + 1], crow[0:H, :, 1], crow[0:H, :, 0], 0.0, ALU.mult, ALU.max)
            v.tensor_tensor_scan(cres[0:H, 1, 0:CHUNKS][:, ::-1], crow[0:H, :, 3][:, ::-1], crow[0:H, :, 2][:, ::-1],
                                 0.0, ALU.mult, ALU.max).then_inc(ends_made, 1)
            v.wait_ge(carry_io, 48)
            for q in range(4):
                v.wait_ge(h_stored[q], 16 * (NT + 1))
            v.tensor_tensor_scan(fwd, keep[:, 0:SCAN], s_T, carry[:, 0:1], ALU.mult, ALU.max).then_inc(shifted, 1)
            v.wait_ge(shifted, 1)
            v.tensor_tensor_scan(fwd[:, ::-1], keep[:, 1:SCAN + 1][:, ::-1], fwd[:, ::-1], carry[:, 1:2],
                                 ALU.mult, ALU.max).then_inc(shifted, 1)
            v.wait_ge(shifted, 2)
            v.tensor_tensor(s_T, s_T, fwd, ALU.subtract).then_inc(shifted, 1)
            v.wait_ge(shifted, 3)

            v.memset(acc, 0.0).then_inc(acc_zero, 1)
            v.wait_ge(acc_zero, 1)
            def add_sums(g, tile):
                for u in range(4):
                    v.wait_ge(segs, 4 * g + u + 9)
                    v.wait_ge(added, 4 * g + u + 4)
                    v.tensor_tensor(acc[:, ds(tile[u] * AW, AW)], ps[:, u, 0:AW], acc[:, ds(tile[u] * AW, AW)],
                                    ALU.add).then_inc(added, 1)

            def weigh(it, q):
                h = q % 2
                v.tensor_tensor(sel[:, 4 * h:4 * h + 4, :], iota_row[:, :].unsqueeze(1).to_broadcast([P, 4, P]),
                                local_t[:, ds(16 * it + 4 * q, 4)].unsqueeze(2).to_broadcast([P, 4, P]), ALU.is_equal)
                if q == 0:
                    v.wait_ge(w_ready, it + 1)
                for u in range(4):
                    v.wait_ge(gath[4 * q + u], 16 * (ITS + it + 1))
                v.tensor_tensor(msg[:, 4 * h:4 * h + 4, 0:D].rearrange("p u (h d) -> p u h d", h=H),
                                h_slot[:, 4 * q:4 * q + 4, :].rearrange("p u (h d) -> p u h d", h=H),
                                w_col[:, 4 * q:4 * q + 4, :].unsqueeze(3).to_broadcast([P, 4, H, HD]),
                                ALU.mult).then_inc(msgs, 1)

            v.sem_inc(added, 4)
            tile = read_tiles(v, 0, 12)
            for q in range(4):
                weigh(0, q)
                if q:
                    add_sums(q - 1, tile[4 * q - 4:4 * q])
            with v.Fori(1, ITS) as it:
                tile = read_tiles(v, 16 * it - 4, 16)
                for q in range(4):
                    weigh(it, q)
                    add_sums(4 * it + q - 1, tile[4 * q:4 * q + 4])
            add_sums(NQ - 1, read_tiles(v, STEPS - 4, 4))
            v.wait_ge(added, STEPS + 4)

            v.sem_inc(fin_made, 2)
            for h in range(2):
                v.sem_inc(stored[h], 16)
            with v.Fori(0, ITN) as it:
                for h in range(2):
                    v.tensor_scalar(den[h][:, 0, :], acc[:, ds((2 * it + h) * AW + D, H)], DEN_EPS, None,
                                    ALU.add).then_inc(den_made, 1)
                for h in range(2):
                    v.wait_ge(den_made, 2 * it + h + 1)
                    v.reciprocal(den[h][:, 1, :], den[h][:, 0, :]).then_inc(rden_made, 1)
                for h in range(2):
                    v.wait_ge(rden_made, 2 * it + h + 1)
                    v.tensor_tensor(res[h].rearrange("p (h d) -> p h d", h=H),
                                    acc[:, ds((2 * it + h) * AW, D)].rearrange("p (h d) -> p h d", h=H),
                                    den[h][:, 1, :].unsqueeze(2).to_broadcast([P, H, HD]), ALU.mult).then_inc(res_made, 1)
                for h in range(2):
                    v.wait_ge(res_made, 2 * it + h + 1)
                    v.tensor_tensor(res[h], res[h], nodes[:, ds((2 * it + h) * D, D)], ALU.add).then_inc(sum_made, 1)
                for h in range(2):
                    v.wait_ge(sum_made, 2 * it + h + 1)
                    v.bn_stats(stats[h][:, :], res[h]).then_inc(fstats_made, 1)
                for h in range(2):
                    v.wait_ge(fstats_made, 2 * it + h + 1)
                    v.sem_inc(fstats_seen, 1)
                    v.bn_aggr(agg2[h][:, :], stats[h][:, :]).then_inc(faggr_made, 1)
                for h in range(2):
                    v.wait_ge(faggr_made, 2 * it + h + 1)
                    v.tensor_scalar(veps[h][:, :], agg2[h][:, 1:2], LN_EPS, None, ALU.add).then_inc(fveps_made, 1)
                for h in range(2):
                    v.wait_ge(frstd_made, 2 * it + h + 1)
                    v.wait_ge(stored[h], 16 * (it + 1))
                    v.tensor_scalar(fin[h], res[h], agg2[h][:, 0:1], rstd[h][:, 0:1], ALU.subtract,
                                    ALU.mult).then_inc(fin_made, 1)

        @block.sync
        def _(sp):
            sp.wait_ge(pads_set, 3)
            for a, arr in enumerate((dst, src, etype)):
                sp.dma_start(rows_i[:, a, 0:FULL, :],
                             arr[0:FULL * P * P].rearrange("(b p e) -> p b e", p=P, e=P)).then_inc(edges_in, 16)
                sp.dma_start(rows_i[0:REST, a, FULL, :],
                             arr[FULL * P * P:(ET - 1) * P].rearrange("(p e) -> p e", e=P)).then_inc(edges_in, 16)
                sp.dma_start(rows_i[REST:REST + 1, a, FULL, 0:TAIL],
                             arr[(ET - 1) * P:E].rearrange("(p e) -> p e", p=1)).then_inc(edges_in, 16)
            for a, att in enumerate((attn_src, attn_dst)):
                sp.dma_start(acol[:, a, :], att.rearrange("h d -> (h d)").rearrange("(c p) -> p c", p=P),
                             allow_slow_non_contiguous=True).then_inc(weights_in, 16)
            sp.dma_start(w_nat, W.rearrange("r (c p) f -> p r c f", p=P)).then_inc(weights_in, 16)
            sp.dma_start(w0_sb, w0.rearrange("(c p) n -> p c n", p=P)).then_inc(weights_in, 16)
            sp.dma_start(w1_sb, w1.rearrange("(c p) n -> p c n", p=P)).then_inc(weights_in, 16)
            sp.dma_start(xT_sb[:, :, 0:N], xT.rearrange("(c p) n -> p c n", p=P)).then_inc(xT_in, 16)
            sp.wait_ge(setup, SU["rows"])
            sp.dma_start(edge_rows_d.rearrange("(b p) n -> p b n", p=P), rows_f).then_inc(rows_stored, 16)
            sp.wait_ge(pads_set, 4)
            for u in range(NACC):
                sp.dma_start(sums_d[u].rearrange("(p n) w -> p (n w)", p=P).rearrange("p (a n) -> p a n", n=NZ),
                             zeros.unsqueeze(1).to_broadcast([P, HALF // NZ, NZ])).then_inc(zeroed, 16)
            sp.wait_ge(setup, SU["tiles"])
            sp.dma_start(step_tile_d.rearrange("(b p) -> p b", p=P), j_i[:, 0:BLK],
                         allow_slow_non_contiguous=True).then_inc(steps_stored, 16)
            sp.wait_ge(setup, SU["step16"])
            sp.dma_start(step_rows_d.rearrange("(b p) a e -> p b a e", p=P), step16).then_inc(steps_stored, 16)
            sp.wait_ge(steps_stored, 32)
            sp.dma_start(tile_row[:, :], step_tile_d.rearrange("(a k) -> a k", a=1)).then_inc(steps_stored, 16)
            sp.wait_ge(steps_stored, 48)

            def source_rows(it):
                for q in range(4):
                    sp.wait_ge(eq_used, 4 * it + q + 1)
                    sp.dma_start(row16[q % 2][:, :, :],
                                 step_rows_d[ds(16 * it + 4 * q, 4), 0, :].partition_broadcast(P)).then_inc(row_in[q % 2], 16)

            source_rows(0)
            sp.wait_ge(setup, SU["end"])
            sp.wait_ge(tables_out, BLK)
            sp.wait_ge(nodes_padded, 1)
            NF = N // P
            sp.dma_start(nodes[:, 0:NF * D].rearrange("p (t w) -> p t w", w=D),
                         x[0:NF * P, :].rearrange("(t p) w -> p t w", p=P)).then_inc(x_in, 16)
            sp.dma_start(nodes[0:N - NF * P, NF * D:(NF + 1) * D], x[NF * P:N, :]).then_inc(x_in, 16)
            with sp.Fori(1, ITS) as it:
                source_rows(it)

            for h in range(2):
                rows_left(sp, h, 2 * ITS)
            with sp.Fori(0, ITN) as it:
                for h in range(2):
                    sp.wait_ge(parts_used, 2 * it + h + 1)
                    for u in range(NACC):
                        sp.dma_start(parts[h][:, u, :], sums_d[u][ds((2 * it + h) * P, P), :]).then_inc(parts_in[h], 16)
            sp.wait_ge(ab_copied, NT + 2)
            for h in range(2):
                sp.wait_ge(node_out[h], 32 * (ITN + 1))
            sp.dma_start(wT_sb, WT.rearrange("(c p) n -> p c n", p=P)).then_inc(tabs_in, 16)

            def destinations(g, h):
                sp.wait_ge(st_built, g + 1)
                sp.dma_start(row16[h][:, :, :],
                             step_rows_d[ds(4 * g, 4), 1, :].partition_broadcast(P)).then_inc(drow_in[h], 16)

            def with_node_tile(b, par, turn):
                sp.wait_ge(h_made, 4 * b + 4)
                sp.dma_start(x1s[par].rearrange("p c n -> p (c n)"), x1T_d[ds(b * P, P), :]).then_inc(x1s_in[par], 16)
                for q in range(4):
                    destinations(4 * b + q, q % 2)

            in_pairs(sp, 0, NT, with_node_tile)
            with sp.Fori(NT, ITS) as b:
                for q in range(4):
                    destinations(4 * b + q, q % 2)
            destinations(NQ, 0)

            sp.wait_ge(ends_made, 1)
            sp.dma_start(d_prev[H:P, :], d_row[0:P - H, 0:1]).then_inc(borders_in, 16)
            sp.dma_start(d_next[0:P - H, :], d_first[H:P, :]).then_inc(borders_in, 16)
            sp.wait_ge(ends_made, 3)
            sp.dma_start(ends_d, ends).then_inc(ends_io, 16)
            sp.wait_ge(ends_io, 16)
            sp.dma_start(crow[0:H, :, :], ends_d.rearrange("(c h) f -> h c f", h=H)).then_inc(ends_io, 16)
            sp.wait_ge(ends_made, 4)
            for a in range(2):
                sp.dma_start(carry_d.rearrange("(c h) f -> h f c", h=H)[:, a, :],
                             cres[0:H, a, a:a + CHUNKS], allow_slow_non_contiguous=True).then_inc(carry_io, 16)
            sp.wait_ge(carry_io, 32)
            sp.dma_start(carry, carry_d).then_inc(carry_io, 16)

            with sp.Fori(0, (NT - 2) // 2) as it:
                for h in range(2):
                    sp.wait_ge(fin_made, 2 * it + h + 3)
                    sp.dma_start(out[ds((2 * it + h) * P, P), :], fin[h]).then_inc(stored[h], 16)
            sp.wait_ge(fin_made, NT - 2 + 3)
            sp.dma_start(out[(NT - 2) * P:N, :], fin[0][0:N - (NT - 2) * P, :]).then_inc(stored[0], 16)
            sp.wait_ge(stored[0], 16 * ((NT - 2) // 2 + 2))
            sp.wait_ge(stored[1], 16 * ((NT - 2) // 2 + 1))

        @block.gpsimd
        def _(g):
            g.iota(it_i, [[1, P]], base=0, channel_multiplier=0).then_inc(iotas, 1)
            g.iota(pt_i, [[0, 1]], base=0, channel_multiplier=1).then_inc(iotas, 1)
            g.wait_ge(setup, SU["tiles"])
            g.wait_ge(rows_stored, 16)
            for b in range(BLK):
                g.indirect_dma_start(step_f[:, b, :], None, edge_rows_d,
                                     bass.IndirectOffsetOnAxis(ap=i_i[:, b:b + 1], axis=0),
                                     bounds_check=KP - 1, oob_is_err=True).then_inc(step_rows, 16)
            node_bound = g.snap(g.to_reg(NP_ - 1))
            row_bound = g.snap(g.to_reg(NP_ * R - 1))

            def scatter(it):
                for q in range(4):
                    h = q % 2
                    g.wait_ge(sums_copied, 4 * it + q + 3)
                    g.wait_ge(slots_ready, 4 * it + q + 1)
                    for u in range(4):
                        if not isinstance(it, int) or q:
                            g.wait_ge(scattered[1 - h][u], 16 * (2 * it + (q + 1) // 2))
                        g.sem_inc(pool_turns, 1)
                        g.indirect_dma_start(sums_d[u],
                                             bass.IndirectOffsetOnAxis(ap=idx_slot[:, 4 * q + u:4 * q + u + 1], axis=0),
                                             sums[h][:, u, :], None, bounds_check=node_bound, oob_is_err=True,
                                             compute_op=ALU.add).then_inc(scattered[h][u], 16)

            g.wait_ge(zeroed, 16 * NACC)
            scatter(0)
            with g.Fori(1, ITS) as it:
                scatter(it)

            with g.Fori(0, ITN) as it:
                for h in range(2):
                    g.wait_ge(parts_in[h], 16 * NACC * (it + 1))
                    g.tensor_tensor(parts[h][:, 2, :], parts[h][:, 2, :], parts[h][:, 3, :], ALU.add).then_inc(pooled, 1)
                for h in range(2):
                    g.wait_ge(veps_made, 2 * it + h + 1)
                    g.tensor_tensor(rstd[h][:, :], veps[h][:, :], minus_half[:, :], ALU.pow).then_inc(rstd_made, 1)

            for h in range(2):
                g.wait_ge(node_out[h], 32 * (ITN + 1))
            a_rows = a_d.rearrange("n (r h) -> (n r) h", h=H)
            with g.Fori(0, ITS) as it:
                for q in range(4):
                    g.wait_ge(idx_ready, 4 * it + q + 1)
                    g.sem_inc(pool_turns, 1)
                    for u in range(4):
                        k = 4 * q + u
                        g.indirect_dma_start(a_slot[:, k, :], None, a_rows,
                                             bass.IndirectOffsetOnAxis(ap=idx_slot[:, k:k + 1], axis=0),
                                             bounds_check=row_bound, oob_is_err=True).then_inc(gath[k], 16)

            for q in range(4):
                g.wait_ge(h_stored[q], 16 * (NT + 1))
            h_rows = h_d.rearrange("n (r w) -> (n r) w", w=D)
            with g.Fori(0, ITS) as it:
                for q in range(4):
                    g.wait_ge(idx_ready, NQ + 4 + 4 * it + q + 1)
                    g.sem_inc(pool_turns, 1)
                    for u in range(4):
                        k = 4 * q + u
                        g.indirect_dma_start(h_slot[:, k, :], None, h_rows,
                                             bass.IndirectOffsetOnAxis(ap=idx_slot[:, k:k + 1], axis=0),
                                             bounds_check=row_bound, oob_is_err=True).then_inc(gath[k], 16)

            with g.Fori(0, ITN) as it:
                for h in range(2):
                    g.wait_ge(fveps_made, 2 * it + h + 1)
                    g.tensor_tensor(rstd[h][:, :], veps[h][:, :], minus_half[:, :], ALU.pow).then_inc(frstd_made, 1)

        @block.scalar
        def _(a):
            a.wait_ge(xT_in, 16)
            a.wait_ge(pads_set, 6)
            a.wait_ge(wab_ps, 1)
            a.sem_inc(y_done, 2)
            with a.Fori(0, ITN) as it:
                for h in range(2):
                    a.wait_ge(y_ps, 2 * it + h + 1)
                    a.copy(xs0[h], xT_sb[:, :, ds((2 * it + h) * P, P)]).then_inc(y_x, 1)
                for h in range(2):
                    a.wait_ge(y_ps, 2 * it + h + 3)
                    a.copy(y_sb[:, ds((2 * it + h) * D, D)], ps[:, h, 0:D]).then_inc(y_done, 1)
            for b in range(BLK):
                a.wait_ge(tables_ps, b + 1)
                bank = ps[:, 2 * (b % 2):2 * (b % 2) + 2, :].rearrange("p a n -> p (a n)")
                cols = slice(b * P, b * P + P)
                for n, t in ((0, dst_t), (2, type_t), (3, idx_t)):
                    a.copy(t[:, cols], bank[:, n * P:n * P + P])
                a.copy(src_t[:, cols], bank[:, P:2 * P]).then_inc(tables_out, 1)

            a.sem_inc(counts_copied, 2)
            a.sem_inc(sums_copied, 2)

            def copy_sums(it, q):
                h = q % 2
                a.wait_ge(sums_made, 4 * it + q + 3)
                rows_left(a, h, 2 * it + q // 2)
                a.copy(sums[h][:, :, :],
                       ps[:, 2 + 2 * h:4 + 2 * h, :].rearrange("p b (u n) -> p (b u) n", u=2)).then_inc(sums_copied, 1)

            def evacuate(it):
                for q in range(4):
                    a.wait_ge(counts_made, 4 * it + q + 3)
                    a.wait_ge(sums_made, 4 * it + q + 1)
                    a.copy(counts[q % 2], ps[:, q % 2, :].rearrange("p (u e) -> p u e", u=4)).then_inc(counts_copied, 1)
                    if q:
                        copy_sums(it, q - 1)
                copy_sums(it, 3)

            a.wait_ge(zeroed, 16 * NACC)
            evacuate(0)
            with a.Fori(1, ITS) as it:
                evacuate(it)

            for h in range(2):
                rows_left(a, h, 2 * ITS)
            a.sem_inc(ab_copied, 2)
            a.sem_inc(x1_kept, 2)
            for h in range(2):
                a.sem_inc(node_out[h], 32)

            def copy_x(it):
                for h in range(2):
                    a.wait_ge(x0_ps, 2 * it + h + 1)
                    a.copy(xs[h], xT_sb[:, :, ds((2 * it + h) * P, P)]).then_inc(x0_x, 1)

            def copy_nodes(it):
                for h in range(2):
                    a.wait_ge(xn_made, 2 * it + h + 3)
                    a.copy(nodes[:, ds((2 * it + h) * D, D)], xn[h]).then_inc(x1_kept, 1)
                for h in range(2):
                    a.wait_ge(xt_ps, 2 * it + h + 3)
                    a.wait_ge(ab_ps, 2 * it + h + 1)
                    a.wait_ge(node_out[h], 32 * (it + 1))
                    a.copy(xts[h], ps[:, 2 + h, 0:DC * P].rearrange("p (c n) -> p c n", c=DC)).then_inc(xts_made, 1)
                for h in range(2):
                    rows = ds((2 * it + h) * P, P)
                    a.wait_ge(xts_made, 2 * it + h + 1)
                    a.dma_start(x1T_d[rows, :], xts[h].rearrange("p c n -> p (c n)")).then_inc(node_out[h], 16)
                    a.wait_ge(ab_ps, 2 * it + h + 3)
                    a.copy(b_sb[:, ds((2 * it + h) * RH, RH)], ps[:, 4 + h, RH:2 * RH])
                    a.copy(a_out[h], ps[:, 4 + h, 0:RH]).then_inc(ab_copied, 1)
                for h in range(2):
                    a.wait_ge(ab_copied, 2 * it + h + 3)
                    a.dma_start(a_d[ds((2 * it + h) * P, P), :], a_out[h]).then_inc(node_out[h], 16)

            copy_x(0)
            with a.Fori(0, ITN - 1) as it:
                copy_x(it + 1)
                copy_nodes(it)
            copy_nodes(ITN - 1)

            for h in range(2):
                a.wait_ge(node_out[h], 32 * (ITN + 1))
            a.wait_ge(tabs_in, 16)
            a.sem_inc(h_copied, 2)
            a.sem_inc(block_out, 1)
            for q in range(4):
                a.sem_inc(h_stored[q], 16)

            def indices(it, q):
                a.copy(idx_slot[:, 4 * q:4 * q + 4], idx_t[:, ds(16 * it + 4 * q, 4)]).then_inc(idx_ready, 1)

            def destinations(b):
                a.copy(dblock, dst_t[:, ds(b * CHUNKS, CHUNKS)].unsqueeze(2)
                       .to_broadcast([P, CHUNKS, H])).then_inc(dblock_made, 1)

            def copy_block(b):
                a.wait_ge(turned, b + 3)
                a.wait_ge(blocks_done, b + 1)
                a.copy(s_row, ps[:, 4, 0:P])
                a.copy(d_row[:, 1:P + 1], ps[:, 4, P:2 * P])
                a.copy(s_T[:, ds(b * P, P)], ps[:, 4, 0:P]).then_inc(block_out, 1)

            for q in range(4):
                indices(0, q)
            destinations(0)
            a.wait_ge(first_out, 1)

            def copy_tables(b, with_h):
                for q in range(4):
                    if with_h:
                        a.wait_ge(h_made, 4 * b + q + 9)
                        a.wait_ge(h_stored[q], 16 * (b + 1))
                        a.copy(h_out[:, q, :], ps[:, 2 + q % 2, :]).then_inc(h_copied, 1)
                        a.wait_ge(h_copied, 4 * b + q + 3)
                        a.dma_start(h_d[ds(b * P, P), 512 * q:512 * q + 512], h_out[:, q, :]).then_inc(h_stored[q], 16)
                    if q == 0 and not (isinstance(b, int) and b == 0):
                        copy_block(b - 1)
                        destinations(b)
                    a.wait_ge(scored, 4 * b + q + 5)
                    indices(b + 1, q)

            copy_tables(0, True)
            with a.Fori(1, NT) as b:
                copy_tables(b, True)
            with a.Fori(NT, ITS) as b:
                copy_tables(b, False)
            copy_block(ITS - 1)

            for q in range(4):
                a.wait_ge(h_stored[q], 16 * (NT + 1))
            a.wait_ge(shifted, 3)

            def exponentials(it):
                a.activation(e_row, s_T[:, ds(it * P, P)], ACT.Exp).then_inc(exps, 1)

            def weights(it):
                a.wait_ge(w_turned, it + 1)
                a.copy(w_col.rearrange("p k h -> p (k h)"), ps[:, 4, 0:P]).then_inc(w_ready, 1)

            def weights_and_indices(it, more):
                for q in range(4):
                    a.wait_ge(segs, 16 * it + 4 * q + 4)
                    if q == 0:
                        a.wait_ge(w_ready, it + 1)
                    a.copy(msg[:, 4 * (q % 2):4 * (q % 2) + 4, D:AW], w_col[:, 4 * q:4 * q + 4, :]).then_inc(w_placed, 1)
                    if more and q == 0:
                        exponentials(it + 1)
                    if more:
                        a.wait_ge(msgs, 4 * it + q + 1)
                        indices(it + 1, q)
                if more:
                    a.wait_ge(w_placed, 4 * it + 4)
                    weights(it + 1)

            for q in range(4):
                indices(0, q)
            exponentials(0)
            weights(0)
            with a.Fori(0, ITS - 1) as it:
                weights_and_indices(it, True)
            weights_and_indices(ITS - 1, False)

        @block.tensor
        def _(t):
            t.wait_ge(setup, SU["firsts"])
            for b in range(BLK):
                mm = t.matmul(ps[:, 4 + b // 4, (b % 4) * P:(b % 4) * P + P], lhsT=cf[:, b:b + 1].to_broadcast([P, P]),
                              rhs=ident[:, :], start=True, stop=True)
            mm.then_inc(firsts_made, 1)
            t.wait_ge(setup, SU["blk"])
            t.wait_ge(weights_in, 80)
            for fc in range(DC):
                for r in range(R):
                    for c in range(DC):
                        mm = t.matmul(ps[:, 6, fc * 2 * RH + r * 2 * H:fc * 2 * RH + (r + 1) * 2 * H],
                                      lhsT=w_nat[:, r, c, fc * P:(fc + 1) * P], rhs=blk[:, c, :],
                                      start=(c == 0), stop=(c == DC - 1))
            mm.then_inc(wab_ps, 1)
            t.sem_inc(y_ps, 2)
            with t.Fori(0, ITN) as it:
                for h in range(2):
                    t.wait_ge(y_x, 2 * it + h + 1)
                    t.wait_ge(y_done, 2 * it + h + 1)
                    for c in range(DC):
                        mm = t.matmul(ps[:, h, 0:D], lhsT=xs0[h][:, c, :], rhs=w1_sb[:, c, :],
                                      start=(c == 0), stop=(c == DC - 1))
                    mm.then_inc(y_ps, 1)
            t.wait_ge(y_done, NT + 2)
            t.wait_ge(setup, SU["local"])
            for b in range(BLK):
                if b >= 2:
                    t.wait_ge(tables_out, b - 1)
                    t.wait_ge(local_out, b - 1)
                for n in range(5):
                    s = step_f[:, b, n * P:(n + 1) * P] if n < 4 else step_local[:, b, :]
                    mm = t.transpose(ps[:, 2 * (b % 2) + n // 4, (n % 4) * P:(n % 4) * P + P], s, ident[:, :])
                mm.then_inc(tables_ps, 1)
            t.wait_ge(tables_out, BLK)
            t.wait_ge(local_out, BLK)

            t.wait_ge(steps_stored, 48)
            t.sem_inc(counts_made, 2)
            t.sem_inc(sums_made, 2)

            def sum_rows(it, q, tile):
                h = q % 2
                t.wait_ge(counts_copied, 4 * it + q + 3)
                t.wait_ge(sums_copied, 4 * it + q + 1)
                for u in range(4):
                    mm = t.matmul(ps[:, 2 + 2 * h + u // 2, (u % 2) * D:(u % 2) * D + D], lhsT=counts[h][:, u, :],
                                  rhs=y_sb[:, ds(tile[4 * q + u] * D, D)], start=True, stop=True)
                mm.then_inc(sums_made, 1)

            with t.Fori(0, ITS) as it:
                tile = read_tiles(t, 16 * it, 16)
                for q in range(4):
                    h = q % 2
                    t.wait_ge(onehots, 4 * it + q + 1)
                    t.wait_ge(counts_copied, 4 * it + q + 1)
                    for u in range(4):
                        mm = t.matmul(ps[:, h, u * P:(u + 1) * P], lhsT=onehot[h][:, u, :], rhs=eq[h][:, u, :],
                                      start=True, stop=True)
                    mm.then_inc(counts_made, 1)
                    if q:
                        sum_rows(it, q - 1, tile)
                sum_rows(it, 3, tile)

            t.wait_ge(sums_copied, NQ + 2)
            t.sem_inc(x0_ps, 2)
            t.sem_inc(xt_ps, 2)
            t.sem_inc(ab_ps, 2)

            def first_product(it):
                for h in range(2):
                    t.wait_ge(x0_x, 2 * it + h + 1)
                    t.wait_ge(x0_used, 2 * it + h + 1)
                    for c in range(DC):
                        mm = t.matmul(ps[:, h, 0:D], lhsT=xs[h][:, c, :], rhs=w0_sb[:, c, :],
                                      start=(c == 0), stop=(c == DC - 1))
                    mm.then_inc(x0_ps, 1)

            def node_products(it):
                for h in range(2):
                    t.wait_ge(xn_made, 2 * it + h + 3)
                    for c in range(DC):
                        mm = t.transpose(ps[:, 2 + h, c * P:(c + 1) * P], xn[h][:, c * P:(c + 1) * P], ident[:, :])
                    mm.then_inc(xt_ps, 1)
                for h in range(2):
                    t.wait_ge(xts_made, 2 * it + h + 1)
                    t.wait_ge(ab_copied, 2 * it + h + 1)
                    for c in range(DC):
                        mm = t.matmul(ps[:, 4 + h, 0:2 * RH], lhsT=xts[h][:, c, :], rhs=wab[:, c, :],
                                      start=(c == 0), stop=(c == DC - 1))
                    mm.then_inc(ab_ps, 1)

            first_product(0)
            with t.Fori(0, ITN - 1) as it:
                first_product(it + 1)
                node_products(it)
            node_products(ITN - 1)

            t.wait_ge(tabs_in, 16)
            t.wait_ge(ab_copied, NT + 2)
            t.wait_ge(dblock_made, 1)
            t.transpose(ps[:, 5, 0:P], dblock.rearrange("p c h -> p (c h)"), ident[:, :]).then_inc(first_turned, 1)
            t.wait_ge(first_out, 1)
            t.sem_inc(b_made, 2)
            t.sem_inc(h_made, 8)
            t.sem_inc(turned, 2)

            def turn(b, par):
                t.wait_ge(scored, 4 * b + 8)
                t.wait_ge(dblock_made, b + 1)
                t.wait_ge(block_out, b + 1)
                t.transpose(ps[:, 4, 0:P], zblock[par].rearrange("p k h -> p (k h)"), ident[:, :])
                t.transpose(ps[:, 4, P:2 * P], dblock.rearrange("p c h -> p (c h)"), ident[:, :]).then_inc(turned, 1)

            def destination_scores(g, h, tile):
                t.wait_ge(st_built, g + 3)
                t.wait_ge(scored, g + 3)
                for u in range(4):
                    mm = t.matmul(ps[:, h, u * RH:(u + 1) * RH], lhsT=st[h][:, u, :],
                                  rhs=b_sb[:, ds(tile[u] * RH, RH)], start=True, stop=True)
                mm.then_inc(b_made, 1)

            def tables(b, par, turns, with_h, last=False):
                tile = read_tiles(t, 16 * b + 4, 12 if last else 16)
                for q in range(4):
                    if q == 0 and not (isinstance(b, int) and b == 0):
                        turn(b - 1, 1 - par)
                    if not (last and q == 3):
                        destination_scores(4 * b + q + 1, (q + 1) % 2, tile[4 * q:4 * q + 4])
                    if with_h:
                        if q == 0:
                            t.wait_ge(x1s_in[par], 16 * (turns + 1))
                        t.wait_ge(h_copied, 4 * b + q + 1)
                        for c in range(DC):
                            mm = t.matmul(ps[:, 2 + q % 2, :], lhsT=x1s[par][:, c, :],
                                          rhs=wT_sb[:, c, 512 * q:512 * q + 512], start=(c == 0), stop=(c == DC - 1))
                        mm.then_inc(h_made, 1)

            destination_scores(0, 0, read_tiles(t, 0, 4))
            tables(0, 0, 0, True)
            in_pairs(t, 1, NT, lambda b, par, turns: tables(b, par, turns, True))
            in_pairs(t, NT, ITS - 1, lambda b, par, turns: tables(b, par, turns, False))
            tables(ITS - 1, (ITS - 1) % 2, 0, False, last=True)
            turn(ITS - 1, (ITS - 1) % 2)

            t.sem_inc(segs, 8)

            def turn_weights(it):
                t.wait_ge(exps, it + 1)
                if not isinstance(it, int):
                    t.wait_ge(w_ready, it)
                t.transpose(ps[:, 4, 0:P], e_row, ident[:, :]).then_inc(w_turned, 1)

            def sum_edges(it, more):
                for q in range(4):
                    t.wait_ge(w_placed, 4 * it + q + 1)
                    t.wait_ge(msgs, 4 * it + q + 1)
                    for u in range(4):
                        k = 4 * (q % 2) + u
                        t.wait_ge(added, 16 * it + 4 * q + u + 1)
                        t.matmul(ps[:, u, 0:AW], lhsT=sel[:, k, :], rhs=msg[:, k, :],
                                 start=True, stop=True).then_inc(segs, 1)
                    if more and q == 1:
                        turn_weights(it + 1)

            turn_weights(0)
            with t.Fori(0, ITS - 1) as it:
                sum_edges(it, True)
            sum_edges(ITS - 1, False)


def kernel(x, src, dst, edge_type_8, L0_gnn_w0, L0_gnn_w1, L1_gnn_W, L1_gnn_attn_src, L1_gnn_attn_dst):
    import numpy as np
    import concourse.bacc as bacc
    from concourse.bass_utils import run_bass_kernel_spmd

    x, W = np.asarray(x), np.asarray(L1_gnn_W)
    n, d = x.shape
    r = W.shape[0]
    arrays = {
        "x": x, "xT": np.ascontiguousarray(x.T),
        "src": np.asarray(src), "dst": np.asarray(dst), "etype": np.asarray(edge_type_8),
        "w0": np.asarray(L0_gnn_w0), "w1": np.asarray(L0_gnn_w1),
        "W": W, "WT": np.ascontiguousarray(W.transpose(2, 0, 1).reshape(d, r * d)),
        "attn_src": np.asarray(L1_gnn_attn_src), "attn_dst": np.asarray(L1_gnn_attn_dst),
    }
    nc = bacc.Bacc("TRN2", target_bir_lowering=False, num_devices=1)
    aps = {k: nc.dram_tensor(k + "_in", a.shape, mybir.dt.from_np(a.dtype), kind="ExternalInput").ap()
           for k, a in arrays.items()}
    out = nc.dram_tensor("out", (n, d), F32, kind="ExternalOutput").ap()
    graph_layers(nc, out=out, **aps)
    r = run_bass_kernel_spmd(nc, [{k + "_in": a for k, a in arrays.items()}], core_ids=[0])
    return r.results[0]["out"]
```

```python
from contextlib import ExitStack

import concourse.bass as bass
from concourse import mybir

P = 128
F32 = mybir.dt.float32
BF16 = mybir.dt.bfloat16
I32 = mybir.dt.int32
I16 = mybir.dt.int16
ALU = mybir.AluOpType
ACT = mybir.ActivationFunctionType
X = mybir.AxisListType.X

BIG = 1.0e30
NO_NODE = 8191.0
LN_EPS = 1e-5
DEN_EPS = 1e-12
SLOPE = 0.2


def graph_layers(nc, x, xT, src, dst, etype, w0, w1, W, WT, attn_src, attn_dst, out):
    N, D = x.shape
    E = src.shape[0]
    R = W.shape[0]
    H, HD = attn_src.shape
    DC = D // P
    NT = -(-N // P) + 1
    NP_ = NT * P
    ET = -(-E // P)
    TAIL = E - (ET - 1) * P
    CHUNKS = 16
    LEN = -(-(ET + NT - 2) // CHUNKS)
    STEPS = CHUNKS * LEN
    BLK = -(-STEPS // P)
    KP = BLK * P
    FULL = (ET - 1) // P
    REST = (ET - 1) - FULL * P
    RH = R * H
    SCAN = LEN * P
    NACC = 4
    assert P == CHUNKS * H and  D == H * HD

    def dram(name, shape, dt):
        return nc.dram_tensor(name, shape, dt, kind="Internal").ap()

    edge_rows_d = dram("edge_rows_d", [KP, 4 * P], F32)
    step_rows_d = dram("step_rows_d", [KP, 2, P], I16)
    step_tile_d = dram("step_tile_d", [KP], I32)
    sums_d = [dram(f"sums_d{u}", [NP_, D], F32) for u in range(NACC)]
    a_d = dram("a_d", [NP_, RH], F32)
    h_d = dram("h_d", [NP_, R * D], F32)
    x1T_d = dram("x1T_d", [NP_, DC * P], F32)
    ends_d = dram("ends_d", [P, 4], F32)
    carry_d = dram("carry_d", [P, 2], F32)

    with ExitStack() as ctx:
        def sb(name, shape, dt):
            return ctx.enter_context(nc.sbuf_tensor(name, shape, dt))

        def sem(name):
            return ctx.enter_context(nc.semaphore(name))

        nodes = sb("nodes", [P, NT * D], F32)
        region = sb("region", [P, 2 * DC * NP_], F32)
        ZW = STEPS * H
        edge_z = sb("edge_z", [P, ZW], F32)
        dst_t = sb("dst_t", [P, KP], F32)
        type_t = sb("type_t", [P, KP], F32)
        local_t = sb("local_t", [P, KP], F32)
        idx_t = sb("idx_t", [P, KP], I32)
        mask_t = sb("mask_t", [P, KP], F32)
        ident = sb("ident", [P, P], F32)
        iota_row = sb("iota_row", [P, P], F32)
        before = sb("before", [P, P], BF16)
        part = sb("part", [P, 1], F32)
        minus_half = sb("minus_half", [P, 2], F32)
        iota8 = sb("iota8", [P, R], F32)
        idx_slot = sb("idx_slot", [P, 16], I32)
        ps = ctx.enter_context(nc.psum_tensor("ps", [P, 8, 512], F32))
        HALF = DC * NP_
        assert D * NT <= HALF

        def view(base, at, *shape):
            n = 1
            for s in shape:
                n *= s
            v = base[:, at:at + n]
            names = "abcd"[:len(shape)]
            if len(shape) > 1:
                v = v.rearrange(f"p ({' '.join(names)}) -> p {' '.join(names)}",
                                **{k: s for k, s in zip(names, shape)})
            return v

        o = 0
        rows_i = view(nodes, o, 3, BLK, P).bitcast(I32); o += 3 * BLK * P
        rows_f = view(nodes, o, BLK, 4 * P); o += BLK * 4 * P
        step_f = view(nodes, o, BLK, 4 * P); o += BLK * 4 * P
        firsts = view(nodes, o, KP); o += KP
        cmp = view(nodes, o, KP); o += KP
        step_local = view(nodes, o, BLK, P); o += BLK * P
        assert o <= NT * D
        w_nat = view(region, HALF + NT * D - R * DC * D, R, DC, D)
        SPLIT = (NT - R * DC) // 2
        o = 2 * KP + 2 * DC * D
        step16 = view(edge_z, o, BLK * P).bitcast(I16).rearrange("p (b a e) -> p b a e", b=BLK, a=2); o += BLK * P
        misc = view(edge_z, o, 512); o += 512
        xs0 = [view(edge_z, o + DC * P * h, DC, P) for h in range(2)]; o += 2 * DC * P
        assert o <= ZW
        NZ = 800
        ki = misc[:, 0:8].bitcast(I32)
        kt = misc[:, 8:16].bitcast(I32)
        kf = misc[:, 16:24]
        kh = misc[:, 24:32]
        jfi = misc[:, 32:40].bitcast(I32)
        cf = misc[:, 40:48]
        i_f = misc[:, 48:56]
        j_f = misc[:, 56:64]
        j128 = misc[:, 64:72]
        i_i = misc[:, 72:80].bitcast(I32)
        j_i = misc[:, 80:88].bitcast(I32)
        acol = misc[:, 96:96 + 2 * DC].rearrange("p (a c) -> p a c", a=2)
        hsel = misc[:, 104:108]
        q32 = misc[:, 108:109]
        tmp4 = misc[:, 112:116]
        it_i = misc[:, 128:256].bitcast(I32)
        pt_i = misc[:, 256:257].bitcast(I32)
        blk = misc[:, 264:264 + DC * 2 * H].rearrange("p (c n) -> p c n", c=DC)
        tile_row = sb("tile_row", [1, KP], I32)
        wab = sb("wab", [P, DC, 2 * RH], F32)

        xT_sb = view(region, 0, DC, NP_)
        y_sb = view(region, HALF, NT * D)
        o = 0
        src_t = view(edge_z, o, KP); o += KP
        trash_t = view(edge_z, o, KP); o += KP
        w0_sb = view(edge_z, o, DC, D); o += DC * D
        w1_sb = view(edge_z, o, DC, D); o += DC * D
        eq = [view(edge_z, o + 256 * h, 256).bitcast(BF16).rearrange("p (u e) -> p u e", u=4) for h in range(2)]; o += 512
        onehot = [view(edge_z, o + 256 * h, 256).bitcast(BF16).rearrange("p (u e) -> p u e", u=4) for h in range(2)]; o += 512
        counts = [view(edge_z, o + 512 * h, 4, P) for h in range(2)]; o += 1024
        xs = [view(edge_z, o + DC * P * h, DC, P) for h in range(2)]; o += 2 * DC * P
        sums = [sb("sums0", [P, 4, D], F32)]
        zeros = sums[0][:, :, :].rearrange("p u n -> p (u n)")[:, 0:NZ]
        sums.append(view(edge_z, o, 4, D)); o += 4 * D
        eqj = view(edge_z, o, 2 * P).bitcast(BF16).rearrange("p (u e) -> p u e", u=4); o += 2 * P
        assert o <= ZW
        row16 = [sb(f"row16_{h}", [P, 4, P], I16) for h in range(2)]
        dup = sb("dup", [P, 8], F32)
        dup2 = sb("dup2", [P, 8], F32)

        parts = [view(region, HALF + 2 * NACC * D * h, NACC, 2, D) for h in range(2)]
        assert 4 * NACC * D <= SCAN
        o = 2 * KP + 2 * DC * D
        x2t = [view(edge_z, o + 2 * DC * P * h, DC, 2 * P) for h in range(2)]; o += 4 * DC * P
        xn = [view(edge_z, o + D * h, D) for h in range(2)]; o += 2 * D
        tmp = [view(edge_z, o + 2 * D * h, 2, D) for h in range(2)]; o += 4 * D
        assert o <= ZW
        xts = [view(edge_z, 0 + DC * P * h, DC, P) for h in range(2)]
        a_out = [view(edge_z, 2 * DC * P + RH * h, RH) for h in range(2)]
        assert 2 * DC * P + 2 * RH <= 2 * KP
        stats = [sb(f"stats{h}", [P, 6], F32) for h in range(2)]
        moments = [sb(f"moments{h}", [P, 2, 2], F32) for h in range(2)]
        veps = [sb(f"veps{h}", [P, 2], F32) for h in range(2)]
        rstd = [sb(f"rstd{h}", [P, 2], F32) for h in range(2)]

        o = 0
        wT_sb = view(region, o, DC, R * D); o += DC * R * D
        h_out = view(region, o, 4, 512); o += 2048
        st = [view(region, o + 4 * P * h, 4, P) for h in range(2)]; o += 8 * P
        prod = view(region, o, 4, H, R); o += 4 * RH
        tmask = view(region, o, 4, R); o += 4 * R
        bsel = view(region, o, 4, H); o += 4 * H
        zt = view(region, o, 4, H); o += 4 * H
        zl = view(region, o, 4, H); o += 4 * H
        a_slot = view(region, o, 16, H); o += 16 * H
        x1s = [view(region, o + DC * P * h, DC, P) for h in range(2)]; o += 2 * DC * P
        zblock = [view(region, o + P * h, 16, H) for h in range(2)]; o += 2 * P
        dblock = view(region, o, CHUNKS, H); o += P
        assert o <= HALF
        o = HALF
        keep = view(region, o, SCAN + 1); o += SCAN + 1
        d_row = view(region, o, P + 1); o += P + 1
        s_row = view(region, o, P); o += P
        run = view(region, o, P); o += P
        lead = view(region, o, P); o += P
        led = view(region, o, P); o += P
        lmax = view(region, o, 2); o += 2
        d_first = view(region, o, 1); o += 1
        d_prev = view(region, o, 1); o += 1
        d_next = view(region, o, 1); o += 1
        k_first = view(region, o, 2); o += 2
        ends = view(region, o, 4); o += 4
        carry = view(region, o, 2); o += 2
        crow = view(region, o, CHUNKS, 4); o += 4 * CHUNKS
        cres = view(region, o, 2, CHUNKS + 1); o += 2 * (CHUNKS + 1)
        h_slot = view(region, o, 16, D)
        b_sb = view(region, o, NT * RH); o += max(NT * RH, 16 * D)
        assert o <= 2 * HALF
        fwd = view(region, 0, SCAN)
        s_T = view(edge_z, 0, SCAN)

        AW = D + H
        o = 0
        acc = view(region, o, NT * AW); o += NT * AW
        msg = view(region, o, 8, AW); o += 8 * AW
        sel = view(region, o, 8, P); o += 8 * P
        e_row = view(region, o, P); o += P
        w_col = view(region, o, 16, H); o += P
        den = view(region, o, 2, 2, H); o += 4 * H
        res = [view(region, o + 2 * D * h, 2, D) for h in range(2)]; o += 4 * D
        fin = [view(region, o + D * h, D) for h in range(2)]; o += 2 * D
        assert o <= HALF + SCAN + 1

        names = """pads_set edges_in weights_in wx_in iotas setup rows_stored firsts_made step_rows steps_stored
            tables_ps tables_out local_out wab_ps x_in xT_in nodes_padded y_x y_ps y_done zeroed
            onehots eq_used dup_scaled slots_ready counts_made counts_copied sums_made sums_copied
            halves_made pooled parts_used x0_ps x0_used relu_made stats_made stats_seen aggr_made veps_made rstd_made
            xn_made x1_kept xt_ps xts_made ab_ps ab_copied
            tabs_in idx_ready h_made h_copied st_built mask_made b_made prod_made bsel_made z_made
            z_sloped scored dblock_made turned block_out keep_made run_made lead_made led_made lmax_made
            blocks_done first_turned first_out ends_made borders_in ends_io carry_io shifted
            exps w_turned w_ready w_placed acc_zero pool_turns msgs segs added
            den_made rden_made res_made sum_made fstats_made fstats_seen faggr_made fveps_made frstd_made
            fin_made""".split()
        (pads_set, edges_in, weights_in, wx_in, iotas, setup, rows_stored, firsts_made, step_rows, steps_stored,
         tables_ps, tables_out, local_out, wab_ps, x_in, xT_in, nodes_padded, y_x, y_ps, y_done, zeroed,
         onehots, eq_used, dup_scaled, slots_ready, counts_made, counts_copied, sums_made, sums_copied,
         halves_made, pooled, parts_used, x0_ps, x0_used, relu_made, stats_made, stats_seen, aggr_made, veps_made, rstd_made,
         xn_made, x1_kept, xt_ps, xts_made, ab_ps, ab_copied,
         tabs_in, idx_ready, h_made, h_copied, st_built, mask_made, b_made, prod_made, bsel_made, z_made,
         z_sloped, scored, dblock_made, turned, block_out, keep_made, run_made, lead_made, led_made, lmax_made,
         blocks_done, first_turned, first_out, ends_made, borders_in, ends_io, carry_io, shifted,
         exps, w_turned, w_ready, w_placed, acc_zero, pool_turns, msgs, segs, added,
         den_made, rden_made, res_made, sum_made, fstats_made, fstats_seen, faggr_made, fveps_made, frstd_made,
         fin_made) = [sem(n) for n in names]
        row_in = [sem(f"row_in{h}") for h in range(2)]
        x1s_in = [sem(f"x1s_in{h}") for h in range(2)]
        drow_in = [sem(f"drow_in{h}") for h in range(2)]
        x0_x = [sem(f"x0_x{h}") for h in range(2)]
        parts_in = [sem(f"parts_in{h}") for h in range(2)]
        node_out = [sem(f"node_out{h}") for h in range(2)]
        stored = [sem(f"stored{h}") for h in range(2)]
        h_stored = [sem(f"h_stored{q}") for q in range(4)]
        scattered = [[sem(f"scattered{h}{u}") for u in range(4)] for h in range(2)]
        gath = [sem(f"gath{k}") for k in range(16)]

        block = ctx.enter_context(nc.Block())
        ds = bass.ds
        NQ = STEPS // 4
        ITN = NT // 2
        ITS = LEN
        assert NT % 2 == 0 and NT < ITS
        SU = {}

        def rows_left(eng, h, times):
            if isinstance(times, int) and times <= 0:
                return
            for u in range(4):
                eng.wait_ge(scattered[h][u], 16 * times)

        def read_tiles(eng, at, n):
            regs = [eng.alloc_register(f"tile{k}_{nc.next_id()}") for k in range(n)]
            eng.load(regs, tile_row[0:1, ds(at, n)])
            return [eng.snap(r, min_val=0, max_val=NT - 1) for r in regs]

        def in_pairs(eng, first, end, body):
            with eng.Fori(0, (end - first) // 2) as i:
                for n in range(first, first + 2):
                    body(2 * i + n, n % 2, i + n // 2)
            if (end - first) % 2:
                body(end - 1, (end - 1) % 2, (end - 1) // 2)

        @block.vector
        def _(v):
            n = [0]

            def do(ins):
                n[0] += 1
                ins.then_inc(setup, 1)
                v.wait_ge(setup, n[0])

            for a, pad in enumerate((int(NO_NODE), 0, 0)):
                v.memset(rows_i[:, a, FULL, :], pad).then_inc(pads_set, 1)
            v.memset(zeros, 0.0).then_inc(pads_set, 1)
            v.memset(xT_sb[:, :, N:NP_], 0.0).then_inc(pads_set, 1)
            v.memset(minus_half[:, :], -0.5).then_inc(pads_set, 1)
            v.wait_ge(iotas, 2)
            do(v.tensor_copy(iota_row[:, :], it_i))
            do(v.tensor_copy(part[:, :], pt_i))
            do(v.tensor_copy(iota8[:, :], it_i[:, 0:R]))
            do(v.tensor_scalar(ident[:, :], iota_row[:, :], part[:, 0:1], None, ALU.is_equal))
            do(v.tensor_scalar(before[:, :], iota_row[:, :], part[:, 0:1], None, ALU.is_lt))
            do(v.tensor_scalar(ki[:, 0:1], pt_i, CHUNKS - 1, None, ALU.bitwise_and))
            do(v.tensor_scalar(kt[:, 0:1], pt_i, 4, None, ALU.logical_shift_right))
            do(v.tensor_copy(kh[:, 0:1], ki[:, 0:1]))
            do(v.tensor_copy(kh[:, 1:2], kt[:, 0:1]))
            do(v.scalar_tensor_tensor(out=kh[:, 2:3], in0=kh[:, 0:1], scalar=float(LEN), in1=kh[:, 1:2],
                                      op0=ALU.mult, op1=ALU.add))
            for b in range(BLK):
                last = v.tensor_scalar(kf[:, b:b + 1], kh[:, 2:3], float(P // CHUNKS * b), None, ALU.add)
            do(last)
            v.wait_ge(edges_in, 16 * 9)
            for a in range(3):
                last = v.tensor_copy(rows_f[:, :, a * P:(a + 1) * P], rows_i[:, a, :, :])
            do(last)
            do(v.scalar_tensor_tensor(out=rows_f[:, :, 3 * P:4 * P], in0=rows_f[:, :, P:2 * P], scalar=float(R),
                                      in1=rows_f[:, :, 2 * P:3 * P], op0=ALU.mult, op1=ALU.add))
            SU["rows"] = n[0]
            do(v.tensor_scalar(jfi[:, 0:BLK], rows_i[:, 0, :, 0], 7, None, ALU.logical_shift_right))
            do(v.tensor_copy(cf[:, 0:BLK], jfi[:, 0:BLK]))
            for b in range(BLK):
                last = v.tensor_scalar(cf[:, b:b + 1], cf[:, b:b + 1], part[:, 0:1], float(P * b), ALU.add, ALU.add)
            do(last)
            SU["firsts"] = n[0]
            v.wait_ge(firsts_made, 1)
            do(v.tensor_copy(firsts, ps[:, 4:6, :].rearrange("p a n -> p (a n)")[:, 0:KP]))
            for b in range(BLK):
                do(v.tensor_scalar(cmp[:, 1:ET], firsts[:, 1:ET], kf[:, b:b + 1], None, ALU.is_le))
                do(v.tensor_reduce(i_f[:, b:b + 1], cmp[:, 1:ET], X, ALU.add))
            do(v.tensor_tensor(j_f[:, 0:BLK], kf[:, 0:BLK], i_f[:, 0:BLK], ALU.subtract))
            do(v.tensor_scalar(j128[:, 0:BLK], j_f[:, 0:BLK], float(P), None, ALU.mult))
            do(v.tensor_copy(i_i[:, 0:BLK], i_f[:, 0:BLK]))
            do(v.tensor_copy(j_i[:, 0:BLK], j_f[:, 0:BLK]))
            SU["tiles"] = n[0]
            v.wait_ge(weights_in, 48)
            do(v.memset(blk, 0.0))
            for h in range(H // DC):
                do(v.tensor_scalar(hsel[:, h:h + 1], part[:, 0:1], float(HD * h), None, ALU.is_ge))
                do(v.tensor_scalar(tmp4[:, h:h + 1], part[:, 0:1], float(HD * (h + 1)), None, ALU.is_lt))
            do(v.tensor_tensor(hsel[:, 0:4], hsel[:, 0:4], tmp4[:, 0:4], ALU.mult))
            for c in range(DC):
                for a in range(2):
                    last = v.tensor_scalar(blk[:, c, a * H + 4 * c:a * H + 4 * c + 4], hsel[:, 0:4],
                                           acol[:, a, c:c + 1], None, ALU.mult)
            do(last)
            SU["blk"] = n[0]
            v.wait_ge(step_rows, 16 * BLK)
            for b in range(BLK):
                last = v.tensor_scalar(step_local[:, b, :], step_f[:, b, 0:P], j128[:, b:b + 1], None, ALU.subtract)
            do(last)
            SU["local"] = n[0]
            do(v.tensor_copy(step16[:, :, 0, :], step_f[:, :, P:2 * P]))
            do(v.tensor_copy(step16[:, :, 1, :], step_local))
            SU["step16"] = n[0]
            for b in range(BLK):
                v.wait_ge(tables_ps, b + 1)
                v.tensor_copy(local_t[:, b * P:b * P + P], ps[:, 2 * (b % 2) + 1, 0:P]).then_inc(local_out, 1)
            v.wait_ge(tables_out, BLK)
            v.wait_ge(local_out, BLK)
            do(v.tensor_scalar(mask_t[:, :], local_t[:, :], 0.0, None, ALU.is_ge))
            do(v.scalar_tensor_tensor(out=mask_t[:, :], in0=local_t[:, :], scalar=float(P), in1=mask_t[:, :],
                                      op0=ALU.is_lt, op1=ALU.mult))
            do(v.tensor_scalar(mask_t[:, :], mask_t[:, :], BIG, -BIG, ALU.mult, ALU.add))
            do(v.tensor_scalar(part[:, :], part[:, :], float(N), None, ALU.add))
            do(v.tensor_scalar(trash_t, src_t, -1.0, part[:, 0:1], ALU.mult, ALU.add))
            do(v.tensor_scalar(part[:, :], part[:, :], float(-N), None, ALU.add))
            v.wait_ge(wab_ps, 1)
            wps = ps[:, 6, 0:DC * 2 * RH].rearrange("p (c r a h) -> p c r a h", c=DC, r=R, a=2)
            for c in range(DC):
                v.tensor_copy(wab[:, c, 0:RH].rearrange("p (r h) -> p r h", r=R), wps[:, c, :, 0, :])
                last = v.tensor_copy(wab[:, c, RH:2 * RH].rearrange("p (h r) -> p r h", r=R), wps[:, c, :, 1, :])
            do(last)
            SU["end"] = n[0]

            v.wait_ge(rows_stored, 16)
            v.memset(nodes[:, N // P * D:NT * D], 0.0).then_inc(nodes_padded, 1)

            v.wait_ge(wab_ps, 1)
            v.wait_ge(steps_stored, 32)
            v.wait_ge(y_x, NT)
            v.sem_inc(eq_used, 2)

            def match_sources(it):
                for q in range(4):
                    h, g, k = q % 2, 4 * it + q, 16 * it + 4 * q
                    v.wait_ge(counts_made, g + 1)
                    v.tensor_tensor(onehot[h], iota_row[:, :].unsqueeze(1).to_broadcast([P, 4, P]),
                                    local_t[:, ds(k, 4)].unsqueeze(2).to_broadcast([P, 4, P]), ALU.is_equal)
                    v.wait_ge(row_in[h], 16 * (2 * it + q // 2 + 1))
                    for u in range(4):
                        last = v.tensor_scalar(eq[h][:, u, :], row16[h][:, u, :], src_t[:, ds(k + u, 1)],
                                               None, ALU.is_equal)
                    last.then_inc(onehots, 1)
                    v.wait_ge(onehots, g + 1)
                    for u in range(4):
                        last = v.tensor_tensor_reduce(out=eqj[:, u, :], in0=eq[h][:, u, :], in1=before[:, :], scale=1.0,
                                                      scalar=0.0, op0=ALU.mult, op1=ALU.add,
                                                      accum_out=dup[:, 4 * h + u:4 * h + u + 1])
                    last.then_inc(eq_used, 1)
                    v.wait_ge(eq_used, g + 3)
                    v.scalar_tensor_tensor(out=dup2[:, 4 * h:4 * h + 4], in0=dup[:, 4 * h:4 * h + 4], scalar=1.0,
                                           in1=trash_t[:, ds(k, 4)], op0=ALU.min,
                                           op1=ALU.mult).then_inc(dup_scaled, 1)
                    v.wait_ge(dup_scaled, g + 1)
                    rows_left(v, h, 2 * it + q // 2 - 1)
                    v.tensor_tensor(idx_slot[:, 4 * q:4 * q + 4], dup2[:, 4 * h:4 * h + 4],
                                    src_t[:, ds(k, 4)], ALU.add).then_inc(slots_ready, 1)

            match_sources(0)
            with v.Fori(1, ITS) as it:
                match_sources(it)

            v.wait_ge(sums_copied, NQ + 2)
            v.wait_ge(x_in, 32)
            for h in range(2):
                rows_left(v, h, 2 * ITS)
            v.sem_inc(parts_used, 2)
            v.sem_inc(x0_used, 2)

            v.sem_inc(xn_made, 4)

            def normalise(it, par):
                v.wait_ge(rstd_made, it + 1)
                for h in range(2):
                    v.wait_ge(xt_ps, 2 * it + h + 1)
                    v.wait_ge(x1_kept, 2 * it + h + 1)
                    v.tensor_scalar(xn[h], tmp[par][:, h, :], moments[par][:, h, 0:1], rstd[par][:, h:h + 1],
                                    ALU.subtract, ALU.mult).then_inc(xn_made, 1)

            def node_sums(it, par, turns):
                x1, sums_of = tmp[par], parts[par]
                v.wait_ge(parts_in[par], 16 * NACC * (turns + 1))
                v.wait_ge(xn_made, 2 * it + 2)
                v.tensor_tensor(x1, sums_of[:, 0, :, :], sums_of[:, 1, :, :], ALU.add).then_inc(halves_made, 1)
                if not (isinstance(it, int) and it == 0):
                    normalise(it - 1, 1 - par)
                v.wait_ge(halves_made, it + 1)
                v.wait_ge(pooled, it + 1)
                v.tensor_tensor(x1, x1, sums_of[:, 2, :, :], ALU.add).then_inc(parts_used, 1)
                v.wait_ge(x0_ps, it + 3)
                v.wait_ge(parts_used, it + 3)
                v.tensor_tensor(x1, ps[:, par, :].rearrange("p (t n) -> p t n", t=2), x1, ALU.add).then_inc(x0_used, 1)
                v.wait_ge(x0_used, it + 3)
                v.scalar_tensor_tensor(out=x1, in0=x1, scalar=0.0,
                                       in1=nodes[:, ds(2 * it * D, 2 * D)].rearrange("p (t n) -> p t n", t=2),
                                       op0=ALU.max, op1=ALU.add).then_inc(relu_made, 1)
                v.wait_ge(relu_made, it + 1)
                for h in range(2):
                    v.bn_stats(stats[h][:, :], x1[:, h, :]).then_inc(stats_made, 1)
                for h in range(2):
                    v.wait_ge(stats_made, 2 * it + h + 1)
                    v.sem_inc(stats_seen, 1)
                    v.bn_aggr(moments[par][:, h, :], stats[h][:, :]).then_inc(aggr_made, 1)
                v.wait_ge(aggr_made, 2 * it + 2)
                v.tensor_scalar(veps[par][:, :], moments[par][:, :, 1], LN_EPS, None, ALU.add).then_inc(veps_made, 1)

            node_sums(0, 0, 0)
            in_pairs(v, 1, ITN, node_sums)
            normalise(ITN - 1, (ITN - 1) % 2)

            v.wait_ge(tabs_in, 16)
            v.wait_ge(x1_kept, NT + 2)
            v.memset(run, 0.0)
            v.memset(lead, 1.0)
            v.memset(lmax, 0.0).then_inc(keep_made, 1)
            v.wait_ge(first_turned, 1)
            v.tensor_copy(d_first, ps[:, 5, 0:1])
            v.tensor_copy(d_row[:, 0:1], ps[:, 5, 0:1]).then_inc(first_out, 1)
            v.sem_inc(st_built, 2)
            v.sem_inc(scored, 4)
            v.sem_inc(blocks_done, 1)

            def compare(b, q):
                h = q % 2
                v.wait_ge(drow_in[h], 16 * (2 * b + q // 2 + 1))
                v.wait_ge(b_made, 4 * b + q + 1)
                for u in range(4):
                    last = v.tensor_scalar(st[h][:, u, :], row16[h][:, u, :], part[:, 0:1], None, ALU.is_equal)
                last.then_inc(st_built, 1)

            def score(b, par, q):
                g, h, k = 4 * b + q, q % 2, 16 * b + 4 * q
                v.tensor_tensor(tmask, type_t[:, ds(k, 4)].unsqueeze(2).to_broadcast([P, 4, R]),
                                iota8[:, :].unsqueeze(1).to_broadcast([P, 4, R]), ALU.is_equal).then_inc(mask_made, 1)
                v.wait_ge(mask_made, g + 1)
                v.wait_ge(b_made, g + 3)
                v.tensor_tensor(prod, ps[:, h, 0:4 * RH].rearrange("p (u h r) -> p u h r", u=4, h=H),
                                tmask.unsqueeze(2).to_broadcast([P, 4, H, R]), ALU.mult).then_inc(prod_made, 1)
                v.wait_ge(prod_made, g + 1)
                v.tensor_reduce(bsel, prod, X, ALU.add).then_inc(bsel_made, 1)
                v.wait_ge(bsel_made, g + 1)
                for u in range(4):
                    v.wait_ge(gath[4 * q + u], 16 * (b + 1))
                v.tensor_tensor(zt, a_slot[:, 4 * q:4 * q + 4, :], bsel, ALU.add).then_inc(z_made, 1)
                v.wait_ge(z_made, g + 1)
                v.scalar_tensor_tensor(out=zl, in0=zt, scalar=SLOPE, in1=zt, op0=ALU.mult,
                                       op1=ALU.max).then_inc(z_sloped, 1)
                v.wait_ge(z_sloped, g + 1)
                if q == 0:
                    v.wait_ge(turned, b + 1)
                v.tensor_tensor(zblock[par][:, 4 * q:4 * q + 4, :], zl,
                                mask_t[:, ds(k, 4)].unsqueeze(2).to_broadcast([P, 4, H]),
                                ALU.add).then_inc(scored, 1)

            def scan_block(b):
                at = ds(b * P, P)
                v.wait_ge(block_out, b + 2)
                v.tensor_tensor(keep[:, at], d_row[:, 1:P + 1], d_row[:, 0:P], ALU.is_equal).then_inc(keep_made, 1)
                v.wait_ge(keep_made, b + 2)
                v.tensor_tensor_scan(run, keep[:, at], s_row, run[:, P - 1:P], ALU.mult, ALU.max).then_inc(run_made, 1)
                v.tensor_tensor_scan(lead, keep[:, at], keep[:, at], lead[:, P - 1:P], ALU.mult,
                                     ALU.mult).then_inc(lead_made, 1)
                v.tensor_copy(d_row[:, 0:1], d_row[:, P:P + 1])
                v.wait_ge(lead_made, b + 1)
                v.tensor_tensor(led, lead, s_row, ALU.mult).then_inc(led_made, 1)
                v.wait_ge(led_made, b + 1)
                v.tensor_reduce(lmax[:, 1:2], led, X, ALU.max).then_inc(lmax_made, 1)
                v.wait_ge(lmax_made, b + 1)
                v.wait_ge(run_made, b + 1)
                v.tensor_tensor(lmax[:, 0:1], lmax[:, 0:1], lmax[:, 1:2], ALU.max).then_inc(blocks_done, 1)

            def score_block(b, par, turn):
                for q in range(4):
                    compare(b + (q + 1) // 4, (q + 1) % 4)
                    score(b, par, q)
                    if q == 1 and not (isinstance(b, int) and b == 0):
                        scan_block(b - 1)
                        v.wait_ge(blocks_done, b + 1)

            v.wait_ge(keep_made, 1)
            v.wait_ge(first_out, 1)
            compare(0, 0)
            score_block(0, 0, 0)
            in_pairs(v, 1, ITS, score_block)
            scan_block(ITS - 1)
            v.wait_ge(blocks_done, ITS + 1)

            v.memset(d_prev, -1.0)
            v.memset(d_next, -1.0).then_inc(ends_made, 1)
            v.wait_ge(borders_in, 32)
            v.tensor_tensor(k_first[:, 0:1], d_first, d_prev, ALU.is_equal)
            v.tensor_tensor(k_first[:, 1:2], d_row[:, 0:1], d_next, ALU.is_equal).then_inc(ends_made, 1)
            v.wait_ge(ends_made, 2)
            v.tensor_copy(keep[:, 0:1], k_first[:, 0:1])
            v.tensor_copy(keep[:, SCAN:SCAN + 1], k_first[:, 1:2])
            v.tensor_copy(ends[:, 0:1], run[:, P - 1:P])
            v.tensor_copy(ends[:, 2:3], lmax[:, 0:1])
            v.tensor_tensor(ends[:, 1:2], lead[:, P - 1:P], k_first[:, 0:1], ALU.mult)
            v.tensor_tensor(ends[:, 3:4], lead[:, P - 1:P], k_first[:, 1:2], ALU.mult).then_inc(ends_made, 1)
            v.memset(cres[0:H, 0, 0:1], 0.0)
            v.memset(cres[0:H, 1, CHUNKS:CHUNKS + 1], 0.0)
            v.wait_ge(ends_io, 32)
            v.tensor_tensor_scan(cres[0:H, 0, 1:CHUNKS + 1], crow[0:H, :, 1], crow[0:H, :, 0], 0.0, ALU.mult, ALU.max)
            v.tensor_tensor_scan(cres[0:H, 1, 0:CHUNKS][:, ::-1], crow[0:H, :, 3][:, ::-1], crow[0:H, :, 2][:, ::-1],
                                 0.0, ALU.mult, ALU.max).then_inc(ends_made, 1)
            v.wait_ge(carry_io, 48)
            for q in range(4):
                v.wait_ge(h_stored[q], 16 * (NT + 1))
            v.tensor_tensor_scan(fwd, keep[:, 0:SCAN], s_T, carry[:, 0:1], ALU.mult, ALU.max).then_inc(shifted, 1)
            v.wait_ge(shifted, 1)
            v.tensor_tensor_scan(fwd[:, ::-1], keep[:, 1:SCAN + 1][:, ::-1], fwd[:, ::-1], carry[:, 1:2],
                                 ALU.mult, ALU.max).then_inc(shifted, 1)
            v.wait_ge(shifted, 2)
            v.tensor_tensor(s_T, s_T, fwd, ALU.subtract).then_inc(shifted, 1)
            v.wait_ge(shifted, 3)

            v.memset(acc[:, 0:SCAN], 0.0).then_inc(acc_zero, 1)
            v.wait_ge(acc_zero, 2)
            def add_sums(g, tile):
                for u in range(4):
                    v.wait_ge(segs, 4 * g + u + 9)
                    v.wait_ge(added, 4 * g + u + 4)
                    v.tensor_tensor(acc[:, ds(tile[u] * AW, AW)], ps[:, u, 0:AW], acc[:, ds(tile[u] * AW, AW)],
                                    ALU.add).then_inc(added, 1)

            def weigh(it, q):
                h = q % 2
                v.tensor_tensor(sel[:, 4 * h:4 * h + 4, :], iota_row[:, :].unsqueeze(1).to_broadcast([P, 4, P]),
                                local_t[:, ds(16 * it + 4 * q, 4)].unsqueeze(2).to_broadcast([P, 4, P]), ALU.is_equal)
                if q == 0:
                    v.wait_ge(w_ready, it + 1)
                for u in range(4):
                    v.wait_ge(gath[4 * q + u], 16 * (ITS + it + 1))
                v.tensor_tensor(msg[:, 4 * h:4 * h + 4, 0:D].rearrange("p u (h d) -> p u h d", h=H),
                                h_slot[:, 4 * q:4 * q + 4, :].rearrange("p u (h d) -> p u h d", h=H),
                                w_col[:, 4 * q:4 * q + 4, :].unsqueeze(3).to_broadcast([P, 4, H, HD]),
                                ALU.mult).then_inc(msgs, 1)

            v.sem_inc(added, 4)
            tile = read_tiles(v, 0, 12)
            for q in range(4):
                weigh(0, q)
                if q:
                    add_sums(q - 1, tile[4 * q - 4:4 * q])
            with v.Fori(1, ITS) as it:
                tile = read_tiles(v, 16 * it - 4, 16)
                for q in range(4):
                    weigh(it, q)
                    add_sums(4 * it + q - 1, tile[4 * q:4 * q + 4])
            add_sums(NQ - 1, read_tiles(v, STEPS - 4, 4))
            v.wait_ge(added, STEPS + 4)

            for h in range(2):
                v.sem_inc(stored[h], 16)

            v.sem_inc(fin_made, 4)

            def finish(it, par):
                v.wait_ge(frstd_made, it + 1)
                for h in range(2):
                    v.wait_ge(stored[h], 16 * (it + 1))
                    v.tensor_scalar(fin[h], res[par][:, h, :], moments[par][:, h, 0:1], rstd[par][:, h:h + 1],
                                    ALU.subtract, ALU.mult).then_inc(fin_made, 1)

            def residual_sums(it, par, turns):
                x2 = res[par]
                two = acc[:, ds(2 * it * AW, 2 * AW)].rearrange("p (t n) -> p t n", t=2)
                v.tensor_scalar(den[:, 0, :, :], two[:, :, D:AW], DEN_EPS, None, ALU.add).then_inc(den_made, 1)
                v.wait_ge(den_made, it + 1)
                v.reciprocal(den[:, 1, :, :], den[:, 0, :, :]).then_inc(rden_made, 1)
                v.wait_ge(rden_made, it + 1)
                v.wait_ge(fin_made, 2 * it + 2)
                v.tensor_tensor(x2.rearrange("p t (h d) -> p t h d", h=H),
                                two[:, :, 0:D].rearrange("p t (h d) -> p t h d", h=H),
                                den[:, 1, :, :].unsqueeze(3).to_broadcast([P, 2, H, HD]), ALU.mult).then_inc(res_made, 1)
                if not (isinstance(it, int) and it == 0):
                    finish(it - 1, 1 - par)
                v.wait_ge(res_made, it + 1)
                v.tensor_tensor(x2, x2, nodes[:, ds(2 * it * D, 2 * D)].rearrange("p (t n) -> p t n", t=2),
                                ALU.add).then_inc(sum_made, 1)
                v.wait_ge(sum_made, it + 1)
                for h in range(2):
                    v.bn_stats(stats[h][:, :], x2[:, h, :]).then_inc(fstats_made, 1)
                for h in range(2):
                    v.wait_ge(fstats_made, 2 * it + h + 1)
                    v.sem_inc(fstats_seen, 1)
                    v.bn_aggr(moments[par][:, h, :], stats[h][:, :]).then_inc(faggr_made, 1)
                v.wait_ge(faggr_made, 2 * it + 2)
                v.tensor_scalar(veps[par][:, :], moments[par][:, :, 1], LN_EPS, None, ALU.add).then_inc(fveps_made, 1)

            residual_sums(0, 0, 0)
            in_pairs(v, 1, ITN, residual_sums)
            finish(ITN - 1, (ITN - 1) % 2)

        @block.sync
        def _(sp):
            sp.wait_ge(pads_set, 3)
            for a, arr in enumerate((dst, src, etype)):
                sp.dma_start(rows_i[:, a, 0:FULL, :],
                             arr[0:FULL * P * P].rearrange("(b p e) -> p b e", p=P, e=P)).then_inc(edges_in, 16)
                sp.dma_start(rows_i[0:REST, a, FULL, :],
                             arr[FULL * P * P:(ET - 1) * P].rearrange("(p e) -> p e", e=P)).then_inc(edges_in, 16)
                sp.dma_start(rows_i[REST:REST + 1, a, FULL, 0:TAIL],
                             arr[(ET - 1) * P:E].rearrange("(p e) -> p e", p=1)).then_inc(edges_in, 16)
            sp.dma_start(w1_sb, w1.rearrange("(c p) n -> p c n", p=P)).then_inc(wx_in, 16)
            sp.dma_start(w0_sb, w0.rearrange("(c p) n -> p c n", p=P)).then_inc(wx_in, 16)
            sp.dma_start(xT_sb[:, :, 0:N], xT.rearrange("(c p) n -> p c n", p=P)).then_inc(xT_in, 16)
            for a, att in enumerate((attn_src, attn_dst)):
                sp.dma_start(acol[:, a, :], att.rearrange("h d -> (h d)").rearrange("(c p) -> p c", p=P),
                             allow_slow_non_contiguous=True).then_inc(weights_in, 16)
            sp.dma_start(w_nat, W.rearrange("r (c p) f -> p r c f", p=P)).then_inc(weights_in, 16)
            sp.wait_ge(setup, SU["rows"])
            sp.dma_start(edge_rows_d.rearrange("(b p) n -> p b n", p=P), rows_f).then_inc(rows_stored, 16)
            sp.wait_ge(pads_set, 4)

            def zero_sums(u):
                sp.dma_start(sums_d[u].rearrange("(p n) w -> p (n w)", p=P).rearrange("p (a n) -> p a n", n=NZ),
                             zeros.unsqueeze(1).to_broadcast([P, HALF // NZ, NZ])).then_inc(zeroed, 16)

            zero_sums(0)
            sp.wait_ge(setup, SU["tiles"])
            sp.dma_start(step_tile_d.rearrange("(b p) -> p b", p=P), j_i[:, 0:BLK],
                         allow_slow_non_contiguous=True).then_inc(steps_stored, 16)
            sp.wait_ge(step_rows, 16 * BLK)
            zero_sums(1)
            sp.wait_ge(setup, SU["step16"])
            sp.dma_start(step_rows_d.rearrange("(b p) a e -> p b a e", p=P), step16).then_inc(steps_stored, 16)
            sp.wait_ge(steps_stored, 32)
            sp.dma_start(tile_row[:, :], step_tile_d.rearrange("(a k) -> a k", a=1)).then_inc(steps_stored, 16)
            sp.wait_ge(steps_stored, 48)
            for u in range(2, NACC):
                zero_sums(u)

            def source_rows(it):
                for q in range(4):
                    sp.wait_ge(eq_used, 4 * it + q + 1)
                    sp.dma_start(row16[q % 2][:, :, :],
                                 step_rows_d[ds(16 * it + 4 * q, 4), 0, :].partition_broadcast(P)).then_inc(row_in[q % 2], 16)

            source_rows(0)
            sp.wait_ge(setup, SU["end"])
            sp.wait_ge(tables_out, BLK)
            sp.wait_ge(nodes_padded, 1)
            NF = N // P
            sp.dma_start(nodes[:, 0:NF * D].rearrange("p (t w) -> p t w", w=D),
                         x[0:NF * P, :].rearrange("(t p) w -> p t w", p=P)).then_inc(x_in, 16)
            sp.dma_start(nodes[0:N - NF * P, NF * D:(NF + 1) * D], x[NF * P:N, :]).then_inc(x_in, 16)
            with sp.Fori(1, ITS) as it:
                source_rows(it)

            for h in range(2):
                rows_left(sp, h, 2 * ITS)

            def load_nodes(it, par, turns):
                sp.wait_ge(parts_used, it + 1)
                for u in range(NACC):
                    sp.dma_start(parts[par][:, u, :, :], sums_d[u][ds(2 * it * P, 2 * P), :]
                                 .rearrange("(t p) n -> p t n", p=P)).then_inc(parts_in[par], 16)
                sp.wait_ge(x0_ps, it + 1)
                sp.dma_start(x2t[par], xT_sb[:, :, ds(2 * it * P, 2 * P)]).then_inc(x0_x[par], 16)

            in_pairs(sp, 0, ITN, load_nodes)

            sp.wait_ge(ab_copied, NT + 2)
            for h in range(2):
                sp.wait_ge(node_out[h], 32 * (ITN + 1))
            sp.dma_start(wT_sb, WT.rearrange("(c p) n -> p c n", p=P)).then_inc(tabs_in, 16)

            def destinations(g, h):
                sp.wait_ge(st_built, g + 1)
                sp.dma_start(row16[h][:, :, :],
                             step_rows_d[ds(4 * g, 4), 1, :].partition_broadcast(P)).then_inc(drow_in[h], 16)

            def with_node_tile(b, par, turn):
                sp.wait_ge(h_made, 4 * b + 4)
                sp.dma_start(x1s[par].rearrange("p c n -> p (c n)"), x1T_d[ds(b * P, P), :]).then_inc(x1s_in[par], 16)
                for q in range(4):
                    destinations(4 * b + q, q % 2)

            in_pairs(sp, 0, NT, with_node_tile)
            with sp.Fori(NT, ITS) as b:
                for q in range(4):
                    destinations(4 * b + q, q % 2)
            destinations(NQ, 0)

            sp.wait_ge(ends_made, 1)
            sp.dma_start(d_prev[H:P, :], d_row[0:P - H, 0:1]).then_inc(borders_in, 16)
            sp.dma_start(d_next[0:P - H, :], d_first[H:P, :]).then_inc(borders_in, 16)
            sp.wait_ge(ends_made, 3)
            sp.dma_start(ends_d, ends).then_inc(ends_io, 16)
            sp.wait_ge(ends_io, 16)
            sp.dma_start(crow[0:H, :, :], ends_d.rearrange("(c h) f -> h c f", h=H)).then_inc(ends_io, 16)
            sp.wait_ge(ends_made, 4)
            for a in range(2):
                sp.dma_start(carry_d.rearrange("(c h) f -> h f c", h=H)[:, a, :],
                             cres[0:H, a, a:a + CHUNKS], allow_slow_non_contiguous=True).then_inc(carry_io, 16)
            sp.wait_ge(carry_io, 32)
            sp.dma_start(carry, carry_d).then_inc(carry_io, 16)

            with sp.Fori(0, (NT - 2) // 2) as it:
                for h in range(2):
                    sp.wait_ge(fin_made, 2 * it + h + 5)
                    sp.dma_start(out[ds((2 * it + h) * P, P), :], fin[h]).then_inc(stored[h], 16)
            sp.wait_ge(fin_made, NT - 2 + 5)
            sp.dma_start(out[(NT - 2) * P:N, :], fin[0][0:N - (NT - 2) * P, :]).then_inc(stored[0], 16)
            sp.wait_ge(stored[0], 16 * ((NT - 2) // 2 + 2))
            sp.wait_ge(stored[1], 16 * ((NT - 2) // 2 + 1))

        @block.gpsimd
        def _(g):
            g.iota(it_i, [[1, P]], base=0, channel_multiplier=0).then_inc(iotas, 1)
            g.iota(pt_i, [[0, 1]], base=0, channel_multiplier=1).then_inc(iotas, 1)
            g.wait_ge(setup, SU["tiles"])
            g.wait_ge(rows_stored, 16)
            for b in range(BLK):
                g.indirect_dma_start(step_f[:, b, :], None, edge_rows_d,
                                     bass.IndirectOffsetOnAxis(ap=i_i[:, b:b + 1], axis=0),
                                     bounds_check=KP - 1, oob_is_err=True).then_inc(step_rows, 16)
            node_bound = g.snap(g.to_reg(NP_ - 1))
            row_bound = g.snap(g.to_reg(NP_ * R - 1))

            def scatter(it):
                for q in range(4):
                    h = q % 2
                    g.wait_ge(sums_copied, 4 * it + q + 3)
                    g.wait_ge(slots_ready, 4 * it + q + 1)
                    for u in range(4):
                        if not isinstance(it, int) or q:
                            g.wait_ge(scattered[1 - h][u], 16 * (2 * it + (q + 1) // 2))
                        g.sem_inc(pool_turns, 1)
                        g.indirect_dma_start(sums_d[u],
                                             bass.IndirectOffsetOnAxis(ap=idx_slot[:, 4 * q + u:4 * q + u + 1], axis=0),
                                             sums[h][:, u, :], None, bounds_check=node_bound, oob_is_err=True,
                                             compute_op=ALU.add).then_inc(scattered[h][u], 16)

            g.wait_ge(zeroed, 16 * NACC)
            scatter(0)
            with g.Fori(1, ITS) as it:
                scatter(it)


            def add_parts(it, par, turns):
                two = parts[par][:, 2:4, :, :]
                g.wait_ge(parts_in[par], 16 * NACC * (turns + 1))
                g.tensor_tensor(two[:, 0, :, :], two[:, 0, :, :], two[:, 1, :, :], ALU.add).then_inc(pooled, 1)

            def inverse_deviation(it, par):
                g.wait_ge(veps_made, it + 1)
                g.tensor_tensor(rstd[par][:, :], veps[par][:, :], minus_half[:, :], ALU.pow).then_inc(rstd_made, 1)

            def add_and_invert(it, par, turns):
                add_parts(it, par, turns)
                inverse_deviation(it - 1, 1 - par)

            add_parts(0, 0, 0)
            in_pairs(g, 1, ITN, add_and_invert)
            inverse_deviation(ITN - 1, (ITN - 1) % 2)

            for h in range(2):
                g.wait_ge(node_out[h], 32 * (ITN + 1))
            a_rows = a_d.rearrange("n (r h) -> (n r) h", h=H)
            with g.Fori(0, ITS) as it:
                for q in range(4):
                    g.wait_ge(idx_ready, 4 * it + q + 1)
                    g.sem_inc(pool_turns, 1)
                    for u in range(4):
                        k = 4 * q + u
                        g.indirect_dma_start(a_slot[:, k, :], None, a_rows,
                                             bass.IndirectOffsetOnAxis(ap=idx_slot[:, k:k + 1], axis=0),
                                             bounds_check=row_bound, oob_is_err=True).then_inc(gath[k], 16)

            for q in range(4):
                g.wait_ge(h_stored[q], 16 * (NT + 1))
            h_rows = h_d.rearrange("n (r w) -> (n r) w", w=D)

            def gather_features(it):
                for q in range(4):
                    g.wait_ge(idx_ready, NQ + 4 + 4 * it + q + 1)
                    g.sem_inc(pool_turns, 1)
                    for u in range(4):
                        k = 4 * q + u
                        g.indirect_dma_start(h_slot[:, k, :], None, h_rows,
                                             bass.IndirectOffsetOnAxis(ap=idx_slot[:, k:k + 1], axis=0),
                                             bounds_check=row_bound, oob_is_err=True).then_inc(gath[k], 16)

            gather_features(0)
            g.wait_ge(shifted, 2)
            g.memset(acc[:, SCAN:NT * AW], 0.0).then_inc(acc_zero, 1)
            with g.Fori(1, ITS) as it:
                gather_features(it)


            def finish(it, par, turns):
                g.wait_ge(fveps_made, it + 1)
                g.tensor_tensor(rstd[par][:, :], veps[par][:, :], minus_half[:, :], ALU.pow).then_inc(frstd_made, 1)

            in_pairs(g, 0, ITN, finish)

        @block.scalar
        def _(a):
            a.wait_ge(xT_in, 16)
            a.wait_ge(pads_set, 6)
            a.sem_inc(y_done, 2)

            def copy_x(it):
                for h in range(2):
                    a.wait_ge(y_ps, 2 * it + h + 1)
                    a.copy(xs0[h], xT_sb[:, :, ds((2 * it + h) * P, P)]).then_inc(y_x, 1)

            def copy_y(it):
                for h in range(2):
                    a.wait_ge(y_ps, 2 * it + h + 3)
                    a.copy(y_sb[:, ds((2 * it + h) * D, D)], ps[:, h, 0:D]).then_inc(y_done, 1)

            copy_x(0)
            with a.Fori(0, SPLIT) as it:
                copy_x(it + 1)
                copy_y(it)
            a.wait_ge(wab_ps, 1)
            with a.Fori(SPLIT, ITN - 1) as it:
                copy_x(it + 1)
                copy_y(it)
            copy_y(ITN - 1)
            for b in range(BLK):
                a.wait_ge(tables_ps, b + 1)
                bank = ps[:, 2 * (b % 2):2 * (b % 2) + 2, :].rearrange("p a n -> p (a n)")
                cols = slice(b * P, b * P + P)
                for n, t in ((0, dst_t), (2, type_t), (3, idx_t)):
                    a.copy(t[:, cols], bank[:, n * P:n * P + P])
                a.copy(src_t[:, cols], bank[:, P:2 * P]).then_inc(tables_out, 1)

            a.sem_inc(counts_copied, 2)
            a.sem_inc(sums_copied, 2)

            def copy_sums(it, q):
                h = q % 2
                a.wait_ge(sums_made, 4 * it + q + 3)
                rows_left(a, h, 2 * it + q // 2)
                a.copy(sums[h][:, :, :],
                       ps[:, 2 + 2 * h:4 + 2 * h, :].rearrange("p b (u n) -> p (b u) n", u=2)).then_inc(sums_copied, 1)

            def evacuate(it):
                for q in range(4):
                    a.wait_ge(counts_made, 4 * it + q + 3)
                    a.wait_ge(sums_made, 4 * it + q + 1)
                    a.copy(counts[q % 2], ps[:, q % 2, :].rearrange("p (u e) -> p u e", u=4)).then_inc(counts_copied, 1)
                    if q:
                        copy_sums(it, q - 1)
                copy_sums(it, 3)

            a.wait_ge(zeroed, 16 * NACC)
            evacuate(0)
            with a.Fori(1, ITS) as it:
                evacuate(it)

            for h in range(2):
                rows_left(a, h, 2 * ITS)
            a.sem_inc(ab_copied, 2)
            a.sem_inc(x1_kept, 2)
            for h in range(2):
                a.sem_inc(node_out[h], 32)

            def copy_nodes(it):
                for h in range(2):
                    a.wait_ge(xn_made, 2 * it + h + 5)
                    a.copy(nodes[:, ds((2 * it + h) * D, D)], xn[h]).then_inc(x1_kept, 1)
                for h in range(2):
                    a.wait_ge(xt_ps, 2 * it + h + 3)
                    a.wait_ge(ab_ps, 2 * it + h + 1)
                    a.wait_ge(node_out[h], 32 * (it + 1))
                    a.copy(xts[h], ps[:, 2 + h, 0:DC * P].rearrange("p (c n) -> p c n", c=DC)).then_inc(xts_made, 1)
                for h in range(2):
                    rows = ds((2 * it + h) * P, P)
                    a.wait_ge(xts_made, 2 * it + h + 1)
                    a.dma_start(x1T_d[rows, :], xts[h].rearrange("p c n -> p (c n)")).then_inc(node_out[h], 16)
                    a.wait_ge(ab_ps, 2 * it + h + 3)
                    a.copy(b_sb[:, ds((2 * it + h) * RH, RH)], ps[:, 4 + h, RH:2 * RH])
                    a.copy(a_out[h], ps[:, 4 + h, 0:RH]).then_inc(ab_copied, 1)
                for h in range(2):
                    a.wait_ge(ab_copied, 2 * it + h + 3)
                    a.dma_start(a_d[ds((2 * it + h) * P, P), :], a_out[h]).then_inc(node_out[h], 16)

            with a.Fori(0, ITN) as it:
                copy_nodes(it)

            for h in range(2):
                a.wait_ge(node_out[h], 32 * (ITN + 1))
            a.wait_ge(tabs_in, 16)
            a.sem_inc(h_copied, 2)
            a.sem_inc(block_out, 1)
            for q in range(4):
                a.sem_inc(h_stored[q], 16)

            def indices(it, q):
                a.copy(idx_slot[:, 4 * q:4 * q + 4], idx_t[:, ds(16 * it + 4 * q, 4)]).then_inc(idx_ready, 1)

            def destinations(b):
                a.copy(dblock, dst_t[:, ds(b * CHUNKS, CHUNKS)].unsqueeze(2)
                       .to_broadcast([P, CHUNKS, H])).then_inc(dblock_made, 1)

            def copy_block(b):
                a.wait_ge(turned, b + 3)
                a.wait_ge(blocks_done, b + 1)
                a.copy(s_row, ps[:, 4, 0:P])
                a.copy(d_row[:, 1:P + 1], ps[:, 4, P:2 * P])
                a.copy(s_T[:, ds(b * P, P)], ps[:, 4, 0:P]).then_inc(block_out, 1)

            for q in range(4):
                indices(0, q)
            destinations(0)
            a.wait_ge(first_out, 1)

            def copy_tables(b, with_h):
                for q in range(4):
                    if with_h:
                        a.wait_ge(h_made, 4 * b + q + 9)
                        a.wait_ge(h_stored[q], 16 * (b + 1))
                        a.copy(h_out[:, q, :], ps[:, 2 + q % 2, :]).then_inc(h_copied, 1)
                        a.wait_ge(h_copied, 4 * b + q + 3)
                        a.dma_start(h_d[ds(b * P, P), 512 * q:512 * q + 512], h_out[:, q, :]).then_inc(h_stored[q], 16)
                    if q == 0 and not (isinstance(b, int) and b == 0):
                        copy_block(b - 1)
                        destinations(b)
                    a.wait_ge(scored, 4 * b + q + 5)
                    indices(b + 1, q)

            copy_tables(0, True)
            with a.Fori(1, NT) as b:
                copy_tables(b, True)
            with a.Fori(NT, ITS) as b:
                copy_tables(b, False)
            copy_block(ITS - 1)

            for q in range(4):
                a.wait_ge(h_stored[q], 16 * (NT + 1))
            a.wait_ge(idx_ready, NQ + 4)
            for q in range(4):
                indices(0, q)
            a.wait_ge(shifted, 3)

            def exponentials(it):
                a.activation(e_row, s_T[:, ds(it * P, P)], ACT.Exp).then_inc(exps, 1)

            def weights(it):
                a.wait_ge(w_turned, it + 1)
                a.copy(w_col.rearrange("p k h -> p (k h)"), ps[:, 4, 0:P]).then_inc(w_ready, 1)

            def weights_and_indices(it, more):
                for q in range(4):
                    a.wait_ge(segs, 16 * it + 4 * q + 4)
                    if q == 0:
                        a.wait_ge(w_ready, it + 1)
                    a.copy(msg[:, 4 * (q % 2):4 * (q % 2) + 4, D:AW], w_col[:, 4 * q:4 * q + 4, :]).then_inc(w_placed, 1)
                    if more and q == 0:
                        exponentials(it + 1)
                    if more:
                        a.wait_ge(msgs, 4 * it + q + 1)
                        indices(it + 1, q)
                if more:
                    a.wait_ge(w_placed, 4 * it + 4)
                    weights(it + 1)

            exponentials(0)
            weights(0)
            with a.Fori(0, ITS - 1) as it:
                weights_and_indices(it, True)
            weights_and_indices(ITS - 1, False)

        @block.tensor
        def _(t):
            t.wait_ge(setup, SU["firsts"])
            for b in range(BLK):
                mm = t.matmul(ps[:, 4 + b // 4, (b % 4) * P:(b % 4) * P + P], lhsT=cf[:, b:b + 1].to_broadcast([P, P]),
                              rhs=ident[:, :], start=True, stop=True)
            mm.then_inc(firsts_made, 1)
            t.sem_inc(y_ps, 2)
            t.wait_ge(wx_in, 32)

            def y_products(it):
                for h in range(2):
                    t.wait_ge(y_x, 2 * it + h + 1)
                    t.wait_ge(y_done, 2 * it + h + 1)
                    for c in range(DC):
                        mm = t.matmul(ps[:, h, 0:D], lhsT=xs0[h][:, c, :], rhs=w1_sb[:, c, :],
                                      start=(c == 0), stop=(c == DC - 1))
                    mm.then_inc(y_ps, 1)

            with t.Fori(0, SPLIT) as it:
                y_products(it)
            t.wait_ge(setup, SU["blk"])
            t.wait_ge(weights_in, 48)
            for fc in range(DC):
                for r in range(R):
                    for c in range(DC):
                        mm = t.matmul(ps[:, 6, fc * 2 * RH + r * 2 * H:fc * 2 * RH + (r + 1) * 2 * H],
                                      lhsT=w_nat[:, r, c, fc * P:(fc + 1) * P], rhs=blk[:, c, :],
                                      start=(c == 0), stop=(c == DC - 1))
            mm.then_inc(wab_ps, 1)
            with t.Fori(SPLIT, ITN) as it:
                y_products(it)
            t.wait_ge(y_done, NT + 2)
            t.wait_ge(setup, SU["local"])
            for b in range(BLK):
                if b >= 2:
                    t.wait_ge(tables_out, b - 1)
                    t.wait_ge(local_out, b - 1)
                for n in range(5):
                    s = step_f[:, b, n * P:(n + 1) * P] if n < 4 else step_local[:, b, :]
                    mm = t.transpose(ps[:, 2 * (b % 2) + n // 4, (n % 4) * P:(n % 4) * P + P], s, ident[:, :])
                mm.then_inc(tables_ps, 1)
            t.wait_ge(tables_out, BLK)
            t.wait_ge(local_out, BLK)

            t.wait_ge(steps_stored, 48)
            t.sem_inc(counts_made, 2)
            t.sem_inc(sums_made, 2)

            def sum_rows(it, q, tile):
                h = q % 2
                t.wait_ge(counts_copied, 4 * it + q + 3)
                t.wait_ge(sums_copied, 4 * it + q + 1)
                for u in range(4):
                    mm = t.matmul(ps[:, 2 + 2 * h + u // 2, (u % 2) * D:(u % 2) * D + D], lhsT=counts[h][:, u, :],
                                  rhs=y_sb[:, ds(tile[4 * q + u] * D, D)], start=True, stop=True)
                mm.then_inc(sums_made, 1)

            with t.Fori(0, ITS) as it:
                tile = read_tiles(t, 16 * it, 16)
                for q in range(4):
                    h = q % 2
                    t.wait_ge(onehots, 4 * it + q + 1)
                    t.wait_ge(counts_copied, 4 * it + q + 1)
                    for u in range(4):
                        mm = t.matmul(ps[:, h, u * P:(u + 1) * P], lhsT=onehot[h][:, u, :], rhs=eq[h][:, u, :],
                                      start=True, stop=True)
                    mm.then_inc(counts_made, 1)
                    if q:
                        sum_rows(it, q - 1, tile)
                sum_rows(it, 3, tile)

            t.wait_ge(sums_copied, NQ + 2)
            t.sem_inc(x0_ps, 2)
            t.sem_inc(xt_ps, 2)
            t.sem_inc(ab_ps, 2)

            def first_product(it, par, turns):
                t.wait_ge(x0_x[par], 16 * (turns + 1))
                t.wait_ge(x0_used, it + 1)
                for h in range(2):
                    for c in range(DC):
                        mm = t.matmul(ps[:, par, h * D:(h + 1) * D], lhsT=x2t[par][:, c, h * P:(h + 1) * P],
                                      rhs=w0_sb[:, c, :], start=(c == 0), stop=(c == DC - 1))
                mm.then_inc(x0_ps, 1)

            def node_products(it):
                for h in range(2):
                    t.wait_ge(xn_made, 2 * it + h + 5)
                    for c in range(DC):
                        mm = t.transpose(ps[:, 2 + h, c * P:(c + 1) * P], xn[h][:, c * P:(c + 1) * P], ident[:, :])
                    mm.then_inc(xt_ps, 1)
                for h in range(2):
                    t.wait_ge(xts_made, 2 * it + h + 1)
                    t.wait_ge(ab_copied, 2 * it + h + 1)
                    for c in range(DC):
                        mm = t.matmul(ps[:, 4 + h, 0:2 * RH], lhsT=xts[h][:, c, :], rhs=wab[:, c, :],
                                      start=(c == 0), stop=(c == DC - 1))
                    mm.then_inc(ab_ps, 1)

            def node_pair(it, par, turns):
                first_product(it, par, turns)
                node_products(it - 1)

            first_product(0, 0, 0)
            in_pairs(t, 1, ITN, node_pair)
            node_products(ITN - 1)

            t.wait_ge(tabs_in, 16)
            t.wait_ge(ab_copied, NT + 2)
            t.wait_ge(dblock_made, 1)
            t.transpose(ps[:, 5, 0:P], dblock.rearrange("p c h -> p (c h)"), ident[:, :]).then_inc(first_turned, 1)
            t.wait_ge(first_out, 1)
            t.sem_inc(b_made, 2)
            t.sem_inc(h_made, 8)
            t.sem_inc(turned, 2)

            def turn(b, par):
                t.wait_ge(scored, 4 * b + 8)
                t.wait_ge(dblock_made, b + 1)
                t.wait_ge(block_out, b + 1)
                t.transpose(ps[:, 4, 0:P], zblock[par].rearrange("p k h -> p (k h)"), ident[:, :])
                t.transpose(ps[:, 4, P:2 * P], dblock.rearrange("p c h -> p (c h)"), ident[:, :]).then_inc(turned, 1)

            def destination_scores(g, h, tile):
                t.wait_ge(st_built, g + 3)
                t.wait_ge(scored, g + 3)
                for u in range(4):
                    mm = t.matmul(ps[:, h, u * RH:(u + 1) * RH], lhsT=st[h][:, u, :],
                                  rhs=b_sb[:, ds(tile[u] * RH, RH)], start=True, stop=True)
                mm.then_inc(b_made, 1)

            def tables(b, par, turns, with_h, last=False):
                tile = read_tiles(t, 16 * b + 4, 12 if last else 16)
                for q in range(4):
                    if q == 0 and not (isinstance(b, int) and b == 0):
                        turn(b - 1, 1 - par)
                    if not (last and q == 3):
                        destination_scores(4 * b + q + 1, (q + 1) % 2, tile[4 * q:4 * q + 4])
                    if with_h:
                        if q == 0:
                            t.wait_ge(x1s_in[par], 16 * (turns + 1))
                        t.wait_ge(h_copied, 4 * b + q + 1)
                        for c in range(DC):
                            mm = t.matmul(ps[:, 2 + q % 2, :], lhsT=x1s[par][:, c, :],
                                          rhs=wT_sb[:, c, 512 * q:512 * q + 512], start=(c == 0), stop=(c == DC - 1))
                        mm.then_inc(h_made, 1)

            destination_scores(0, 0, read_tiles(t, 0, 4))
            tables(0, 0, 0, True)
            in_pairs(t, 1, NT, lambda b, par, turns: tables(b, par, turns, True))
            in_pairs(t, NT, ITS - 1, lambda b, par, turns: tables(b, par, turns, False))
            tables(ITS - 1, (ITS - 1) % 2, 0, False, last=True)
            turn(ITS - 1, (ITS - 1) % 2)

            t.sem_inc(segs, 8)

            def turn_weights(it):
                t.wait_ge(exps, it + 1)
                if not isinstance(it, int):
                    t.wait_ge(w_ready, it)
                t.transpose(ps[:, 4, 0:P], e_row, ident[:, :]).then_inc(w_turned, 1)

            def sum_edges(it, more):
                for q in range(4):
                    t.wait_ge(w_placed, 4 * it + q + 1)
                    t.wait_ge(msgs, 4 * it + q + 1)
                    for u in range(4):
                        k = 4 * (q % 2) + u
                        t.wait_ge(added, 16 * it + 4 * q + u + 1)
                        t.matmul(ps[:, u, 0:AW], lhsT=sel[:, k, :], rhs=msg[:, k, :],
                                 start=True, stop=True).then_inc(segs, 1)
                    if more and q == 1:
                        turn_weights(it + 1)

            turn_weights(0)
            with t.Fori(0, ITS - 1) as it:
                sum_edges(it, True)
            sum_edges(ITS - 1, False)


def kernel(x, src, dst, edge_type_8, L0_gnn_w0, L0_gnn_w1, L1_gnn_W, L1_gnn_attn_src, L1_gnn_attn_dst):
    import numpy as np
    import concourse.bacc as bacc
    from concourse.bass_utils import run_bass_kernel_spmd

    x, W = np.asarray(x), np.asarray(L1_gnn_W)
    n, d = x.shape
    r = W.shape[0]
    arrays = {
        "x": x, "xT": np.ascontiguousarray(x.T),
        "src": np.asarray(src), "dst": np.asarray(dst), "etype": np.asarray(edge_type_8),
        "w0": np.asarray(L0_gnn_w0), "w1": np.asarray(L0_gnn_w1),
        "W": W, "WT": np.ascontiguousarray(W.transpose(2, 0, 1).reshape(d, r * d)),
        "attn_src": np.asarray(L1_gnn_attn_src), "attn_dst": np.asarray(L1_gnn_attn_dst),
    }
    nc = bacc.Bacc("TRN2", target_bir_lowering=False, num_devices=1)
    aps = {k: nc.dram_tensor(k + "_in", a.shape, mybir.dt.from_np(a.dtype), kind="ExternalInput").ap()
           for k, a in arrays.items()}
    out = nc.dram_tensor("out", (n, d), F32, kind="ExternalOutput").ap()
    graph_layers(nc, out=out, **aps)
    r = run_bass_kernel_spmd(nc, [{k + "_in": a for k, a in arrays.items()}], core_ids=[0])
    return r.results[0]["out"]
```
